# Optimizing a Trainium2 kernel written in Bass

```python
import numpy as np
import jax
import jax.numpy as jnp

def _softmax(x, axis=-1):
    return jax.nn.softmax(x, axis=axis)

def _gelu(x):
    return jax.nn.gelu(x, approximate=True)

def _silu(x):
    return jax.nn.silu(x)

def _sigmoid(x):
    return jax.nn.sigmoid(x)

def _layernorm(x, axis=-1, eps=1e-05):
    m = jnp.mean(x, axis=axis, keepdims=True)
    v = jnp.var(x, axis=axis, keepdims=True)
    return (x - m) / jnp.sqrt(v + eps)

def _scatter_add(tgt, idx, src, axis=0):
    return tgt.at[idx].add(src)

def _segment_sum(src, seg, n):
    return jax.ops.segment_sum(src, seg, n)
kernel_name = 'mk_gnn_resnorm_d4_gnn_r16_836a42'

def setup_inputs(seed: int=0):
    np.random.seed(seed)
    _w = jnp.asarray

    def _rec_inputs():
        import jax
        import jax.numpy as jnp
        _gk = jax.random.key(seed)
        x = -0.000202 + 1 * jax.random.normal(jax.random.fold_in(_gk, 1), (6250, 128), jnp.float32)
        src = jax.random.randint(jax.random.fold_in(_gk, 2), (100000,), 0, 6250, jnp.int32)
        dst = jnp.minimum((6250 * jax.random.uniform(jax.random.fold_in(_gk, 3), (100000,)) ** 2.0).astype(jnp.int32), 99999)
        _o = jnp.argsort(dst, stable=True)
        src = src[_o]
        dst = dst[_o]
        edge_attr_10 = jax.random.uniform(jax.random.fold_in(_gk, 12), (100000, 10), jnp.float32, 0.0, 1)
        edge_attr_4 = 0.00109026 + 0.999989 * jax.random.normal(jax.random.fold_in(_gk, 13), (100000, 4), jnp.float32)
        node_vec1 = jax.random.uniform(jax.random.fold_in(_gk, 15), (6250, 1), jnp.float32, 0.0, 1)
        return (x, src, dst, edge_attr_10, edge_attr_4, node_vec1)
    x, src, dst, edge_attr_10, edge_attr_4, node_vec1 = _rec_inputs()

    def _L0_gnn_setup():
        import math
        import jax
        import jax.numpy as jnp
        import numpy as np
        MUL = 32
        N_NODES = 3125
        N_EDGES = 50000
        N_BASIS = 10
        N_HID = 100
        NUM_NEIGHBORS = 16.0

        def _fctp(x0, x1, attr, W0, W1):
            inv = 1.0 / math.sqrt(W0.shape[0])
            o0 = attr * (x0 @ W0) * inv
            o1 = attr[:, :, None] * jnp.einsum('nud,uw->nwd', x1, W1) * inv
            return (o0, o1)

        def _forward(node_input, node_attr, edge_attr, edge_length_embedded, W_sc0, W_sc1, W_l10, W_l11, W_l20, W_l21, W_fc1, W_fc2, edge_src, edge_dst):
            N = node_input.shape[0]
            x0 = node_input[:, :MUL]
            x1 = node_input[:, MUL:].reshape(N, MUL, 3)
            s0, s1 = _fctp(x0, x1, node_attr, W_sc0, W_sc1)
            y0, y1 = _fctp(x0, x1, node_attr, W_l10, W_l11)
            h = jax.nn.silu(edge_length_embedded @ W_fc1 * (1.0 / math.sqrt(N_BASIS)))
            w = h @ W_fc2 * (1.0 / math.sqrt(N_HID))
            w1, w2, w3, w4 = (w[:, 0 * MUL:1 * MUL], w[:, 1 * MUL:2 * MUL], w[:, 2 * MUL:3 * MUL], w[:, 3 * MUL:4 * MUL])
            x0s = y0[edge_src]
            x1s = y1[edge_src]
            ea0 = edge_attr[:, :1]
            ea1 = edge_attr[:, 1:]
            mid0a = w1 * x0s * ea0
            mid0b = w4 * jnp.einsum('eum,em->eu', x1s, ea1) * (1.0 / math.sqrt(3.0))
            mid1a = (w2 * x0s)[:, :, None] * ea1[:, None, :]
            mid1b = w3[:, :, None] * x1s * ea0[:, None, :]
            E = edge_attr.shape[0]
            edge_features = jnp.concatenate([mid0a, mid0b, mid1a.reshape(E, -1), mid1b.reshape(E, -1)], axis=1)
            agg = jax.ops.segment_sum(edge_features, edge_dst, num_segments=N)
            agg = agg * (1.0 / math.sqrt(NUM_NEIGHBORS))
            m0 = agg[:, :2 * MUL]
            m1 = agg[:, 2 * MUL:].reshape(N, 2 * MUL, 3)
            z0, z1 = _fctp(m0, m1, node_attr, W_l20, W_l21)
            c_s = math.sin(math.pi / 8.0)
            c_x = math.cos(math.pi / 8.0)
            out0 = c_s * s0 + c_x * z0
            out1 = c_s * s1 + c_x * z1
            return jnp.concatenate([out0, out1.reshape(N, -1)], axis=1)
        key = jax.random.key(seed)
        ks = jax.random.split(key, 14)
        return {'node_input': jax.random.normal(ks[0], (N_NODES, 4 * MUL), jnp.float32), 'node_attr': jnp.ones((N_NODES, 1), jnp.float32), 'edge_src': jax.random.randint(ks[1], (N_EDGES,), 0, N_NODES, dtype=jnp.int32), 'edge_dst': jax.random.randint(ks[2], (N_EDGES,), 0, N_NODES, dtype=jnp.int32), 'edge_attr': jax.random.normal(ks[3], (N_EDGES, 4), jnp.float32), 'edge_length_embedded': jax.random.uniform(ks[4], (N_EDGES, N_BASIS), dtype=jnp.float32), 'W_sc0': jax.random.normal(ks[5], (MUL, MUL), jnp.float32), 'W_sc1': jax.random.normal(ks[6], (MUL, MUL), jnp.float32), 'W_l10': jax.random.normal(ks[7], (MUL, MUL), jnp.float32), 'W_l11': jax.random.normal(ks[8], (MUL, MUL), jnp.float32), 'W_l20': jax.random.normal(ks[9], (2 * MUL, MUL), jnp.float32), 'W_l21': jax.random.normal(ks[10], (2 * MUL, MUL), jnp.float32), 'W_fc1': jax.random.normal(ks[11], (N_BASIS, N_HID), jnp.float32), 'W_fc2': jax.random.normal(ks[12], (N_HID, 4 * MUL), jnp.float32)}
    _L0_gnn_all = _L0_gnn_setup()
    _L0_gnn_in = {k: v for k, v in _L0_gnn_all.items() if k in ('W_sc0', 'W_sc1', 'W_l10', 'W_l11', 'W_l20', 'W_l21', 'W_fc1', 'W_fc2')}
    del _L0_gnn_all

    def _L1_gnn_setup():
        import jax, jax.numpy as jnp
        import numpy as np
        N_NODES = 3125
        N_EDGES = 50000
        DIM = 128
        BN_EPS = 1e-05
        key = jax.random.key(seed)
        ks = jax.random.split(key, 12)
        d = DIM
        s = 1.0 / np.sqrt(d)
        x = jax.random.normal(ks[0], (N_NODES, d), dtype=jnp.float32)
        edge_index = jax.random.randint(ks[1], (2, N_EDGES), 0, N_NODES, dtype=jnp.int64)
        W_msg = jax.random.uniform(ks[2], (d, d), jnp.float32, -s, s)
        b_msg = jax.random.uniform(ks[3], (d,), jnp.float32, -s, s)
        sa = 1.0 / np.sqrt(2 * d)
        W_att = jax.random.uniform(ks[4], (2 * d, 1), jnp.float32, -sa, sa)
        b_att = jax.random.uniform(ks[5], (1,), jnp.float32, -sa, sa)
        W_ih = jax.random.uniform(ks[6], (3 * d, d), jnp.float32, -s, s)
        b_ih = jax.random.uniform(ks[7], (3 * d,), jnp.float32, -s, s)
        W_hh = jax.random.uniform(ks[8], (3 * d, d), jnp.float32, -s, s)
        b_hh = jax.random.uniform(ks[9], (3 * d,), jnp.float32, -s, s)
        gamma = jnp.ones((d,), jnp.float32)
        beta = jnp.zeros((d,), jnp.float32)
        return {'x': x, 'edge_index': edge_index, 'W_msg': W_msg, 'b_msg': b_msg, 'W_att': W_att, 'b_att': b_att, 'W_ih': W_ih, 'b_ih': b_ih, 'W_hh': W_hh, 'b_hh': b_hh, 'gamma': gamma, 'beta': beta}
    _L1_gnn_all = _L1_gnn_setup()
    _L1_gnn_in = {k: v for k, v in _L1_gnn_all.items() if k in ('W_msg', 'b_msg', 'W_att', 'b_att', 'W_ih', 'b_ih', 'W_hh', 'b_hh', 'gamma', 'beta')}
    del _L1_gnn_all

    def _L2_gnn_setup():
        import jax, jax.numpy as jnp
        import numpy as np
        N = 3125
        E = 50000
        D = 128
        MAX_NODES = 4
        EPS = 1e-05

        def sort_conv(x, edge_index, blank, W, b, cw, cb, a):
            n, d = x.shape
            e = edge_index.shape[1]
            src, dst = (edge_index[0], edge_index[1])
            msgs = x[src]
            order = jnp.argsort(dst)
            dst_s = dst[order]
            counts = jax.ops.segment_sum(jnp.ones((e,), jnp.int32), dst, num_segments=n + 1)
            starts = jnp.concatenate([jnp.zeros((1,), jnp.int32), jnp.cumsum(counts)[:-1].astype(jnp.int32)])
            pos = jnp.arange(e, dtype=jnp.int32) - starts[dst_s]
            slot = jnp.where(pos < MAX_NODES, pos, MAX_NODES)
            dense = jnp.zeros((n + 1, MAX_NODES + 1, d), x.dtype).at[dst_s, slot].set(msgs[order])
            mask = jnp.zeros((n + 1, MAX_NODES + 1), bool).at[dst_s, slot].set(True)
            dense, mask = (dense[:, :MAX_NODES], mask[:, :MAX_NODES])
            blank_p = W @ blank + b
            filled = dense + (~mask)[..., None].astype(x.dtype) * blank_p
            srt = jnp.sort(filled, axis=1)
            out = jnp.einsum('nmd,m->nd', srt, cw) + cb
            node_out, blank_new = (out[:-1], out[-1])
            return (a * x + node_out, a * blank + blank_new)

        def batch_norm(h, g, be):
            mu = h.mean(0)
            var = h.var(0)
            return (h - mu) / jnp.sqrt(var + EPS) * g + be
        key = jax.random.key(seed)
        ks = jax.random.split(key, 16)
        inp = {'x': jax.random.normal(ks[0], (N, D), jnp.float32), 'edge_index': jax.random.randint(ks[1], (2, E), 0, N, jnp.int32)}
        for i in range(2):
            o = 2 + 6 * i
            W = jax.random.normal(ks[o], (D, D), jnp.float32) * (2.0 / (D + D)) ** 0.5
            W = W / jnp.linalg.norm(W, axis=1, keepdims=True)
            inp[f'W{i}'] = W
            inp[f'b{i}'] = jnp.zeros((D,), jnp.float32)
            inp[f'cw{i}'] = jax.random.normal(ks[o + 1], (MAX_NODES,), jnp.float32) * (2.0 / (MAX_NODES + 1)) ** 0.5
            inp[f'cb{i}'] = jnp.zeros((1,), jnp.float32)
            inp[f'a{i}'] = jax.random.uniform(ks[o + 2], (1,), jnp.float32, -1.0, 1.0)
            inp[f'g{i}'] = jnp.ones((D,), jnp.float32)
            inp[f'be{i}'] = jnp.zeros((D,), jnp.float32)
            inp[f'blank{i}'] = jnp.zeros((D,), jnp.float32)
        return inp
    _L2_gnn_all = _L2_gnn_setup()
    _L2_gnn_in = {k: v for k, v in _L2_gnn_all.items() if k in ('W0', 'b0', 'cw0', 'cb0', 'a0', 'g0', 'be0', 'blank0', 'W1', 'b1', 'cw1', 'cb1', 'a1', 'g1', 'be1', 'blank1')}
    del _L2_gnn_all

    def _L3_gnn_setup():
        import jax, jax.numpy as jnp
        import numpy as np
        N_NODES = 1250
        N_EDGES = 20000
        D_IN = 128
        D_HID = 256
        BN_EPS = 1e-05

        def _lin_init(key, out_dim, in_dim, bias=True):
            kw, kb = jax.random.split(key)
            s = 1.0 / np.sqrt(in_dim)
            W = jax.random.uniform(kw, (out_dim, in_dim), jnp.float32, -s, s)
            if bias:
                b = jax.random.uniform(kb, (out_dim,), jnp.float32, -s, s)
                return (W, b)
            return W

        def _sage(z, src, dst, Wl, bl, Wr, n_nodes):
            msg = z[src]
            agg = jax.ops.segment_sum(msg, dst, num_segments=n_nodes)
            cnt = jax.ops.segment_sum(jnp.ones((src.shape[0], 1), z.dtype), dst, num_segments=n_nodes)
            mean = agg / jnp.maximum(cnt, 1.0)
            return mean @ Wl.T + bl + z @ Wr.T

        def _bn(z, gamma, beta):
            m = jnp.mean(z, axis=0)
            v = jnp.var(z, axis=0)
            return (z - m) * jax.lax.rsqrt(v + BN_EPS) * gamma + beta
        key = jax.random.key(seed)
        ks = jax.random.split(key, 16)
        x = jax.random.normal(ks[0], (N_NODES, D_IN), jnp.float32)
        edge_index = jax.random.randint(ks[1], (2, N_EDGES), 0, N_NODES, jnp.int64)
        enc_W, enc_b = _lin_init(ks[2], D_IN, D_IN)
        Wl0, bl0 = _lin_init(ks[3], D_HID, D_IN)
        Wr0 = _lin_init(ks[4], D_HID, D_IN, bias=False)
        Wl1, bl1 = _lin_init(ks[5], D_HID, D_HID)
        Wr1 = _lin_init(ks[6], D_HID, D_HID, bias=False)
        Wl2, bl2 = _lin_init(ks[7], D_HID, D_HID)
        Wr2 = _lin_init(ks[8], D_HID, D_HID, bias=False)
        Wl3, bl3 = _lin_init(ks[9], D_IN, D_HID)
        Wr3 = _lin_init(ks[10], D_IN, D_HID, bias=False)
        g0 = jnp.ones((D_HID,), jnp.float32)
        b0 = jnp.zeros((D_HID,), jnp.float32)
        g1 = jnp.ones((D_HID,), jnp.float32)
        b1 = jnp.zeros((D_HID,), jnp.float32)
        g2 = jnp.ones((D_HID,), jnp.float32)
        b2 = jnp.zeros((D_HID,), jnp.float32)
        dec_W, dec_b = _lin_init(ks[11], D_IN, D_IN)
        return dict(x=x, edge_index=edge_index, enc_W=enc_W, enc_b=enc_b, Wl0=Wl0, bl0=bl0, Wr0=Wr0, Wl1=Wl1, bl1=bl1, Wr1=Wr1, Wl2=Wl2, bl2=bl2, Wr2=Wr2, Wl3=Wl3, bl3=bl3, Wr3=Wr3, g0=g0, b0=b0, g1=g1, b1=b1, g2=g2, b2=b2, dec_W=dec_W, dec_b=dec_b)
    _L3_gnn_all = _L3_gnn_setup()
    _L3_gnn_in = {k: v for k, v in _L3_gnn_all.items() if k in ('enc_W', 'enc_b', 'Wl0', 'bl0', 'Wr0', 'Wl1', 'bl1', 'Wr1', 'Wl2', 'bl2', 'Wr2', 'Wl3', 'bl3', 'Wr3', 'g0', 'b0', 'g1', 'b1', 'g2', 'b2', 'dec_W', 'dec_b')}
    del _L3_gnn_all
    return {'x': x, 'src': src, 'dst': dst, 'edge_attr_10': edge_attr_10, 'edge_attr_4': edge_attr_4, 'node_vec1': node_vec1, 'L0_gnn_W_sc0': _L0_gnn_in['W_sc0'], 'L0_gnn_W_sc1': _L0_gnn_in['W_sc1'], 'L0_gnn_W_l10': _L0_gnn_in['W_l10'], 'L0_gnn_W_l11': _L0_gnn_in['W_l11'], 'L0_gnn_W_l20': _L0_gnn_in['W_l20'], 'L0_gnn_W_l21': _L0_gnn_in['W_l21'], 'L0_gnn_W_fc1': _L0_gnn_in['W_fc1'], 'L0_gnn_W_fc2': _L0_gnn_in['W_fc2'], 'L1_gnn_W_msg': _L1_gnn_in['W_msg'], 'L1_gnn_b_msg': _L1_gnn_in['b_msg'], 'L1_gnn_W_att': _L1_gnn_in['W_att'], 'L1_gnn_b_att': _L1_gnn_in['b_att'], 'L1_gnn_W_ih': _L1_gnn_in['W_ih'], 'L1_gnn_b_ih': _L1_gnn_in['b_ih'], 'L1_gnn_W_hh': _L1_gnn_in['W_hh'], 'L1_gnn_b_hh': _L1_gnn_in['b_hh'], 'L1_gnn_gamma': _L1_gnn_in['gamma'], 'L1_gnn_beta': _L1_gnn_in['beta'], 'L2_gnn_W0': _L2_gnn_in['W0'], 'L2_gnn_b0': _L2_gnn_in['b0'], 'L2_gnn_cw0': _L2_gnn_in['cw0'], 'L2_gnn_cb0': _L2_gnn_in['cb0'], 'L2_gnn_a0': _L2_gnn_in['a0'], 'L2_gnn_g0': _L2_gnn_in['g0'], 'L2_gnn_be0': _L2_gnn_in['be0'], 'L2_gnn_blank0': _L2_gnn_in['blank0'], 'L2_gnn_W1': _L2_gnn_in['W1'], 'L2_gnn_b1': _L2_gnn_in['b1'], 'L2_gnn_cw1': _L2_gnn_in['cw1'], 'L2_gnn_cb1': _L2_gnn_in['cb1'], 'L2_gnn_a1': _L2_gnn_in['a1'], 'L2_gnn_g1': _L2_gnn_in['g1'], 'L2_gnn_be1': _L2_gnn_in['be1'], 'L2_gnn_blank1': _L2_gnn_in['blank1'], 'L3_gnn_enc_W': _L3_gnn_in['enc_W'], 'L3_gnn_enc_b': _L3_gnn_in['enc_b'], 'L3_gnn_Wl0': _L3_gnn_in['Wl0'], 'L3_gnn_bl0': _L3_gnn_in['bl0'], 'L3_gnn_Wr0': _L3_gnn_in['Wr0'], 'L3_gnn_Wl1': _L3_gnn_in['Wl1'], 'L3_gnn_bl1': _L3_gnn_in['bl1'], 'L3_gnn_Wr1': _L3_gnn_in['Wr1'], 'L3_gnn_Wl2': _L3_gnn_in['Wl2'], 'L3_gnn_bl2': _L3_gnn_in['bl2'], 'L3_gnn_Wr2': _L3_gnn_in['Wr2'], 'L3_gnn_Wl3': _L3_gnn_in['Wl3'], 'L3_gnn_bl3': _L3_gnn_in['bl3'], 'L3_gnn_Wr3': _L3_gnn_in['Wr3'], 'L3_gnn_g0': _L3_gnn_in['g0'], 'L3_gnn_b0': _L3_gnn_in['b0'], 'L3_gnn_g1': _L3_gnn_in['g1'], 'L3_gnn_b1': _L3_gnn_in['b1'], 'L3_gnn_g2': _L3_gnn_in['g2'], 'L3_gnn_b2': _L3_gnn_in['b2'], 'L3_gnn_dec_W': _L3_gnn_in['dec_W'], 'L3_gnn_dec_b': _L3_gnn_in['dec_b']}

def reference(x, src, dst, edge_attr_10, edge_attr_4, node_vec1, L0_gnn_W_sc0, L0_gnn_W_sc1, L0_gnn_W_l10, L0_gnn_W_l11, L0_gnn_W_l20, L0_gnn_W_l21, L0_gnn_W_fc1, L0_gnn_W_fc2, L1_gnn_W_msg, L1_gnn_b_msg, L1_gnn_W_att, L1_gnn_b_att, L1_gnn_W_ih, L1_gnn_b_ih, L1_gnn_W_hh, L1_gnn_b_hh, L1_gnn_gamma, L1_gnn_beta, L2_gnn_W0, L2_gnn_b0, L2_gnn_cw0, L2_gnn_cb0, L2_gnn_a0, L2_gnn_g0, L2_gnn_be0, L2_gnn_blank0, L2_gnn_W1, L2_gnn_b1, L2_gnn_cw1, L2_gnn_cb1, L2_gnn_a1, L2_gnn_g1, L2_gnn_be1, L2_gnn_blank1, L3_gnn_enc_W, L3_gnn_enc_b, L3_gnn_Wl0, L3_gnn_bl0, L3_gnn_Wr0, L3_gnn_Wl1, L3_gnn_bl1, L3_gnn_Wr1, L3_gnn_Wl2, L3_gnn_bl2, L3_gnn_Wr2, L3_gnn_Wl3, L3_gnn_bl3, L3_gnn_Wr3, L3_gnn_g0, L3_gnn_b0, L3_gnn_g1, L3_gnn_b1, L3_gnn_g2, L3_gnn_b2, L3_gnn_dec_W, L3_gnn_dec_b):
    import jax
    import jax.numpy as jnp

    def _L0_gnn_ref(node_input, node_attr, edge_src, edge_dst, edge_attr, edge_length_embedded, W_sc0, W_sc1, W_l10, W_l11, W_l20, W_l21, W_fc1, W_fc2):
        import math
        import jax
        import jax.numpy as jnp
        import numpy as np
        MUL = 32
        N_NODES = 3125
        N_EDGES = 50000
        N_BASIS = 10
        N_HID = 100
        NUM_NEIGHBORS = 16.0

        def _fctp(x0, x1, attr, W0, W1):
            inv = 1.0 / math.sqrt(W0.shape[0])
            o0 = attr * (x0 @ W0) * inv
            o1 = attr[:, :, None] * jnp.einsum('nud,uw->nwd', x1, W1) * inv
            return (o0, o1)

        def _forward(node_input, node_attr, edge_attr, edge_length_embedded, W_sc0, W_sc1, W_l10, W_l11, W_l20, W_l21, W_fc1, W_fc2, edge_src, edge_dst):
            N = node_input.shape[0]
            x0 = node_input[:, :MUL]
            x1 = node_input[:, MUL:].reshape(N, MUL, 3)
            s0, s1 = _fctp(x0, x1, node_attr, W_sc0, W_sc1)
            y0, y1 = _fctp(x0, x1, node_attr, W_l10, W_l11)
            h = jax.nn.silu(edge_length_embedded @ W_fc1 * (1.0 / math.sqrt(N_BASIS)))
            w = h @ W_fc2 * (1.0 / math.sqrt(N_HID))
            w1, w2, w3, w4 = (w[:, 0 * MUL:1 * MUL], w[:, 1 * MUL:2 * MUL], w[:, 2 * MUL:3 * MUL], w[:, 3 * MUL:4 * MUL])
            x0s = y0[edge_src]
            x1s = y1[edge_src]
            ea0 = edge_attr[:, :1]
            ea1 = edge_attr[:, 1:]
            mid0a = w1 * x0s * ea0
            mid0b = w4 * jnp.einsum('eum,em->eu', x1s, ea1) * (1.0 / math.sqrt(3.0))
            mid1a = (w2 * x0s)[:, :, None] * ea1[:, None, :]
            mid1b = w3[:, :, None] * x1s * ea0[:, None, :]
            E = edge_attr.shape[0]
            edge_features = jnp.concatenate([mid0a, mid0b, mid1a.reshape(E, -1), mid1b.reshape(E, -1)], axis=1)
            agg = jax.ops.segment_sum(edge_features, edge_dst, num_segments=N)
            agg = agg * (1.0 / math.sqrt(NUM_NEIGHBORS))
            m0 = agg[:, :2 * MUL]
            m1 = agg[:, 2 * MUL:].reshape(N, 2 * MUL, 3)
            z0, z1 = _fctp(m0, m1, node_attr, W_l20, W_l21)
            c_s = math.sin(math.pi / 8.0)
            c_x = math.cos(math.pi / 8.0)
            out0 = c_s * s0 + c_x * z0
            out1 = c_s * s1 + c_x * z1
            return jnp.concatenate([out0, out1.reshape(N, -1)], axis=1)
        return _forward(node_input, node_attr, edge_attr, edge_length_embedded, W_sc0, W_sc1, W_l10, W_l11, W_l20, W_l21, W_fc1, W_fc2, edge_src, edge_dst)

    def _L1_gnn_ref(x, edge_index, W_msg, b_msg, W_att, b_att, W_ih, b_ih, W_hh, b_hh, gamma, beta):
        import jax, jax.numpy as jnp
        import numpy as np
        N_NODES = 3125
        N_EDGES = 50000
        DIM = 128
        BN_EPS = 1e-05
        num_nodes, d = x.shape
        src = edge_index[0]
        dst = edge_index[1]
        xs = x[src]
        xd = x[dst]
        att = jax.nn.sigmoid(xs @ W_att[:d] + xd @ W_att[d:] + b_att)
        messages = (xs @ W_msg + b_msg) * att
        aggregated = jax.ops.segment_sum(messages, dst, num_segments=num_nodes)
        gi = aggregated @ W_ih.T + b_ih
        gh = x @ W_hh.T + b_hh
        i_r, i_z, i_n = jnp.split(gi, 3, axis=1)
        h_r, h_z, h_n = jnp.split(gh, 3, axis=1)
        r = jax.nn.sigmoid(i_r + h_r)
        z = jax.nn.sigmoid(i_z + h_z)
        n = jnp.tanh(i_n + r * h_n)
        h_new = (1.0 - z) * n + z * x
        mean = jnp.mean(h_new, axis=0)
        var = jnp.var(h_new, axis=0)
        return gamma * (h_new - mean) * jax.lax.rsqrt(var + BN_EPS) + beta

    def _L2_gnn_ref(x, edge_index, W0, b0, cw0, cb0, a0, g0, be0, blank0, W1, b1, cw1, cb1, a1, g1, be1, blank1):
        import jax, jax.numpy as jnp
        import numpy as np
        N = 3125
        E = 50000
        D = 128
        MAX_NODES = 4
        EPS = 1e-05

        def sort_conv(x, edge_index, blank, W, b, cw, cb, a):
            n, d = x.shape
            e = edge_index.shape[1]
            src, dst = (edge_index[0], edge_index[1])
            msgs = x[src]
            order = jnp.argsort(dst)
            dst_s = dst[order]
            counts = jax.ops.segment_sum(jnp.ones((e,), jnp.int32), dst, num_segments=n + 1)
            starts = jnp.concatenate([jnp.zeros((1,), jnp.int32), jnp.cumsum(counts)[:-1].astype(jnp.int32)])
            pos = jnp.arange(e, dtype=jnp.int32) - starts[dst_s]
            slot = jnp.where(pos < MAX_NODES, pos, MAX_NODES)
            dense = jnp.zeros((n + 1, MAX_NODES + 1, d), x.dtype).at[dst_s, slot].set(msgs[order])
            mask = jnp.zeros((n + 1, MAX_NODES + 1), bool).at[dst_s, slot].set(True)
            dense, mask = (dense[:, :MAX_NODES], mask[:, :MAX_NODES])
            blank_p = W @ blank + b
            filled = dense + (~mask)[..., None].astype(x.dtype) * blank_p
            srt = jnp.sort(filled, axis=1)
            out = jnp.einsum('nmd,m->nd', srt, cw) + cb
            node_out, blank_new = (out[:-1], out[-1])
            return (a * x + node_out, a * blank + blank_new)

        def batch_norm(h, g, be):
            mu = h.mean(0)
            var = h.var(0)
            return (h - mu) / jnp.sqrt(var + EPS) * g + be
        layers = [(W0, b0, cw0, cb0, a0, g0, be0, blank0), (W1, b1, cw1, cb1, a1, g1, be1, blank1)]
        for W, b, cw, cb, a, g, be, blank in layers:
            h, _ = sort_conv(x, edge_index, blank, W, b, cw, cb, a)
            h = batch_norm(h, g, be)
            x = x + h
        return x

    def _L3_gnn_ref(x, edge_index, enc_W, enc_b, Wl0, bl0, Wr0, Wl1, bl1, Wr1, Wl2, bl2, Wr2, Wl3, bl3, Wr3, g0, b0, g1, b1, g2, b2, dec_W, dec_b):
        import jax, jax.numpy as jnp
        import numpy as np
        N_NODES = 1250
        N_EDGES = 20000
        D_IN = 128
        D_HID = 256
        BN_EPS = 1e-05

        def _lin_init(key, out_dim, in_dim, bias=True):
            kw, kb = jax.random.split(key)
            s = 1.0 / np.sqrt(in_dim)
            W = jax.random.uniform(kw, (out_dim, in_dim), jnp.float32, -s, s)
            if bias:
                b = jax.random.uniform(kb, (out_dim,), jnp.float32, -s, s)
                return (W, b)
            return W

        def _sage(z, src, dst, Wl, bl, Wr, n_nodes):
            msg = z[src]
            agg = jax.ops.segment_sum(msg, dst, num_segments=n_nodes)
            cnt = jax.ops.segment_sum(jnp.ones((src.shape[0], 1), z.dtype), dst, num_segments=n_nodes)
            mean = agg / jnp.maximum(cnt, 1.0)
            return mean @ Wl.T + bl + z @ Wr.T

        def _bn(z, gamma, beta):
            m = jnp.mean(z, axis=0)
            v = jnp.var(z, axis=0)
            return (z - m) * jax.lax.rsqrt(v + BN_EPS) * gamma + beta
        src, dst = (edge_index[0], edge_index[1])
        n = x.shape[0]
        z = x @ enc_W.T + enc_b
        z = jax.nn.relu(_bn(_sage(z, src, dst, Wl0, bl0, Wr0, n), g0, b0))
        z = jax.nn.relu(_bn(_sage(z, src, dst, Wl1, bl1, Wr1, n), g1, b1))
        z = jax.nn.relu(_bn(_sage(z, src, dst, Wl2, bl2, Wr2, n), g2, b2))
        z = _sage(z, src, dst, Wl3, bl3, Wr3, n)
        z = z @ dec_W.T + dec_b
        return z
    edge_index = jnp.stack([src, dst])
    x = _layernorm(x + _L0_gnn_ref(x, node_vec1, src, dst, edge_attr_4, edge_attr_10, L0_gnn_W_sc0, L0_gnn_W_sc1, L0_gnn_W_l10, L0_gnn_W_l11, L0_gnn_W_l20, L0_gnn_W_l21, L0_gnn_W_fc1, L0_gnn_W_fc2), axis=-1)
    x = _layernorm(x + _L1_gnn_ref(x, edge_index, L1_gnn_W_msg, L1_gnn_b_msg, L1_gnn_W_att, L1_gnn_b_att, L1_gnn_W_ih, L1_gnn_b_ih, L1_gnn_W_hh, L1_gnn_b_hh, L1_gnn_gamma, L1_gnn_beta), axis=-1)
    x = _layernorm(x + _L2_gnn_ref(x, edge_index, L2_gnn_W0, L2_gnn_b0, L2_gnn_cw0, L2_gnn_cb0, L2_gnn_a0, L2_gnn_g0, L2_gnn_be0, L2_gnn_blank0, L2_gnn_W1, L2_gnn_b1, L2_gnn_cw1, L2_gnn_cb1, L2_gnn_a1, L2_gnn_g1, L2_gnn_be1, L2_gnn_blank1), axis=-1)
    x = _layernorm(x + _L3_gnn_ref(x, edge_index, L3_gnn_enc_W, L3_gnn_enc_b, L3_gnn_Wl0, L3_gnn_bl0, L3_gnn_Wr0, L3_gnn_Wl1, L3_gnn_bl1, L3_gnn_Wr1, L3_gnn_Wl2, L3_gnn_bl2, L3_gnn_Wr2, L3_gnn_Wl3, L3_gnn_bl3, L3_gnn_Wr3, L3_gnn_g0, L3_gnn_b0, L3_gnn_g1, L3_gnn_b1, L3_gnn_g2, L3_gnn_b2, L3_gnn_dec_W, L3_gnn_dec_b), axis=-1)
    return x

_drawn_inputs = setup_inputs


def setup_inputs(seed=0):
    import zlib

    import numpy as np

    out = dict(_drawn_inputs(seed))
    spreads = {'L1_gnn_gamma': (1.0, 0.2),
     'L1_gnn_beta': (0.0, 0.1),
     'L2_gnn_b0': (0.0, 0.762),
     'L2_gnn_g0': (1.0, 0.2),
     'L2_gnn_be0': (0.0, 0.1),
     'L2_gnn_blank0': (0.0, 0.8),
     'L2_gnn_b1': (0.0, 2.0),
     'L2_gnn_g1': (1.0, 0.2),
     'L2_gnn_be1': (0.0, 0.1),
     'L2_gnn_blank1': (0.0, 0.8),
     'L3_gnn_g0': (1.0, 0.2),
     'L3_gnn_b0': (0.0, 0.368),
     'L3_gnn_g1': (1.0, 0.2),
     'L3_gnn_b1': (0.0, 0.397),
     'L3_gnn_g2': (1.0, 0.2),
     'L3_gnn_b2': (0.0, 0.306)}
    factors = {'L1_gnn_b_hh': 2.929,
     'L2_gnn_W0': 5.541,
     'L2_gnn_W1': 5.83,
     'L3_gnn_enc_b': 64.0,
     'L3_gnn_bl0': 64.0,
     'L3_gnn_bl1': 64.0,
     'L3_gnn_bl2': 64.0,
     'L3_gnn_bl3': 3.011}
    for name, (base, spread) in spreads.items():
        noise = np.random.default_rng([zlib.crc32(name.encode()), seed]).standard_normal(out[name].shape)
        drawn = base * np.exp(spread * noise) if base else spread * noise
        out[name] = jnp.asarray(drawn.astype(out[name].dtype))
    for name, factor in factors.items():
        out[name] = (out[name] * factor).astype(out[name].dtype)
    return out
```

```python
import math
from contextlib import ExitStack

import concourse.bass as bass
from concourse import mybir

F32 = mybir.dt.float32
I32 = mybir.dt.int32
ALU = mybir.AluOpType
ACT = mybir.ActivationFunctionType
DVE_E = mybir.EngineType.DVE
ACT_E = mybir.EngineType.Activation

P = 128
N_NODES = 6250
N_EDGES = 100000
BLOCKS = -(-N_NODES // P)
NP = BLOCKS * P
GROUP_TILES = 4
RING = 4
GROUPS = 196
TILES = GROUPS * GROUP_TILES
ITERS = GROUPS // RING
WIN = 128
REGION = 6400
CHUNK = 448
CHUNKS = NP // CHUNK
MUL = 32
HID = 100
BASIS = 10
SLOTS = 4
EPS = 1e-5
WINDOWS = NP // WIN
BASE_COLS = -(-GROUPS // P)
LOOK = 2
assert TILES * P >= N_EDGES and REGION >= N_NODES + WIN and CHUNK * CHUNKS == NP


def holds_back(value):
    return not isinstance(value, int) or value > 0


def looped(eng, count, body):
    body(0)
    if count > 1:
        with eng.Fori(1, count) as i:
            body(i)


class Scope:
    BANKS = (100, 170)
    turn = 0

    def __init__(self, nc, name):
        self.nc, self.name, self.stack, self.sems = nc, name, ExitStack(), []
        self.first = Scope.BANKS[Scope.turn]
        Scope.turn = 1 - Scope.turn

    def __enter__(self):
        return self

    def __exit__(self, *a):
        self.stack.__exit__(*a)
        if self.sems:
            self.nc.gpsimd.sem_clear(range(self.first, self.first + len(self.sems)))
            for sem in self.sems:
                self.nc.release_semaphore(sem)

    def sb(self, name, shape, dt=F32):
        return self.stack.enter_context(self.nc.sbuf_tensor(f"{self.name}_{name}", shape, dt))

    def ps(self, name, shape):
        return self.stack.enter_context(self.nc.psum_tensor(f"{self.name}_{name}_ps", shape, F32))

    def sem(self, name):
        self.sems.append(self.nc.alloc_semaphore(f"{self.name}_{name}", self.first + len(self.sems)))
        return self.sems[-1]

    def block(self):
        return self.stack.enter_context(self.nc.Block())


class Gathers:

    def __init__(self, nc, slots):
        self.sems = [nc.alloc_semaphore(f"gathered{k}", 240 + k) for k in range(slots)]
        self.base = [0] * slots

    def count(self, k, tiles):
        return 16 * tiles + self.base[k]

    def end_phase(self, slots, tiles):
        for k in range(slots):
            self.base[k] += 16 * tiles


def cols(region, start, width):
    return region[:, bass.ds(start, width)]


def load_phase(nc, name, pairs):
    with Scope(nc, name) as s:
        loaded = s.sem("loaded")
        block = s.block()

        @block.sync
        def _(sp):
            for dst, src in pairs:
                sp.dma_start(dst, src).then_inc(loaded, 16)
            sp.wait_ge(loaded, 16 * len(pairs))


def table_phase(nc, name, sources, table, width, ident, func=None, params=None, copy_back=False,
                rhs=None, bias=None, row_scale=None):
    K = len(sources)
    SUB = 7
    with Scope(nc, name) as s:
        stage = s.sb("stage", [P, SUB, K, P])
        rows = s.sb("rows", [P, SUB, width])
        turned = s.ps("turned", [P, SUB, 512])
        staged, flipped, evacuated, copied = s.sem("staged"), s.sem("flipped"), s.sem("evacuated"), s.sem("copied")
        stored = [s.sem(f"stored{b}") for b in range(SUB)]
        block = s.block()

        @block.scalar
        def _(act):
            def body(i):
                for b in range(SUB):
                    n = i * SUB + b
                    if holds_back(n - SUB + 1):
                        act.wait_ge(flipped, n - SUB + 1)
                    if copy_back:
                        if holds_back(n - SUB + 1):
                            act.wait_ge(copied, n - SUB + 1)
                    for k in range(K):
                        src = cols(sources[k], n * P, P)
                        if params is None:
                            ins = nc.scalar.activation(stage[:, b, k, :], src, ACT.Identity)
                        else:
                            scale, shift = params[k]
                            ins = nc.scalar.activation(stage[:, b, k, :], src, func, bias=shift, scale=scale)
                    ins.then_inc(staged, 1)
            looped(act, BLOCKS // SUB, body)

        @block.tensor
        def _(pe):
            def body(i):
                for b in range(SUB):
                    n = i * SUB + b
                    if holds_back(n - SUB + 1):
                        pe.wait_ge(evacuated, n - SUB + 1)
                    pe.wait_ge(staged, n + 1)
                    if rhs is None:
                        for k in range(K):
                            ins = nc.tensor.transpose(turned[:, b, k * P:(k + 1) * P], stage[:, b, k, :], ident[:])
                    else:
                        for k in range(K):
                            ins = nc.tensor.matmul(turned[:, b, 0:width], stage[:, b, k, :], rhs[k],
                                                   start=(k == 0), stop=(k == K - 1 and bias is None))
                        if bias is not None:
                            ones, row = bias
                            ins = nc.tensor.matmul(turned[:, b, 0:width], ones, row, start=False, stop=True)
                    ins.then_inc(flipped, 1)
            looped(pe, BLOCKS // SUB, body)

        @block.vector
        def _(dve):
            def body(i):
                for b in range(SUB):
                    n = i * SUB + b
                    if holds_back(16 * i):
                        dve.wait_ge(stored[b], 16 * i)
                    dve.wait_ge(flipped, n + 1)
                    if row_scale is None:
                        ins = nc.vector.tensor_copy(rows[:, b, :], turned[:, b, 0:width])
                    else:
                        ins = nc.vector.tensor_scalar(rows[:, b, :], turned[:, b, 0:width],
                                                      cols(row_scale, n, 1), None, ALU.mult)
                    ins.then_inc(evacuated, 1)
                    if copy_back:
                        for k in range(K):
                            ins = nc.vector.tensor_copy(cols(sources[k], n * P, P), stage[:, b, k, :])
                        ins.then_inc(copied, 1)
            looped(dve, BLOCKS // SUB, body)

        @block.sync
        def _(sp):
            def body(i):
                for b in range(SUB):
                    n = i * SUB + b
                    sp.wait_ge(evacuated, n + 1)
                    sp.dma_start(table[bass.ds(n * P, P), :], rows[:, b, :]).then_inc(stored[b], 16)
            looped(sp, BLOCKS // SUB, body)
            for b in range(SUB):
                sp.wait_ge(stored[b], 16 * (BLOCKS // SUB))


def linear_phase(nc, name, terms, outs):
    M = len(outs)
    with Scope(nc, name) as s:
        acc = s.ps("acc", [P, 2, M, 512])
        summed, evacuated = s.sem("summed"), s.sem("evacuated")
        block = s.block()

        @block.tensor
        def _(pe):
            def body(i):
                for c in range(2):
                    n = i * 2 + c
                    if holds_back(n - 1):
                        pe.wait_ge(evacuated, n - 1)
                    for m in range(M):
                        for k, (lhsT, region) in enumerate(terms):
                            ins = nc.tensor.matmul(acc[:, c, m, 0:CHUNK], lhsT[m], cols(region, n * CHUNK, CHUNK),
                                                   start=(k == 0), stop=(k == len(terms) - 1))
                    ins.then_inc(summed, 1)
            looped(pe, CHUNKS // 2, body)

        @block.scalar
        def _(act):
            def body(i):
                for c in range(2):
                    n = i * 2 + c
                    act.wait_ge(summed, n + 1)
                    for m, (region, bias) in enumerate(outs):
                        ins = nc.scalar.activation(cols(region, n * CHUNK, CHUNK), acc[:, c, m, 0:CHUNK],
                                                   ACT.Identity, bias=bias)
                    ins.then_inc(evacuated, 1)
            looped(act, CHUNKS // 2, body)


def layernorm_phase(nc, name, X, mean_w, eps):
    with Scope(nc, name) as s:
        mean_ps, var_ps = s.ps("mean", [P, 2, 512]), s.ps("var", [P, 2, 512])
        xc, sq = s.sb("xc", [P, 2, CHUNK]), s.sb("sq", [P, 2, CHUNK])
        sd, rs = s.sb("sd", [P, 2, CHUNK]), s.sb("rs", [P, 2, CHUNK])
        meaned, centred, squared = s.sem("meaned"), s.sem("centred"), s.sem("squared")
        vared, rooted, inverted, done = s.sem("vared"), s.sem("rooted"), s.sem("inverted"), s.sem("done")
        block = s.block()

        @block.tensor
        def _(pe):
            def body(i):
                for c in range(2):
                    n = 2 * i + c
                    if holds_back(n - 1):
                        pe.wait_ge(centred, n - 1)
                    nc.tensor.matmul(mean_ps[:, c, 0:CHUNK], mean_w[:], cols(X, n * CHUNK, CHUNK),
                                     start=True, stop=True).then_inc(meaned, 1)
                for c in range(2):
                    n = 2 * i + c
                    if holds_back(n - 1):
                        pe.wait_ge(rooted, n - 1)
                    pe.wait_ge(squared, n + 1)
                    nc.tensor.matmul(var_ps[:, c, 0:CHUNK], mean_w[:], sq[:, c, :],
                                     start=True, stop=True).then_inc(vared, 1)
            looped(pe, CHUNKS // 2, body)

        @block.scalar
        def _(act):
            def body(i):
                for c in range(2):
                    n = 2 * i + c
                    if holds_back(n - 1):
                        act.wait_ge(vared, n - 1)
                    act.wait_ge(centred, n + 1)
                    nc.scalar.activation(sq[:, c, :], xc[:, c, :], ACT.Square).then_inc(squared, 1)
                for c in range(2):
                    n = 2 * i + c
                    if holds_back(n - 1):
                        act.wait_ge(inverted, n - 1)
                    act.wait_ge(vared, n + 1)
                    nc.scalar.activation(sd[:, c, :], var_ps[:, c, 0:CHUNK], ACT.Sqrt,
                                         bias=eps[:, 0:1]).then_inc(rooted, 1)
            looped(act, CHUNKS // 2, body)

        @block.vector
        def _(dve):
            def body(i):
                for c in range(2):
                    n = 2 * i + c
                    if holds_back(n - 1):
                        dve.wait_ge(done, n - 1)
                    dve.wait_ge(meaned, n + 1)
                    nc.vector.tensor_tensor(xc[:, c, :], cols(X, n * CHUNK, CHUNK), mean_ps[:, c, 0:CHUNK],
                                            ALU.subtract).then_inc(centred, 1)
                for c in range(2):
                    n = 2 * i + c
                    dve.wait_ge(rooted, n + 1)
                    nc.vector.reciprocal(rs[:, c, :], sd[:, c, :]).then_inc(inverted, 1)
                for c in range(2):
                    n = 2 * i + c
                    dve.wait_ge(inverted, n + 1)
                    nc.vector.tensor_tensor(cols(X, n * CHUNK, CHUNK), xc[:, c, :], rs[:, c, :],
                                            ALU.mult).then_inc(done, 1)
            looped(dve, CHUNKS // 2, body)


def batchnorm_params_phase(nc, name, items, eps):
    with Scope(nc, name) as s:
        K = len(items)
        stats = s.sb("stats", [P, K, CHUNKS, 6])
        mv, sd, rs, ms = s.sb("mv", [P, K, 2]), s.sb("sd", [P, K]), s.sb("rs", [P, K]), s.sb("ms", [P, K])
        counted, aggregated, rooted, step = s.sem("counted"), s.sem("aggregated"), s.sem("rooted"), s.sem("step")
        block = s.block()

        @block.vector
        def _(dve):
            for k, (region, *_) in enumerate(items):
                for c in range(CHUNKS):
                    end = min((c + 1) * CHUNK, N_NODES)
                    nc.vector.bn_stats(stats[:, k, c, :], region[:, c * CHUNK:end]).then_inc(counted, 1)
                dve.wait_ge(counted, (k + 1) * CHUNKS)
                nc.vector.bn_aggr(mv[:, k, :], stats[:, k, :, :].rearrange("p c s -> p (c s)")).then_inc(aggregated, 1)
            for k, (_, gamma, beta, scale, shift) in enumerate(items):
                dve.wait_ge(rooted, k + 1)
                nc.vector.reciprocal(rs[:, k:k + 1], sd[:, k:k + 1]).then_inc(step, 1)
                dve.wait_ge(step, 3 * k + 1)
                nc.vector.tensor_tensor(scale, rs[:, k:k + 1], gamma, ALU.mult).then_inc(step, 1)
                dve.wait_ge(step, 3 * k + 2)
                nc.vector.tensor_tensor(ms[:, k:k + 1], mv[:, k, 0:1], scale, ALU.mult).then_inc(step, 1)
                dve.wait_ge(step, 3 * k + 3)
                nc.vector.tensor_tensor(shift, beta, ms[:, k:k + 1], ALU.subtract)

        @block.scalar
        def _(act):
            for k in range(K):
                act.wait_ge(aggregated, k + 1)
                nc.scalar.activation(sd[:, k:k + 1], mv[:, k, 1:2], ACT.Sqrt, bias=eps[:, 0:1]).then_inc(rooted, 1)


def add_normed_phase(nc, name, out, base, H, scale, shift):
    cuts = [0, NP // 2, NP]
    with Scope(nc, name) as s:
        normed, done = s.sem("normed"), s.sem("done")
        block = s.block()

        @block.scalar
        def _(act):
            for a, b in zip(cuts, cuts[1:]):
                nc.scalar.activation(H[:, a:b], H[:, a:b], ACT.Identity, bias=shift, scale=scale).then_inc(normed, 1)

        @block.vector
        def _(dve):
            for j, (a, b) in enumerate(zip(cuts, cuts[1:])):
                dve.wait_ge(normed, j + 1)
                nc.vector.tensor_tensor(out[:, a:b], base[:, a:b], H[:, a:b], ALU.add).then_inc(done, 1)


def zero_phase(nc, name, regions):
    with Scope(nc, name) as s:
        block = s.block()

        @block.vector
        def _(dve):
            for r in regions:
                nc.vector.memset(r, 0.0)


class TensorMath:

    def __init__(self, nc, T, w, y, y_ea0, ea, y_ea1, w2_y0, dot, prod_a, prod_b):
        by_channel = "p t (c u) -> p t c u"
        self.nc, self.by3, self.w2_y0, self.dot, self.y_ea1 = nc, [P, T, 3, MUL], w2_y0, dot, y_ea1
        self.w = w.rearrange("p (t c u) -> p t c u", c=4, u=MUL)
        self.y, self.y_ea0 = y.rearrange(by_channel, u=MUL), y_ea0.rearrange(by_channel, u=MUL)
        self.a, self.b = prod_a.rearrange(by_channel, u=MUL), prod_b.rearrange(by_channel, u=MUL)
        self.ea1 = ea.rearrange("p (t x) -> p t x", x=4)[:, :, 1:4].unsqueeze(3).broadcast_to(self.by3)

    def mult(self, out, a, b):
        return self.nc.vector.tensor_tensor(out, a, b, ALU.mult)

    def y1_times_ea1(self):
        return self.mult(self.y_ea1, self.y[:, :, 1:4, :], self.ea1)

    def y0_weighed(self):
        return self.mult(self.w2_y0, self.w[:, :, 1, :], self.y[:, :, 0, :])

    def dot_first(self):
        return self.nc.vector.tensor_tensor(self.dot[:, :, 0, :], self.y_ea1[:, :, 0, :], self.y_ea1[:, :, 1, :], ALU.add)

    def dot_second(self):
        return self.nc.vector.tensor_tensor(self.dot[:, :, 1, :], self.dot[:, :, 0, :], self.y_ea1[:, :, 2, :], ALU.add)

    def a_scalars(self):
        return self.mult(self.a[:, :, 0, :], self.w[:, :, 0, :], self.y_ea0[:, :, 0, :])

    def a_vectors(self):
        return self.mult(self.a[:, :, 1:4, :], self.w[:, :, 2:3, :].broadcast_to(self.by3), self.y_ea0[:, :, 1:4, :])

    def b_vectors(self):
        return self.mult(self.b[:, :, 0:3, :], self.w2_y0.unsqueeze(2).broadcast_to(self.by3), self.ea1)

    def b_scalars(self):
        return self.mult(self.b[:, :, 3, :], self.w[:, :, 3, :], self.dot[:, :, 1, :])


def edge_pass(nc, gathers, name, kind, table, width, src_dram, rel, iota, bases, aggs, extra):
    tensor, gate, plain = kind == "tensor", kind == "gate", kind == "sum"
    A = 1 if gate else 2 if tensor else width // P
    with Scope(nc, name) as s:
        idx = s.sb("idx", [P, RING, GROUP_TILES], I32)
        rows = s.sb("rows", [P, RING, GROUP_TILES, width])
        hot = s.sb("hot", [P, 2, GROUP_TILES, WIN])
        sums = [s.ps(f"sums{a}", [P, 2, 512]) for a in range(A)]
        idx_loaded = [s.sem(f"idx_loaded{h}") for h in range(RING)]
        gathered = gathers.sems
        tick = s.sem("tick")
        hot_made, operands_made = s.sem("hot_made"), s.sem("operands_made")
        summed, added = s.sem("summed"), s.sem("added")
        if tensor:
            edge_in = s.sb("edge_in", [BASIS, 4, GROUP_TILES * P])
            hidden = s.sb("hidden", [HID, 2, GROUP_TILES * P])
            y_ea0, y_ea1 = s.sb("y_ea0", [P, 2, GROUP_TILES, P]), s.sb("y_ea1", [P, GROUP_TILES, 3, MUL])
            w2_y0, dot = s.sb("w2_y0", [P, GROUP_TILES, MUL]), s.sb("dot", [P, GROUP_TILES, 2, MUL])
            prod_a, prod_b = s.sb("prod_a", [P, 2, GROUP_TILES, P]), s.sb("prod_b", [P, 2, GROUP_TILES, P])
            ea0_made, step, dotted = s.sem("ea0_made"), s.sem("step"), s.sem("dotted")
            hidden_ps, weight_ps = s.ps("hidden", [P, 2, 512]), s.ps("weight", [P, 2, 512])
            edge_in_loaded = [s.sem(f"edge_in_loaded{h}") for h in range(4)]
            hidden_summed, hidden_made, weight_made = s.sem("hidden_summed"), s.sem("hidden_made"), s.sem("weight_made")
        if gate:
            sig = s.sb("sig", [P, 2, GROUP_TILES, WIN])
            hot_sig = s.sb("hot_sig", [P, 2, GROUP_TILES, WIN])
            slot_in = s.sb("slot_in", [P, 2, GROUP_TILES, SLOTS + 1])
            slot_ps = s.ps("slot", [P, 2, 512])
            sig_made, slot_made = s.sem("sig_made"), s.sem("slot_made")
        n_acc = A + (1 if gate else 0)
        block = s.block()

        @block.sync
        def _(sp):
            if tensor:
                for q in range(LOOK):
                    sp.dma_start(edge_in[:, q, :], extra["edge_in"][:, q * 512:(q + 1) * 512])\
                        .then_inc(edge_in_loaded[q], 16)

            def body(i):
                for h in range(RING):
                    q = i * RING + h
                    if holds_back(q - RING + 1):
                        sp.wait_ge(summed, q - RING + 1)
                    sp.dma_start(idx[:, h, :], cols(src_dram, q * GROUP_TILES, GROUP_TILES)).then_inc(idx_loaded[h], 16)
                    if tensor:
                        r = (h + LOOK) % 4
                        if holds_back(q + LOOK - 4 + 1):
                            sp.wait_ge(hidden_summed, q + LOOK - 4 + 1)
                        sp.dma_start(edge_in[:, r, :], cols(extra["edge_in"], (q + LOOK) * 512, 512))\
                            .then_inc(edge_in_loaded[r], 16)
            looped(sp, ITERS, body)
            if tensor:
                for r in range(4):
                    sp.wait_ge(edge_in_loaded[r], 16 * (ITERS + (r < LOOK)))

        @block.gpsimd
        def _(pool):
            def body(i):
                for h in range(RING):
                    q = i * RING + h
                    if holds_back(q - RING + 1):
                        pool.wait_ge(summed, q - RING + 1)
                    pool.wait_ge(idx_loaded[h], 16 * i + 16)
                    pool.sem_inc(tick, 1)
                    for t in range(GROUP_TILES):
                        nc.gpsimd.indirect_dma_start(
                            rows[:, h, t, :], None, table, bass.IndirectOffsetOnAxis(ap=idx[:, h, t:t + 1], axis=0)
                        ).then_inc(gathered[h], 16)
            looped(pool, ITERS, body)

        def load_bases(engine, at, count):
            _, values = nc.values_load_multi_w_load_instructions(
                bases[0:1, bass.ds(at, count)], engines=[engine], min_val=0, max_val=N_NODES - 1,
                skip_runtime_bounds_check_because="bases are nodes: 0 to N_NODES - 1")
            return values

        @block.scalar
        def _(act):
            if tensor:
                def silu(q, r):
                    if holds_back(q - 1):
                        act.wait_ge(weight_made, q - 1)
                    act.wait_ge(hidden_summed, q + 1)
                    nc.scalar.activation(hidden[:, r, :], hidden_ps[0:HID, r, :], ACT.Silu,
                                         scale=1.0 / math.sqrt(BASIS)).then_inc(hidden_made, 1)
                silu(0, 0)

                def body(i):
                    for h in range(RING):
                        q, r = i * RING + h, h % 2
                        silu(q + 1, (h + 1) % 2)
                        if holds_back(q - 1):
                            act.wait_ge(operands_made, q - 1)
                        act.wait_ge(gathered[h], gathers.count(h, GROUP_TILES * (i + 1)))
                        for t in range(GROUP_TILES):
                            ins = nc.scalar.activation(y_ea0[:, r, t, :], rows[:, h, t, :], ACT.Copy,
                                                       scale=cols(extra["edge_attr"], (q * GROUP_TILES + t) * 4, 1))
                        ins.then_inc(ea0_made, 1)
                looped(act, ITERS, body)
            if gate:
                def body(i):
                    base = load_bases(ACT_E, i * RING + 1, RING)
                    for h in range(RING):
                        q, r = i * RING + h, h % 2
                        if holds_back(q - 1):
                            act.wait_ge(summed, q - 1)
                        nc.scalar.activation(slot_in[:, r, :, :].rearrange("p t c -> p (t c)"),
                                             cols(extra["slots"], q * GROUP_TILES * (SLOTS + 1), GROUP_TILES * (SLOTS + 1)),
                                             ACT.Identity).then_inc(slot_made, 1)
                        if holds_back(q - 1):
                            act.wait_ge(operands_made, q - 1)
                        act.wait_ge(gathered[h], gathers.count(h, GROUP_TILES * (i + 1)))
                        for t in range(GROUP_TILES):
                            ins = nc.scalar.activation(sig[:, r, t, :], cols(extra["at_dst"], base[h], WIN),
                                                       ACT.Sigmoid, bias=rows[:, h, t, P:P + 1])
                        ins.then_inc(sig_made, 1)
                looped(act, ITERS, body)

        @block.tensor
        def _(pe):
            def hidden_layer(i, q, r4):
                if holds_back(q - 1):
                    pe.wait_ge(hidden_made, q - 1)
                pe.wait_ge(edge_in_loaded[r4], 16 * i + 16)
                nc.tensor.matmul(hidden_ps[0:HID, r4 % 2, :], extra["w_fc1"], edge_in[:, r4, :],
                                 start=True, stop=True).then_inc(hidden_summed, 1)

            def weights(q, r):
                if holds_back(q - 1):
                    pe.wait_ge(operands_made, q - 1)
                pe.wait_ge(hidden_made, q + 1)
                for t in range(GROUP_TILES):
                    ins = nc.tensor.matmul(weight_ps[:, r, t * P:(t + 1) * P], hidden[:, r, t * P:(t + 1) * P],
                                           extra["w_fc2"], start=True, stop=True)
                ins.then_inc(weight_made, 1)

            if tensor:
                hidden_layer(0, 0, 0)
                hidden_layer(0, 1, 1)
                weights(0, 0)

            def body(i):
                for h in range(RING):
                    q, r = i * RING + h, h % 2
                    if tensor:
                        r4 = (h + LOOK) % 4
                        hidden_layer(i + (1 if h + LOOK >= 4 else 0), q + LOOK, r4)
                        weights(q + 1, (h + 1) % 2)
                    if holds_back((q - 1) * n_acc):
                        pe.wait_ge(added, (q - 1) * n_acc)
                    if gate:
                        pe.wait_ge(slot_made, q + 1)
                    if not plain:
                        pe.wait_ge(operands_made, q + 1)
                    else:
                        pe.wait_ge(hot_made, q + 1)
                        pe.wait_ge(gathered[h], gathers.count(h, GROUP_TILES * (i + 1)))
                    for t in range(GROUP_TILES):
                        first, last = t == 0, t == GROUP_TILES - 1
                        if plain:
                            for a in range(A):
                                ins = nc.tensor.matmul(sums[a][:, r, 0:WIN], rows[:, h, t, a * P:(a + 1) * P],
                                                       hot[:, r, t, :], start=first, stop=last)
                        elif gate:
                            nc.tensor.matmul(sums[0][:, r, 0:WIN], rows[:, h, t, 0:P], hot_sig[:, r, t, :],
                                             start=first, stop=last)
                            ins = nc.tensor.matmul(slot_ps[0:SLOTS + 1, r, 0:WIN], slot_in[:, r, t, :],
                                                   hot[:, r, t, :], start=first, stop=last)
                        else:
                            nc.tensor.matmul(sums[0][:, r, 0:WIN], prod_a[:, r, t, :], hot[:, r, t, :],
                                             start=first, stop=last)
                            ins = nc.tensor.matmul(sums[1][:, r, 0:WIN], prod_b[:, r, t, :], hot[:, r, t, :],
                                                   start=first, stop=last)
                    ins.then_inc(summed, 1)
            looped(pe, ITERS, body)

        @block.vector
        def _(dve):
            targets = [(sums[a], P, aggs[a]) for a in range(A)]
            if gate:
                targets.append((slot_ps, SLOTS + 1, extra["slot_sums"]))

            def add_up(q, r, start):
                dve.wait_ge(summed, q + 1)
                if holds_back(q * n_acc):
                    dve.wait_ge(added, q * n_acc)
                for a, (ps, rws, region) in enumerate(targets):
                    into = region[0:rws, bass.ds(start, WIN)]
                    nc.vector.tensor_tensor(into, into, ps[0:rws, r, 0:WIN], ALU.add).then_inc(added, 1)

            def operands(i, h):
                q, r = i * RING + h, h % 2
                if holds_back(q - 1):
                    dve.wait_ge(summed, q - 1)
                nc.vector.tensor_tensor(hot[:, r, :, :], iota[:].unsqueeze(1).broadcast_to([P, GROUP_TILES, WIN]),
                                        cols(rel, q * GROUP_TILES, GROUP_TILES).unsqueeze(2).broadcast_to([P, GROUP_TILES, WIN]),
                                        ALU.is_equal).then_inc(hot_made, 1)
                if gate:
                    dve.wait_ge(hot_made, q + 1)
                    dve.wait_ge(sig_made, q + 1)
                    nc.vector.tensor_tensor(hot_sig[:, r, :, :], hot[:, r, :, :], sig[:, r, :, :],
                                            ALU.mult).then_inc(operands_made, 1)
                if tensor:
                    m = TensorMath(nc, GROUP_TILES, weight_ps[:, r, :], rows[:, h, :, :], y_ea0[:, r, :, :],
                                   cols(extra["edge_attr"], q * GROUP_TILES * 4, GROUP_TILES * 4), y_ea1[:],
                                   w2_y0[:], dot[:], prod_a[:, r, :, :], prod_b[:, r, :, :])
                    dve.wait_ge(gathered[h], gathers.count(h, GROUP_TILES * (i + 1)))
                    if holds_back(q):
                        dve.wait_ge(operands_made, q)
                    m.y1_times_ea1().then_inc(step, 1)
                    dve.wait_ge(weight_made, q + 1)
                    m.y0_weighed().then_inc(step, 1)
                    dve.wait_ge(step, 3 * q + 1)
                    m.dot_first().then_inc(step, 1)
                    dve.wait_ge(ea0_made, q + 1)
                    m.a_scalars()
                    dve.wait_ge(step, 3 * q + 3)
                    m.dot_second().then_inc(dotted, 1)
                    m.b_vectors()
                    m.a_vectors()
                    dve.wait_ge(dotted, q + 1)
                    m.b_scalars().then_inc(operands_made, 1)

            def body(i):
                starts = load_bases(DVE_E, i * RING, RING)
                for h in range(RING):
                    operands(i, h)
                    if not (isinstance(i, int) and i == 0 and h == 0):
                        add_up(i * RING + h - 1, (h - 1) % 2, starts[h])
            looped(dve, ITERS, body)
            add_up(GROUPS - 1, (GROUPS - 1) % 2, load_bases(DVE_E, GROUPS, 1)[0])
            dve.wait_ge(added, GROUPS * n_acc)
    gathers.end_phase(RING, GROUP_TILES * ITERS)


class Far:

    def __init__(self, nc, sb):
        self.any, self.group = sb("far_any", [1, 1], I32), sb("far_group", [1, WINDOWS], I32)
        self.shift = sb("far_shift", [P, WINDOWS])
        self.gathered = nc.alloc_semaphore("far_gathered", 250)
        self.passes = 0


def prep_phase(nc, rel, bases, far, inputs, ident):
    with Scope(nc, "prep") as s:
        dst, base_bc = s.sb("dst", [P, TILES], I32), s.sb("base_bc", [P, GROUPS], I32)
        base_cols, starts = s.sb("base_cols", [P, 2, BASE_COLS], I32), s.sb("starts", [P, WINDOWS])
        base_f, delta = s.sb("base_f", [P, BASE_COLS]), s.sb("delta", [P, BASE_COLS])
        ones = s.sb("ones", [P, P])
        passed, stepped = s.sb("passed", [P, BASE_COLS, WINDOWS]), s.sb("stepped", [P, BASE_COLS, WINDOWS])
        last, none, off = s.sb("last", [P, WINDOWS]), s.sb("none", [P, WINDOWS]), s.sb("off", [P, WINDOWS])
        most, top = s.sb("most", [P, 1]), s.sb("top", [1, 1])
        count_ps, base_ps, most_ps = s.ps("count", [P, 512]), s.ps("base", [P, 512]), s.ps("most", [1, 512])
        loaded, step, counted, turned = s.sem("loaded"), s.sem("step"), s.sem("counted"), s.sem("turned")
        block = s.block()

        @block.sync
        def _(sp):
            sp.dma_start(dst[:], inputs["dst"]).then_inc(loaded, 16)
            sp.dma_start(base_bc[:], inputs["bases"][0:1, 1:1 + GROUPS].broadcast_to([P, GROUPS])).then_inc(loaded, 16)
            sp.dma_start(bases[:], inputs["bases"]).then_inc(loaded, 16)
            sp.dma_start(base_cols[:].rearrange("p a k -> p (a k)"), inputs["base_cols"]).then_inc(loaded, 16)
            sp.dma_start(starts[:], inputs["win_start"]).then_inc(loaded, 16)
            sp.wait_ge(loaded, 80)

        @block.vector
        def _(dve):
            done = 0

            def after(ins):
                nonlocal done
                done += 1
                ins.then_inc(step, 1)
                dve.wait_ge(step, done)

            dve.wait_ge(loaded, 80)
            nc.vector.memset(ones[:], 1.0)
            nc.vector.tensor_copy(base_f[:], base_cols[:, 0, :])
            nc.vector.tensor_tensor(delta[:], base_cols[:, 0, :], base_cols[:, 1, :], ALU.subtract)
            shape = [P, GROUPS, GROUP_TILES]
            after(nc.vector.tensor_tensor(rel[:, 0:TILES].rearrange("p (g t) -> p g t", t=GROUP_TILES),
                                          dst[:].rearrange("p (g t) -> p g t", t=GROUP_TILES),
                                          base_bc[:].unsqueeze(2).broadcast_to(shape), ALU.subtract))
            for k in range(BASE_COLS):
                nc.vector.tensor_scalar(passed[:, k, :], starts[:], base_f[:, k:k + 1], None, ALU.is_gt)
            for k in range(BASE_COLS):
                nc.vector.tensor_scalar(stepped[:, k, :], starts[:], base_f[:, k:k + 1], delta[:, k:k + 1],
                                        ALU.is_gt, ALU.mult)
            after(nc.vector.reduce_max(most[:], rel[:, 0:TILES], mybir.AxisListType.X))
            dve.wait_ge(counted, 1)
            nc.vector.tensor_scalar(far.group[:], count_ps[0:1, 0:WINDOWS], -1.0, 0.0, ALU.add, ALU.max)
            after(nc.vector.tensor_copy(last[:], base_ps[:, 0:WINDOWS]))
            nc.vector.tensor_scalar(none[:], last[:], 0.0, -float(after_all_nodes()), ALU.is_equal, ALU.mult)
            after(nc.vector.scalar_tensor_tensor(off[:], last[:], -1.0, starts[:], ALU.add, ALU.subtract))
            nc.vector.tensor_tensor(far.shift[:], off[:], none[:], ALU.add)
            dve.wait_ge(turned, 1)
            after(nc.vector.reduce_max(top[:], most_ps[:, 0:P], mybir.AxisListType.X))
            nc.vector.tensor_scalar(far.any[:], top[:], float(WIN), None, ALU.is_ge)

        @block.tensor
        def _(pe):
            pe.wait_ge(step, 2)
            for src, ps in ((passed, count_ps), (stepped, base_ps)):
                for k in range(BASE_COLS):
                    ins = nc.tensor.matmul(ps[:, 0:WINDOWS], ones[:], src[:, k, :],
                                           start=(k == 0), stop=(k == BASE_COLS - 1))
            ins.then_inc(counted, 1)
            nc.tensor.transpose(most_ps[:, 0:P], most[:], ident[:]).then_inc(turned, 1)


def after_all_nodes():
    return 1 << 17


def far_pass(nc, far, name, kind, table, width, src_dram, rel, iota, aggs, extra):
    tensor, gate, plain = kind == "tensor", kind == "gate", kind == "sum"
    A = 1 if gate else 2 if tensor else width // P
    T = GROUP_TILES
    before = far.passes * (WINDOWS - 1) * T * 16
    with Scope(nc, name) as s:
        idx, rows = s.sb("idx", [P, T], I32), s.sb("rows", [P, T, width])
        moved, match, past = s.sb("moved", [P, T]), s.sb("match", [P, T, WIN]), s.sb("past", [P, T])
        hot = s.sb("hot", [P, T, WIN])
        sums = [s.ps(f"sums{a}", [P, 512]) for a in range(A)]
        loaded, step, hot_made, summed = s.sem("loaded"), s.sem("step"), s.sem("hot_made"), s.sem("summed")
        done, tick, sp_tick, operands_made = s.sem("done"), s.sem("tick"), s.sem("sp_tick"), s.sem("operands_made")
        targets = [(sums[a], P, aggs[a]) for a in range(A)]
        if tensor:
            edge_in, hidden = s.sb("edge_in", [BASIS, T * P]), s.sb("hidden", [HID, T * P])
            y_ea0, y_ea1 = s.sb("y_ea0", [P, T, P]), s.sb("y_ea1", [P, T, 3, MUL])
            w2_y0, dot = s.sb("w2_y0", [P, T, MUL]), s.sb("dot", [P, T, 2, MUL])
            prod_a, prod_b = s.sb("prod_a", [P, T, P]), s.sb("prod_b", [P, T, P])
            hidden_ps, weight_ps = s.ps("hidden", [P, 512]), s.ps("weight", [P, 512])
            hidden_summed, hidden_made, weight_made = s.sem("hidden_summed"), s.sem("hidden_made"), s.sem("weight_made")
            ea0_made, prepared = s.sem("ea0_made"), s.sem("prepared")
        if gate:
            sig, hot_sig = s.sb("sig", [P, T, WIN]), s.sb("hot_sig", [P, T, WIN])
            slot_in = s.sb("slot_in", [P, T * (SLOTS + 1)])
            slot_ps = s.ps("slot", [P, 512])
            sig_made = s.sem("sig_made")
            targets.append((slot_ps, SLOTS + 1, extra["slot_sums"]))
        STEPS = 1 + len(targets)
        block = s.block()

        def windows(eng, body, group=True):
            with eng.If(eng.value_load(far.any[0:1, 0:1], min_val=0, max_val=1)):
                with eng.Fori(1, WINDOWS) as w:
                    body(w, eng.value_load(far.group[0:1, bass.ds(w, 1)], min_val=0, max_val=GROUPS - 1) if group else None)

        @block.sync
        def _(sp):
            def body(w, g):
                sp.wait_ge(done, w)
                sp.sem_inc(sp_tick, 1)
                sp.dma_start(idx[:], cols(src_dram, g * T, T)).then_inc(loaded, 16)
                if tensor:
                    sp.dma_start(edge_in[:], cols(extra["edge_in"], g * (T * P), T * P)).then_inc(loaded, 16)
            windows(sp, body)

        @block.gpsimd
        def _(pool):
            def body(w, g):
                pool.wait_ge(loaded, w * (32 if tensor else 16))
                pool.sem_inc(tick, 1)
                for t in range(T):
                    nc.gpsimd.indirect_dma_start(
                        rows[:, t, :], None, table, bass.IndirectOffsetOnAxis(ap=idx[:, t:t + 1], axis=0)
                    ).then_inc(far.gathered, 16)
            windows(pool, body, group=False)

        @block.scalar
        def _(act):
            if tensor:
                def body(w, g):
                    act.wait_ge(hidden_summed, w)
                    nc.scalar.activation(hidden[:], hidden_ps[0:HID, 0:T * P], ACT.Silu,
                                         scale=1.0 / math.sqrt(BASIS)).then_inc(hidden_made, 1)
                    act.wait_ge(far.gathered, w * (16 * T) + before)
                    for t in range(T):
                        ins = nc.scalar.activation(y_ea0[:, t, :], rows[:, t, :], ACT.Copy,
                                                   scale=cols(extra["edge_attr"], g * (T * 4) + t * 4, 1))
                    ins.then_inc(ea0_made, 1)
                windows(act, body)
            if gate:
                def body(w, g):
                    act.wait_ge(done, w)
                    nc.scalar.activation(slot_in[:], cols(extra["slots"], g * (T * (SLOTS + 1)), T * (SLOTS + 1)), ACT.Identity)
                    act.wait_ge(far.gathered, w * (16 * T) + before)
                    for t in range(T):
                        ins = nc.scalar.activation(sig[:, t, :], cols(extra["at_dst"], w * WIN, WIN),
                                                   ACT.Sigmoid, bias=rows[:, t, P:P + 1])
                    ins.then_inc(sig_made, 1)
                windows(act, body)

        @block.tensor
        def _(pe):
            def body(w, _):
                if tensor:
                    pe.wait_ge(loaded, w * 32)
                    nc.tensor.matmul(hidden_ps[0:HID, 0:T * P], extra["w_fc1"], edge_in[:],
                                     start=True, stop=True).then_inc(hidden_summed, 1)
                    pe.wait_ge(hidden_made, w)
                    for t in range(T):
                        ins = nc.tensor.matmul(weight_ps[:, t * P:(t + 1) * P], hidden[:, t * P:(t + 1) * P],
                                               extra["w_fc2"], start=True, stop=True)
                    ins.then_inc(weight_made, 1)
                if plain:
                    pe.wait_ge(hot_made, w)
                    pe.wait_ge(far.gathered, w * (16 * T) + before)
                else:
                    pe.wait_ge(operands_made, w)
                for t in range(T):
                    first, last = t == 0, t == T - 1
                    if plain:
                        for a in range(A):
                            ins = nc.tensor.matmul(sums[a][:, 0:WIN], rows[:, t, a * P:(a + 1) * P], hot[:, t, :],
                                                   start=first, stop=last)
                    elif gate:
                        nc.tensor.matmul(sums[0][:, 0:WIN], rows[:, t, 0:P], hot_sig[:, t, :], start=first, stop=last)
                        ins = nc.tensor.matmul(slot_ps[0:SLOTS + 1, 0:WIN],
                                               slot_in[:, t * (SLOTS + 1):(t + 1) * (SLOTS + 1)], hot[:, t, :],
                                               start=first, stop=last)
                    else:
                        nc.tensor.matmul(sums[0][:, 0:WIN], prod_a[:, t, :], hot[:, t, :], start=first, stop=last)
                        ins = nc.tensor.matmul(sums[1][:, 0:WIN], prod_b[:, t, :], hot[:, t, :], start=first, stop=last)
                ins.then_inc(summed, 1)
            windows(pe, body, group=False)

        @block.vector
        def _(dve):
            dve.sem_inc(done, 1)

            def body(w, g):
                dve.wait_ge(done, w)
                r = cols(rel, g * T, T)
                shape = [P, T, WIN]
                nc.vector.tensor_scalar(past[:], r, float(WIN), None, ALU.is_ge)
                nc.vector.tensor_scalar(moved[:], r, cols(far.shift, w, 1), None, ALU.add).then_inc(step, 1)
                dve.wait_ge(step, w * 2 - 1)
                nc.vector.tensor_tensor(match[:], iota[:].unsqueeze(1).broadcast_to(shape),
                                        moved[:].unsqueeze(2).broadcast_to(shape), ALU.is_equal).then_inc(step, 1)
                dve.wait_ge(step, w * 2)
                nc.vector.tensor_tensor(hot[:], match[:], past[:].unsqueeze(2).broadcast_to(shape),
                                        ALU.mult).then_inc(hot_made, 1)
                if gate:
                    dve.wait_ge(hot_made, w)
                    dve.wait_ge(sig_made, w)
                    nc.vector.tensor_tensor(hot_sig[:], hot[:], sig[:], ALU.mult).then_inc(operands_made, 1)
                if tensor:
                    m = TensorMath(nc, T, weight_ps[:, 0:T * P], rows[:], y_ea0[:],
                                   cols(extra["edge_attr"], g * (T * 4), T * 4), y_ea1[:], w2_y0[:], dot[:],
                                   prod_a[:], prod_b[:])
                    dve.wait_ge(far.gathered, w * (16 * T) + before)
                    m.y1_times_ea1()
                    dve.wait_ge(weight_made, w)
                    m.y0_weighed().then_inc(prepared, 1)
                    dve.wait_ge(prepared, w * 3 - 2)
                    m.dot_first().then_inc(prepared, 1)
                    dve.wait_ge(prepared, w * 3 - 1)
                    m.dot_second().then_inc(prepared, 1)
                    dve.wait_ge(ea0_made, w)
                    m.a_scalars()
                    m.a_vectors()
                    m.b_vectors()
                    dve.wait_ge(prepared, w * 3)
                    m.b_scalars().then_inc(operands_made, 1)
                dve.wait_ge(summed, w)
                for ps, rws, region in targets:
                    into = region[0:rws, bass.ds(w * WIN, WIN)]
                    ins = nc.vector.tensor_tensor(into, into, ps[0:rws, 0:WIN], ALU.add)
                ins.then_inc(done, 1)
            windows(dve, body)
    far.passes += 1


def tensor_post_phase(nc, X, aggs, lhs, attr_bc):
    with Scope(nc, "tpost") as s:
        acc = s.ps("acc", [P, 2, 512])
        scaled = s.sb("scaled", [P, 2, CHUNK])
        summed, weighed, added = s.sem("summed"), s.sem("weighed"), s.sem("added")
        block = s.block()

        @block.tensor
        def _(pe):
            def body(i):
                for c in range(2):
                    n = i * 2 + c
                    if holds_back(n - 1):
                        pe.wait_ge(weighed, n - 1)
                    for k, region in enumerate([X] + aggs):
                        ins = nc.tensor.matmul(acc[:, c, 0:CHUNK], lhs[k], cols(region, n * CHUNK, CHUNK),
                                               start=(k == 0), stop=(k == len(aggs)))
                    ins.then_inc(summed, 1)
            looped(pe, CHUNKS // 2, body)

        @block.vector
        def _(dve):
            def body(i):
                for c in range(2):
                    n = i * 2 + c
                    dve.wait_ge(summed, n + 1)
                    if holds_back(n - 1):
                        dve.wait_ge(added, n - 1)
                    nc.vector.tensor_tensor(scaled[:, c, :], acc[:, c, 0:CHUNK], cols(attr_bc, n * CHUNK, CHUNK),
                                            ALU.mult).then_inc(weighed, 1)
                for c in range(2):
                    n = i * 2 + c
                    dve.wait_ge(weighed, n + 1)
                    nc.vector.tensor_tensor(cols(X, n * CHUNK, CHUNK), cols(X, n * CHUNK, CHUNK), scaled[:, c, :],
                                            ALU.add).then_inc(added, 1)
            looped(dve, CHUNKS // 2, body)


def slot_columns_phase(nc, inputs, slots):
    with Scope(nc, "slotc") as s:
        dst, src = s.sb("dst", [P, TILES], I32), s.sb("src", [P, TILES], I32)
        before = s.sb("before", [P, SLOTS, TILES], I32)
        ge = s.sb("ge", [P, SLOTS, TILES])
        rank = s.sb("rank", [P, SLOTS, TILES])
        loaded, step = s.sem("loaded"), s.sem("step")
        block = s.block()

        @block.sync
        def _(sp):
            sp.dma_start(dst[:], inputs["dst"]).then_inc(loaded, 16)
            sp.dma_start(src[:], inputs["src"]).then_inc(loaded, 16)
            sp.dma_start(before[:].rearrange("p s t -> p (s t)"), inputs["dst_before"]).then_inc(loaded, 16)
            sp.wait_ge(loaded, 48)

        @block.vector
        def _(dve):
            dve.wait_ge(loaded, 48)
            out = slots.rearrange("p (t c) -> p t c", c=SLOTS + 1)
            nc.vector.tensor_tensor(ge[:], before[:], dst[:].unsqueeze(1).broadcast_to([P, SLOTS, TILES]),
                                    ALU.is_equal).then_inc(step, 1)
            nc.vector.memset(out[:, :, SLOTS:SLOTS + 1], 1.0)
            dve.wait_ge(step, 1)
            nc.vector.tensor_scalar(rank[:, 0, :], ge[:, 0, :], -1.0, 1.0, ALU.mult, ALU.add)
            nc.vector.tensor_tensor(rank[:, 1:SLOTS, :], ge[:, 0:SLOTS - 1, :], ge[:, 1:SLOTS, :],
                                    ALU.subtract).then_inc(step, 1)
            dve.wait_ge(step, 2)
            for j in range(SLOTS):
                nc.vector.tensor_tensor(out[:, :, j], rank[:, j, :], src[:], ALU.mult)


def slot_tables_phase(nc, slot_sums, slot_idx, inv_count, ident, pick_count):
    C = SLOTS + 1
    with Scope(nc, "slott") as s:
        turned = s.ps("turned", [P, BLOCKS * C])
        spread = s.ps("spread", [P, 2, 512])
        cnt = s.sb("cnt", [P, 2, CHUNK])
        sl, empty, full = s.sb("sl", [P, BLOCKS, C]), s.sb("empty", [P, BLOCKS, SLOTS]), s.sb("full", [P, BLOCKS, SLOTS])
        flipped, spreaded, floored, step, inverted = (s.sem("flipped"), s.sem("spreaded"), s.sem("floored"),
                                                      s.sem("step"), s.sem("inverted"))
        block = s.block()

        @block.tensor
        def _(pe):
            for b in range(BLOCKS):
                ins = nc.tensor.transpose(turned[:, b * C:(b + 1) * C], slot_sums[0:C, b * P:(b + 1) * P], ident[0:C, 0:C])
            ins.then_inc(flipped, 1)

            def body(i):
                for c in range(2):
                    n = 2 * i + c
                    if holds_back(n - 1):
                        pe.wait_ge(floored, n - 1)
                    nc.tensor.matmul(spread[:, c, 0:CHUNK], pick_count, slot_sums[0:C, bass.ds(n * CHUNK, CHUNK)],
                                     start=True, stop=True).then_inc(spreaded, 1)
            looped(pe, CHUNKS // 2, body)

        @block.vector
        def _(dve):
            dve.wait_ge(flipped, 1)
            nc.vector.tensor_copy(sl[:].rearrange("p b c -> p (b c)"), turned[:]).then_inc(step, 1)
            dve.wait_ge(step, 1)
            for j in range(SLOTS):
                ins = nc.vector.tensor_scalar(empty[:, :, j], sl[:, :, SLOTS], float(j), float(N_NODES), ALU.is_le, ALU.mult)
            ins.then_inc(step, 1)
            dve.wait_ge(step, 2)
            nc.vector.tensor_tensor(slot_idx.rearrange("p (b s) -> p b s", s=SLOTS), sl[:, :, 0:SLOTS], empty[:], ALU.add)

            def body(i):
                for c in range(2):
                    n = 2 * i + c
                    dve.wait_ge(spreaded, n + 1)
                    if holds_back(n - 1):
                        dve.wait_ge(inverted, n - 1)
                    nc.vector.tensor_scalar(cnt[:, c, :], spread[:, c, 0:CHUNK], 1.0, None, ALU.max).then_inc(floored, 1)
                for c in range(2):
                    n = 2 * i + c
                    dve.wait_ge(floored, n + 1)
                    nc.vector.reciprocal(cols(inv_count, n * CHUNK, CHUNK), cnt[:, c, :]).then_inc(inverted, 1)
            looped(dve, CHUNKS // 2, body)


def gru_phase(nc, X, agg, H, w):
    names = ("r", "z", "in", "hn")
    with Scope(nc, "gru") as s:
        ps = {g: s.ps(g, [P, 2, 512]) for g in names}
        t = {g: s.sb(g, [P, 2, CHUNK]) for g in ("r", "z", "hn", "rh", "pre", "n", "d", "e")}
        summed, gated, mixed, tanhed, done, step = (s.sem("summed"), s.sem("gated"), s.sem("mixed"),
                                                    s.sem("tanhed"), s.sem("done"), s.sem("step"))
        block = s.block()

        @block.tensor
        def _(pe):
            def body(i):
                for c in range(2):
                    n = 2 * i + c
                    if holds_back(n - 1):
                        pe.wait_ge(gated, n - 1)
                    if holds_back(n - 1):
                        pe.wait_ge(mixed, n - 1)
                    x, m = cols(X, n * CHUNK, CHUNK), cols(agg, n * CHUNK, CHUNK)
                    for k, g in enumerate(("r", "z")):
                        nc.tensor.matmul(ps[g][:, c, 0:CHUNK], w["ih"][:, k * P:(k + 1) * P], m, start=True, stop=False)
                        nc.tensor.matmul(ps[g][:, c, 0:CHUNK], w["hh"][:, k * P:(k + 1) * P], x, start=False, stop=True)
                    nc.tensor.matmul(ps["in"][:, c, 0:CHUNK], w["ih"][:, 2 * P:3 * P], m, start=True, stop=True)
                    nc.tensor.matmul(ps["hn"][:, c, 0:CHUNK], w["hh"][:, 2 * P:3 * P], x, start=True, stop=True).then_inc(summed, 1)
            looped(pe, CHUNKS // 2, body)

        @block.scalar
        def _(act):
            def body(i):
                for c in range(2):
                    n = 2 * i + c
                    if holds_back(n - 1):
                        act.wait_ge(done, n - 1)
                    act.wait_ge(summed, n + 1)
                    nc.scalar.activation(t["r"][:, c, :], ps["r"][:, c, 0:CHUNK], ACT.Sigmoid, bias=w["b_r"])
                    nc.scalar.activation(t["z"][:, c, :], ps["z"][:, c, 0:CHUNK], ACT.Sigmoid, bias=w["b_z"])
                    nc.scalar.activation(t["hn"][:, c, :], ps["hn"][:, c, 0:CHUNK], ACT.Identity, bias=w["b_hn"]).then_inc(gated, 1)
                for c in range(2):
                    n = 2 * i + c
                    act.wait_ge(mixed, n + 1)
                    nc.scalar.activation(t["n"][:, c, :], t["pre"][:, c, :], ACT.Tanh, bias=w["b_in"]).then_inc(tanhed, 1)
            looped(act, CHUNKS // 2, body)

        @block.vector
        def _(dve):
            def body(i):
                for c in range(2):
                    n = 2 * i + c
                    dve.wait_ge(gated, n + 1)
                    if holds_back(n - 1):
                        dve.wait_ge(tanhed, n - 1)
                    nc.vector.tensor_tensor(t["rh"][:, c, :], t["r"][:, c, :], t["hn"][:, c, :], ALU.mult).then_inc(step, 1)
                    dve.wait_ge(step, 6 * i + c + 1)
                    nc.vector.tensor_tensor(t["pre"][:, c, :], t["rh"][:, c, :], ps["in"][:, c, 0:CHUNK],
                                            ALU.add).then_inc(mixed, 1)
                for c in range(2):
                    n = 2 * i + c
                    dve.wait_ge(tanhed, n + 1)
                    nc.vector.tensor_tensor(t["d"][:, c, :], cols(X, n * CHUNK, CHUNK), t["n"][:, c, :],
                                            ALU.subtract).then_inc(step, 1)
                    dve.wait_ge(step, 6 * i + 2 + 2 * c + 1)
                    nc.vector.tensor_tensor(t["e"][:, c, :], t["d"][:, c, :], t["z"][:, c, :], ALU.mult).then_inc(step, 1)
                    dve.wait_ge(step, 6 * i + 2 + 2 * c + 2)
                    nc.vector.tensor_tensor(cols(H, n * CHUNK, CHUNK), t["e"][:, c, :], t["n"][:, c, :],
                                            ALU.add).then_inc(done, 1)
            looped(dve, CHUNKS // 2, body)


def blank_row_phase(nc, name, blank, w_T, b_row, table):
    with Scope(nc, name) as s:
        ps, row = s.ps("ps", [1, P]), s.sb("row", [1, P])
        summed, added, stored = s.sem("summed"), s.sem("added"), s.sem("stored")
        block = s.block()

        @block.tensor
        def _(pe):
            nc.tensor.matmul(ps[:], blank, w_T, start=True, stop=True).then_inc(summed, 1)

        @block.vector
        def _(dve):
            dve.wait_ge(summed, 1)
            nc.vector.tensor_tensor(row[:], ps[:], b_row, ALU.add).then_inc(added, 1)

        @block.sync
        def _(sp):
            sp.wait_ge(added, 1)
            sp.dma_start(table[N_NODES:N_NODES + 1, :], row[:]).then_inc(stored, 16)
            sp.wait_ge(stored, 16)


def sort_phase(nc, gathers, name, X, H, table, slot_idx, w, ident):
    SUB = 7
    with Scope(nc, name) as s:
        idx = s.sb("idx", [P, SUB, SLOTS], I32)
        rows = s.sb("rows", [P, SUB, SLOTS, P])
        t1, t2, t3 = s.sb("t1", [P, SLOTS, P]), s.sb("t2", [P, SLOTS, P]), s.sb("t3", [P, 2, P])
        acc = s.sb("acc", [P, 3, P])
        out = s.sb("out", [P, SUB, P])
        turned = s.ps("turned", [P, SUB, 512])
        idx_copied = [s.sem(f"idx_copied{b}") for b in range(SUB)]
        gathered = gathers.sems
        tick, step, sorted_, flipped, done = s.sem("tick"), s.sem("step"), s.sem("sorted"), s.sem("flipped"), s.sem("done")
        block = s.block()

        @block.sync
        def _(sp):
            def body(i):
                for b in range(SUB):
                    n = i * SUB + b
                    if holds_back(n - SUB + 1):
                        sp.wait_ge(sorted_, n - SUB + 1)
                    sp.dma_start(idx[:, b, :], cols(slot_idx, n * SLOTS, SLOTS)).then_inc(idx_copied[b], 16)
            looped(sp, BLOCKS // SUB, body)

        @block.gpsimd
        def _(pool):
            def body(i):
                for b in range(SUB):
                    n = i * SUB + b
                    if holds_back(n - SUB + 1):
                        pool.wait_ge(sorted_, n - SUB + 1)
                    pool.wait_ge(idx_copied[b], 16 * i + 16)
                    pool.sem_inc(tick, 1)
                    for j in range(SLOTS):
                        nc.gpsimd.indirect_dma_start(
                            rows[:, b, j, :], None, table, bass.IndirectOffsetOnAxis(ap=idx[:, b, j:j + 1], axis=0)
                        ).then_inc(gathered[b], 16)
            looped(pool, BLOCKS // SUB, body)

        @block.tensor
        def _(pe):
            def body(i):
                for b in range(SUB):
                    n = i * SUB + b
                    if holds_back(n - SUB + 1):
                        pe.wait_ge(done, n - SUB + 1)
                    pe.wait_ge(sorted_, n + 1)
                    nc.tensor.transpose(turned[:, b, 0:P], out[:, b, :], ident[:]).then_inc(flipped, 1)
            looped(pe, BLOCKS // SUB, body)

        @block.vector
        def _(dve):
            STEPS = 5

            def finish(n, b):
                dve.wait_ge(flipped, n + 1)
                nc.vector.scalar_tensor_tensor(cols(H, n * P, P), cols(X, n * P, P), w["a"], turned[:, b, 0:P],
                                               ALU.mult, ALU.add).then_inc(done, 1)

            def body(i):
                for b in range(SUB):
                    n = i * SUB + b

                    def after(k):
                        dve.wait_ge(step, n * STEPS + k)
                    dve.wait_ge(gathered[b], gathers.count(b, SLOTS * (i + 1)))
                    if holds_back(n - SUB + 1):
                        dve.wait_ge(flipped, n - SUB + 1)
                    r = rows[:, b, :, :]
                    nc.vector.tensor_tensor(t1[:, 0:2, :], r[:, 0:4:2, :], r[:, 1:4:2, :], ALU.min)
                    nc.vector.tensor_tensor(t1[:, 2:4, :], r[:, 0:4:2, :], r[:, 1:4:2, :], ALU.max).then_inc(step, 1)
                    after(1)
                    if holds_back(n):
                        dve.wait_ge(sorted_, n)
                    nc.vector.tensor_tensor(t2[:, 0:2, :], t1[:, 0:4:2, :], t1[:, 1:4:2, :], ALU.min)
                    nc.vector.tensor_tensor(t2[:, 2:4, :], t1[:, 0:4:2, :], t1[:, 1:4:2, :], ALU.max).then_inc(step, 1)
                    after(2)
                    nc.vector.tensor_tensor(t3[:, 0, :], t2[:, 1, :], t2[:, 2, :], ALU.min)
                    nc.vector.tensor_tensor(t3[:, 1, :], t2[:, 1, :], t2[:, 2, :], ALU.max)
                    nc.vector.tensor_scalar(acc[:, 0, :], t2[:, 0, :], w["cw"][:, 0:1], w["cb"], ALU.mult, ALU.add).then_inc(step, 1)
                    after(3)
                    nc.vector.scalar_tensor_tensor(acc[:, 1, :], t3[:, 0, :], w["cw"][:, 1:2], acc[:, 0, :],
                                                   ALU.mult, ALU.add).then_inc(step, 1)
                    after(4)
                    nc.vector.scalar_tensor_tensor(acc[:, 2, :], t3[:, 1, :], w["cw"][:, 2:3], acc[:, 1, :],
                                                   ALU.mult, ALU.add).then_inc(step, 1)
                    after(5)
                    nc.vector.scalar_tensor_tensor(out[:, b, :], t2[:, 3, :], w["cw"][:, 3:4], acc[:, 2, :],
                                                   ALU.mult, ALU.add).then_inc(sorted_, 1)
                    if not (isinstance(i, int) and i == 0 and b == 0):
                        finish(n - 1, (b - 1) % SUB)
            looped(dve, BLOCKS // SUB, body)
            finish(BLOCKS - 1, SUB - 1)
    gathers.end_phase(SUB, SLOTS * (BLOCKS // SUB))


def sage_phase(nc, name, aggs, inv_count, zs, wl, wr, biases, outs):
    M, K = len(outs), len(aggs)
    with Scope(nc, name) as s:
        acc = s.ps("acc", [P, 2, M, 512])
        mean = s.sb("mean", [P, 2, K, CHUNK])
        both = s.sb("both", [P, 2, CHUNK])
        averaged, summed, evacuated, joined = s.sem("averaged"), s.sem("summed"), s.sem("evacuated"), s.sem("joined")
        block = s.block()

        @block.vector
        def _(dve):
            def body(i):
                for c in range(2):
                    n = 2 * i + c
                    if holds_back(n - 1):
                        dve.wait_ge(summed if wl is not None else joined, n - 1)
                    for k in range(K):
                        ins = nc.vector.tensor_tensor(mean[:, c, k, :], cols(aggs[k], n * CHUNK, CHUNK),
                                                      cols(inv_count, n * CHUNK, CHUNK), ALU.mult)
                    ins.then_inc(averaged, 1)
                    if wl is None:
                        if holds_back(n - 1):
                            dve.wait_ge(evacuated, n - 1)
                        dve.wait_ge(averaged, n + 1)
                        dve.wait_ge(summed, n + 1)
                        nc.vector.tensor_tensor(both[:, c, :], mean[:, c, 0, :], acc[:, c, 0, 0:CHUNK],
                                                ALU.add).then_inc(joined, 1)
            looped(dve, CHUNKS // 2, body)

        @block.tensor
        def _(pe):
            def body(i):
                for c in range(2):
                    n = 2 * i + c
                    if holds_back(n - 1):
                        pe.wait_ge(evacuated, n - 1)
                    if wl is not None:
                        pe.wait_ge(averaged, n + 1)
                    for m in range(M):
                        terms = [(wr[k], cols(zs[k], n * CHUNK, CHUNK)) for k in range(len(zs))]
                        if wl is not None:
                            terms += [(wl[k], mean[:, c, k, :]) for k in range(K)]
                        for k, (lhsT, rhs) in enumerate(terms):
                            ins = nc.tensor.matmul(acc[:, c, m, 0:CHUNK], lhsT[:, m * P:(m + 1) * P], rhs,
                                                   start=(k == 0), stop=(k == len(terms) - 1))
                    ins.then_inc(summed, 1)
            looped(pe, CHUNKS // 2, body)

        @block.scalar
        def _(act):
            def body(i):
                for c in range(2):
                    n = 2 * i + c
                    act.wait_ge(summed if wl is not None else joined, n + 1)
                    for m in range(M):
                        src = acc[:, c, m, 0:CHUNK] if wl is not None else both[:, c, :]
                        ins = nc.scalar.activation(cols(outs[m], n * CHUNK, CHUNK), src, ACT.Identity, bias=biases[:, m:m + 1])
                    ins.then_inc(evacuated, 1)
            looped(act, CHUNKS // 2, body)


def gnn_kernel(nc, inp, out, stop=99):
    Scope.turn = 0
    gathers = Gathers(nc, 7)
    sbuf = ExitStack()
    with sbuf:
        def sb(name, shape, dt=F32):
            return sbuf.enter_context(nc.sbuf_tensor(name, shape, dt))

        def dram(name, shape):
            return nc.dram_tensor(name, shape, F32, kind="Internal").ap()

        X, A, B, C, D, E = (sb(n, [P, REGION]) for n in ("x", "ra", "rb", "rc", "rd", "re"))
        rel = sb("rel", [P, TILES + GROUP_TILES])
        bases = sb("bases", [1, GROUPS + 1], I32)
        iota, ident = sb("iota", [P, WIN]), sb("ident", [P, P])
        mean_w, eps = sb("mean_w", [P, P]), sb("eps", [P, 1])
        slot_idx = sb("slot_idx", [P, BLOCKS * SLOTS], I32)
        scale, shift = sb("scale", [P, 2]), sb("shift", [P, 2])

        load_phase(nc, "load0", [(X[:, 0:NP], inp["x_T"]), (iota[:], inp["iota"]), (ident[:], inp["ident"])])
        far = Far(nc, sb)
        prep_phase(nc, rel, bases, far, inp, ident)
        with Scope(nc, "const") as s:
            block = s.block()

            @block.vector
            def _(dve):
                nc.vector.memset(mean_w[:], 1.0 / P)
                nc.vector.memset(eps[:], EPS)
                nc.vector.memset(rel[:, TILES:], -1.0)

        def edges(name, kind, table, width, aggs, **extra):
            zero_phase(nc, name + "_zero", [r[:] for r in aggs])
            edge_pass(nc, gathers, name, kind, table, width, inp["src"], rel, iota, bases, aggs, extra)
            far_pass(nc, far, name + "_far", kind, table, width, inp["src"], rel, iota, aggs, extra)

        with ExitStack() as st:
            def w(name, shape):
                return st.enter_context(nc.sbuf_tensor(name, shape, F32))
            wl1, wsc, wa, wb = w("wl1", [P, P]), w("wsc", [P, P]), w("wa", [P, P]), w("wb", [P, P])
            fc1, fc2, attr_col = w("fc1", [BASIS, HID]), w("fc2", [HID, P]), w("attr_col", [P, BLOCKS])
            edge_attr = D[:, 0:TILES * 4]
            load_phase(nc, "load_w0", [(wl1[:], inp["t_l1"]), (wsc[:], inp["t_sc"]), (wa[:], inp["t_l2a"]),
                                       (wb[:], inp["t_l2b"]), (fc1[:], inp["t_fc1"]), (fc2[:], inp["t_fc2"]),
                                       (attr_col[:], inp["attr_col"]), (edge_attr, inp["edge_attr"]),
                                       (C[:, 0:NP], inp["attr_row"].broadcast_to([P, NP]))])
            s_in, s_mid = 1.0 / math.sqrt(MUL), 1.0 / math.sqrt(2 * MUL) / math.sqrt(16.0)
            c_s, c_x = math.sin(math.pi / 8.0), math.cos(math.pi / 8.0)
            with Scope(nc, "scale_w0") as s:
                block = s.block()

                @block.vector
                def _(dve):
                    nc.vector.tensor_scalar(wl1[:], wl1[:], s_in, None, ALU.mult)
                    nc.vector.tensor_scalar(wsc[:], wsc[:], s_in * c_s, None, ALU.mult)
                    nc.vector.tensor_scalar(wa[:], wa[:], s_mid * c_x, None, ALU.mult)
                    nc.vector.tensor_scalar(wb[:, :], wb[:, :], s_mid * c_x, None, ALU.mult)
                    nc.vector.tensor_scalar(fc2[:], fc2[:], 1.0 / math.sqrt(HID), None, ALU.mult)
            with Scope(nc, "scale_w0b") as s:
                block = s.block()

                @block.vector
                def _(dve):
                    nc.vector.tensor_scalar(wb[3 * MUL:P, :], wb[3 * MUL:P, :], 1.0 / math.sqrt(3.0), None, ALU.mult)
            t0 = dram("table_tensor", (NP, P))
            table_phase(nc, "tab0", [X], t0, P, ident, rhs=[wl1[:]], row_scale=attr_col)
            edges("pass0", "tensor", t0, P, [A, B], edge_in=inp["edge_in"], edge_attr=edge_attr, w_fc1=fc1[:], w_fc2=fc2[:])
            tensor_post_phase(nc, X, [A, B], [wsc[:], wa[:], wb[:]], C)
        layernorm_phase(nc, "ln0", X, mean_w, eps)

        if stop > 0:
            with ExitStack() as st:
                def w(name, shape):
                    return st.enter_context(nc.sbuf_tensor(name, shape, F32))
                wmsg, bmsg, ones = w("wmsg", [P, P + 1]), w("bmsg", [1, P + 1]), w("ones", [1, P])
                wdst, batt = w("wdst", [P, P]), w("batt", [P, 1])
                wih, whh, gb = w("wih", [P, 3 * P]), w("whh", [P, 3 * P]), w("gb", [P, 8])
                pick = w("pick", [SLOTS + 1, P])
                gsum = w("gsum", [P, 2])
                load_phase(nc, "load_w1", [(wmsg[:], inp["g_msg"]), (bmsg[:], inp["g_bmsg"]), (ones[:], inp["ones_row"]),
                                           (wdst[:], inp["g_dst"]), (batt[:], inp["g_batt"].broadcast_to([P, 1])),
                                           (wih[:], inp["g_ih"]), (whh[:], inp["g_hh"]), (gb[:], inp["g_vec"]),
                                           (pick[:], inp["pick"])])
                with Scope(nc, "gsum") as s:
                    block = s.block()

                    @block.vector
                    def _(dve):
                        nc.vector.tensor_tensor(gsum[:], gb[:, 0:2], gb[:, 3:5], ALU.add)
                t1 = dram("table_gate", (NP, P + 1))
                table_phase(nc, "tab1", [X], t1, P + 1, ident, rhs=[wmsg[:]], bias=(ones[:], bmsg[:]))
                linear_phase(nc, "atdst", [([wdst[:]], X)], [(C, batt[:, 0:1])])
                zero_phase(nc, "zero_c", [C[:, NP:REGION]])
                slots = D[:, 0:TILES * (SLOTS + 1)]
                slot_columns_phase(nc, inp, slots)
                zero_phase(nc, "zero_e", [E[:]])
                edges("pass1", "gate", t1, P + 1, [A], at_dst=C, slots=slots, slot_sums=E[0:SLOTS + 1, :])
                slot_tables_phase(nc, E, slot_idx[:], C, ident, pick[:])
                gru_phase(nc, X, A, B, dict(ih=wih, hh=whh, b_r=gsum[:, 0:1], b_z=gsum[:, 1:2], b_in=gb[:, 2:3],
                                            b_hn=gb[:, 5:6]))
                batchnorm_params_phase(nc, "bn1", [(B, gb[:, 6:7], gb[:, 7:8], scale[:, 0:1], shift[:, 0:1])], eps)
            add_normed_phase(nc, "res1", X, X, B, scale[:, 0:1], shift[:, 0:1])
            layernorm_phase(nc, "ln1", X, mean_w, eps)

        if stop > 1:
            for k, (src, dst) in enumerate([(X, B), (B, B)]):
                with ExitStack() as st:
                    def w(name, shape):
                        return st.enter_context(nc.sbuf_tensor(f"{name}{k}", shape, F32))
                    wT, brow, vec, sc = w("swT", [P, P]), w("sb", [1, P]), w("svec", [P, 3]), w("ssc", [P, 6])
                    load_phase(nc, f"load_w2{k}", [(wT[:], inp[f"s_w{k}"]), (brow[:], inp[f"s_b{k}"]), (vec[:], inp[f"s_vec{k}"]),
                                                   (sc[:], inp[f"s_sc{k}"].broadcast_to([P, 6]))])
                    t2 = dram(f"table_sort{k}", (NP, P))
                    table_phase(nc, f"tab2{k}", [src], t2, P, ident)
                    blank_row_phase(nc, f"blank{k}", vec[:, 2:3], wT[:], brow[:], t2)
                    sort_phase(nc, gathers, f"sort{k}", src, A, t2, slot_idx, dict(cw=sc[:, 0:4], cb=sc[:, 4:5], a=sc[:, 5:6]), ident)
                    batchnorm_params_phase(nc, f"bn2{k}", [(A, vec[:, 0:1], vec[:, 1:2], scale[:, 0:1], shift[:, 0:1])], eps)
                    add_normed_phase(nc, f"res2{k}", dst, src, A, scale[:, 0:1], shift[:, 0:1])
            with Scope(nc, "res2") as s:
                block = s.block()

                @block.vector
                def _(dve):
                    nc.vector.tensor_tensor(X[:, 0:NP], X[:, 0:NP], B[:, 0:NP], ALU.add)
            layernorm_phase(nc, "ln2", X, mean_w, eps)

        if stop > 2:
            with ExitStack() as st:
                def w(name, shape):
                    return st.enter_context(nc.sbuf_tensor("sage_" + name, shape, F32))
                H = 2 * P
                vec = w("avec", [P, 3 + 3 * 6])
                enc, dec = w("enc", [P, P]), w("dec", [P, P])
                wl = [w(f"wl{k}", [P, 1 if k == 0 else 2, P if k == 3 else H]) for k in range(4)]
                wr = [w(f"wr{k}", [P, 1 if k == 0 else 2, P if k == 3 else H]) for k in range(4)]
                flat = "p k m -> p (k m)"
                load_phase(nc, "load_w3", [(vec[:], inp["a_vec"]), (enc[:], inp["a_enc"]), (dec[:], inp["a_dec"])]
                           + [(wl[k][:].rearrange(flat), inp[f"a_wl{k}"]) for k in range(4)]
                           + [(wr[k][:].rearrange(flat), inp[f"a_wr{k}"]) for k in range(4)])
                linear_phase(nc, "enc", [([enc[:]], X)], [(D, vec[:, 0:1])])
                zs, params = [D], None
                for k in range(3):
                    K = len(zs)
                    tab = dram(f"table_sage{k}", (NP, K * P))
                    table_phase(nc, f"tab3{k}", zs, tab, K * P, ident, func=ACT.Relu, params=params,
                                copy_back=params is not None)
                    aggs = [A, B][:K]
                    edges(f"pass3{k}", "sum", tab, K * P, aggs)
                    bl = inp_cols(vec, k, 0)
                    sage_phase(nc, f"sage{k}", aggs, C, zs, [wl[k][:, j, :] for j in range(K)],
                               [wr[k][:, j, :] for j in range(K)], bl, [D, E])
                    zs = [D, E]
                    g, b = inp_cols(vec, k, 1), inp_cols(vec, k, 2)
                    batchnorm_params_phase(nc, f"bn3{k}", [(zs[m], g[:, m:m + 1], b[:, m:m + 1], scale[:, m:m + 1],
                                                            shift[:, m:m + 1]) for m in range(2)], eps)
                    params = [(scale[:, m:m + 1], shift[:, m:m + 1]) for m in range(2)]
                tab = dram("table_sage3", (NP, P))
                table_phase(nc, "tab33", zs, tab, P, ident, func=ACT.Relu, params=params, copy_back=True,
                            rhs=[wl[3][:, j, :] for j in range(2)])
                edges("pass33", "sum", tab, P, [A])
                sage_phase(nc, "sage3", [A], C, zs, None, [wr[3][:, j, :] for j in range(2)], vec[:, 2:3], [B])
                linear_phase(nc, "dec", [([dec[:]], B)], [(A, vec[:, 1:2])])
                with Scope(nc, "res3") as s:
                    block = s.block()

                    @block.vector
                    def _(dve):
                        nc.vector.tensor_tensor(X[:, 0:NP], X[:, 0:NP], A[:, 0:NP], ALU.add)
            layernorm_phase(nc, "ln3", X, mean_w, eps)
        table_phase(nc, "out", [X], out, P, ident)


def inp_cols(vec, layer, what):
    at = 3 + layer * 6 + 2 * what
    return vec[:, at:at + 2]


def host_layout(inputs):
    import numpy as np
    g = {k: np.asarray(v) for k, v in inputs.items()}
    E_PAD = TILES * P
    f32 = np.float32

    def edges(a, fill=0):
        v = np.full(E_PAD, fill, a.dtype)
        v[:N_EDGES] = a
        return v.reshape(TILES, P).T

    def stack(W):
        return W.reshape(-1, P, W.shape[1]).transpose(1, 0, 2).reshape(P, -1)

    def comp(d):
        return slice(MUL + d, P, 3)

    src, dst = g["src"], g["dst"]
    nowhere = -1
    o = {}
    x_T = np.zeros((P, NP), f32)
    x_T[:, :N_NODES] = g["x"].T
    o["x_T"] = x_T
    o["src"], o["dst"] = edges(src), edges(dst, nowhere)
    before = []
    for j in range(1, SLOTS + 1):
        b = np.full(N_EDGES, -1, dst.dtype)
        b[j:] = dst[:-j]
        before.append(edges(b, -1))
    o["dst_before"] = np.concatenate(before, 1)
    bases = np.zeros((1, GROUPS + 1), dst.dtype)
    firsts = dst[::GROUP_TILES * P]
    bases[0, 1:1 + len(firsts)] = firsts
    o["bases"] = bases
    after_all = 1 << 20
    base_col = np.full((2, BASE_COLS * P), after_all, dst.dtype)
    base_col[0, :len(firsts)], base_col[1, 1:len(firsts)] = firsts, firsts[:-1]
    base_col[1, 0] = -1
    o["base_cols"] = base_col.reshape(2, BASE_COLS, P).transpose(2, 0, 1).reshape(P, 2 * BASE_COLS)
    ea = np.zeros((E_PAD, 4), f32)
    ea[:N_EDGES] = g["edge_attr_4"]
    o["edge_attr"] = ea.reshape(TILES, P, 4).transpose(1, 0, 2).reshape(P, TILES * 4)
    ein = np.zeros((BASIS, (GROUPS + LOOK) * GROUP_TILES * P), f32)
    ein[:, :N_EDGES] = g["edge_attr_10"].T
    o["edge_in"] = ein
    attr = np.zeros((NP,), f32)
    attr[:N_NODES] = g["node_vec1"][:, 0]
    o["attr_row"], o["attr_col"] = attr[None, :], attr.reshape(BLOCKS, P).T

    l1, sc, l2a, l2b = (np.zeros((P, P), f32) for _ in range(4))
    l1[:MUL, :MUL], sc[:MUL, :MUL] = g["L0_gnn_W_l10"], g["L0_gnn_W_sc0"]
    l2a[:MUL, :MUL] = g["L0_gnn_W_l20"][:MUL]
    l2b[3 * MUL:, :MUL] = g["L0_gnn_W_l20"][MUL:]
    for d in range(3):
        l1[comp(d), MUL * (d + 1):MUL * (d + 2)] = g["L0_gnn_W_l11"]
        sc[comp(d), comp(d)] = g["L0_gnn_W_sc1"]
        l2a[MUL * (d + 1):MUL * (d + 2), comp(d)] = g["L0_gnn_W_l21"][MUL:]
        l2b[MUL * d:MUL * (d + 1), comp(d)] = g["L0_gnn_W_l21"][:MUL]
    o["t_l1"], o["t_sc"], o["t_l2a"], o["t_l2b"] = l1, sc, l2a, l2b
    o["t_fc1"], o["t_fc2"] = g["L0_gnn_W_fc1"], g["L0_gnn_W_fc2"]

    p = "L1_gnn_"
    att = g[p + "W_att"]
    o["g_msg"] = np.concatenate([g[p + "W_msg"], att[:P]], 1)
    o["g_bmsg"] = np.concatenate([g[p + "b_msg"], np.zeros(1, f32)])[None, :]
    o["g_dst"] = np.repeat(att[P:], P, 1)
    o["g_batt"] = g[p + "b_att"].reshape(1, 1)
    o["g_ih"], o["g_hh"] = g[p + "W_ih"].T, g[p + "W_hh"].T
    o["g_vec"] = np.stack([*g[p + "b_ih"].reshape(3, P), *g[p + "b_hh"].reshape(3, P), g[p + "gamma"], g[p + "beta"]], 1)
    p = "L2_gnn_"
    for k in range(2):
        o[f"s_w{k}"], o[f"s_b{k}"] = g[p + f"W{k}"].T, g[p + f"b{k}"][None, :]
        o[f"s_vec{k}"] = np.stack([g[p + f"g{k}"], g[p + f"be{k}"], g[p + f"blank{k}"]], 1)
        o[f"s_sc{k}"] = np.concatenate([g[p + f"cw{k}"], g[p + f"cb{k}"], g[p + f"a{k}"]])[None, :]
    p = "L3_gnn_"
    o["a_enc"], o["a_dec"] = g[p + "enc_W"].T, g[p + "dec_W"].T
    for k in range(4):
        o[f"a_wl{k}"], o[f"a_wr{k}"] = stack(g[p + f"Wl{k}"].T), stack(g[p + f"Wr{k}"].T)
    v = [g[p + "enc_b"], g[p + "dec_b"], g[p + "bl3"]]
    for k in range(3):
        for n in (f"bl{k}", f"g{k}", f"b{k}"):
            v += [*g[p + n].reshape(2, P)]
    o["a_vec"] = np.stack(v, 1)

    o["win_start"] = np.tile(np.arange(WINDOWS, dtype=f32) * WIN, (P, 1))
    o["iota"] = np.tile(np.arange(WIN, dtype=f32), (P, 1))
    o["ident"] = np.eye(P, dtype=f32)
    o["ones_row"] = np.ones((1, P), f32)
    pick = np.zeros((SLOTS + 1, P), f32)
    pick[SLOTS] = 1.0
    o["pick"] = pick
    return {k: np.ascontiguousarray(a) for k, a in o.items()}


STOP = 99


def kernel(**inputs):
    import numpy as _np
    import concourse.bacc as _bacc
    from concourse import mybir as _mybir
    from concourse.bass_utils import run_bass_kernel_spmd as _run

    nc = _bacc.Bacc("TRN2", target_bir_lowering=False, num_devices=1)
    arrays, aps = {}, {}
    for name, a in host_layout(inputs).items():
        arrays[f"in_{name}"] = a
        aps[name] = nc.dram_tensor(f"in_{name}", a.shape, _mybir.dt.from_np(a.dtype), kind="ExternalInput").ap()
    out = nc.dram_tensor("out_0", (NP, P), _mybir.dt.float32, kind="ExternalOutput").ap()
    gnn_kernel(nc, aps, out, STOP)
    r = _run(nc, [arrays], core_ids=[0])
    return _np.asarray(r.results[0]["out_0"])[:N_NODES]
```

```python
import math
from contextlib import ExitStack

import concourse.bass as bass
from concourse import mybir

F32 = mybir.dt.float32
I32 = mybir.dt.int32
ALU = mybir.AluOpType
ACT = mybir.ActivationFunctionType
DVE_E = mybir.EngineType.DVE
PE_E = mybir.EngineType.PE

P = 128
N_NODES = 6250
N_EDGES = 100000
BLOCKS = -(-N_NODES // P)
NP = BLOCKS * P
GROUP_TILES = 4
RING = 4
GROUPS = 196
TILES = GROUPS * GROUP_TILES
ITERS = GROUPS // RING
WIN = 128
REGION = 6400
CHUNK = 448
CHUNKS = NP // CHUNK
MUL = 32
HID = 100
BASIS = 10
SLOTS = 4
EPS = 1e-5
WINDOWS = NP // WIN
BASE_COLS = -(-GROUPS // P)
LOOK = 2
assert ITERS == BLOCKS and TILES * P >= N_EDGES and REGION >= N_NODES + WIN and CHUNK * CHUNKS == NP


def holds_back(value):
    return not isinstance(value, int) or value > 0


def looped(eng, count, body):
    body(0)
    if count > 1:
        with eng.Fori(1, count) as i:
            body(i)


def looped_but_last(eng, count, body):
    looped(eng, count - 1, body)
    body(count - 1)


def chunk_stats(nc, stats, region, chunk):
    width = min(CHUNK, N_NODES - chunk * CHUNK) if isinstance(chunk, int) else CHUNK
    return nc.vector.bn_stats(cols(stats, chunk * 6, 6), cols(region, chunk * CHUNK, width))


class Scope:
    BANKS = (100, 170)
    turn = 0

    def __init__(self, nc, name):
        self.nc, self.name, self.stack, self.sems = nc, name, ExitStack(), []
        self.first = Scope.BANKS[Scope.turn]
        Scope.turn = 1 - Scope.turn

    def __enter__(self):
        return self

    def __exit__(self, *a):
        self.stack.__exit__(*a)
        if self.sems:
            self.nc.gpsimd.sem_clear(range(self.first, self.first + len(self.sems)))
            for sem in self.sems:
                self.nc.release_semaphore(sem)

    def sb(self, name, shape, dt=F32):
        return self.stack.enter_context(self.nc.sbuf_tensor(f"{self.name}_{name}", shape, dt))

    def ps(self, name, shape):
        return self.stack.enter_context(self.nc.psum_tensor(f"{self.name}_{name}_ps", shape, F32))

    def sem(self, name):
        self.sems.append(self.nc.alloc_semaphore(f"{self.name}_{name}", self.first + len(self.sems)))
        return self.sems[-1]

    def block(self):
        return self.stack.enter_context(self.nc.Block())


class Gathers:

    def __init__(self, nc, slots):
        self.sems = [nc.alloc_semaphore(f"gathered{k}", 240 + k) for k in range(slots)]
        self.base = [0] * slots

    def count(self, k, tiles):
        return 16 * tiles + self.base[k]

    def end_phase(self, slots, tiles):
        for k in range(slots):
            self.base[k] += 16 * tiles


def cols(region, start, width):
    return region[:, bass.ds(start, width)]


class Loads:
    count = 0

    def __init__(self, nc, name, pairs):
        self.nc, self.name, self.pairs = nc, name, pairs
        self.loaded = nc.alloc_semaphore(f"{name}_loaded", (247, 248, 249, 251, 252, 253, 254)[Loads.count])
        Loads.count += 1

    def start(self):
        with Scope(self.nc, self.name + "_start") as s:
            block = s.block()

            @block.sync
            def _(sp):
                for dst, src in self.pairs:
                    sp.dma_start(dst, src).then_inc(self.loaded, 16)

    def await_all(self):
        with Scope(self.nc, self.name + "_await") as s:
            block = s.block()

            @block.sync
            def _(sp):
                sp.wait_ge(self.loaded, 16 * len(self.pairs))


def table_phase(nc, name, sources, table, width, ident, func=None, params=None, rhs=None, row_scale=None,
                clear=()):
    K = len(sources)
    SUB = 7
    with Scope(nc, name) as s:
        stage = s.sb("stage", [P, SUB, K, P])
        rows = s.sb("rows", [P, SUB, width])
        turned = s.ps("turned", [P, SUB, 512])
        staged, flipped, evacuated = s.sem("staged"), s.sem("flipped"), s.sem("evacuated")
        stored = [s.sem(f"stored{b}") for b in range(SUB)]
        block = s.block()

        @block.gpsimd
        def _(pool):
            for region in clear:
                nc.gpsimd.memset(region, 0.0)

        @block.scalar
        def _(act):
            def body(i):
                for b in range(SUB):
                    n = i * SUB + b
                    if holds_back(n - SUB + 1):
                        act.wait_ge(flipped, n - SUB + 1)
                    for k in range(K):
                        src = cols(sources[k], n * P, P)
                        if params is None:
                            ins = nc.scalar.activation(stage[:, b, k, :], src, ACT.Identity)
                        else:
                            scale, shift = params[k]
                            ins = nc.scalar.activation(stage[:, b, k, :], src, func, bias=shift, scale=scale)
                    ins.then_inc(staged, 1)
            looped(act, BLOCKS // SUB, body)

        @block.tensor
        def _(pe):
            def body(i):
                for b in range(SUB):
                    n = i * SUB + b
                    if holds_back(n - SUB + 1):
                        pe.wait_ge(evacuated, n - SUB + 1)
                    pe.wait_ge(staged, n + 1)
                    if rhs is None:
                        for k in range(K):
                            ins = nc.tensor.transpose(turned[:, b, k * P:(k + 1) * P], stage[:, b, k, :], ident[:])
                    else:
                        for k in range(K):
                            ins = nc.tensor.matmul(turned[:, b, 0:width], stage[:, b, k, :], rhs[k],
                                                   start=(k == 0), stop=(k == K - 1))
                    ins.then_inc(flipped, 1)
            looped(pe, BLOCKS // SUB, body)

        @block.vector
        def _(dve):
            def body(i):
                for b in range(SUB):
                    n = i * SUB + b
                    if holds_back(16 * i):
                        dve.wait_ge(stored[b], 16 * i)
                    dve.wait_ge(flipped, n + 1)
                    if row_scale is None:
                        ins = nc.vector.tensor_copy(rows[:, b, :], turned[:, b, 0:width])
                    else:
                        ins = nc.vector.tensor_scalar(rows[:, b, :], turned[:, b, 0:width],
                                                      cols(row_scale, n, 1), None, ALU.mult)
                    ins.then_inc(evacuated, 1)
            looped(dve, BLOCKS // SUB, body)

        @block.sync
        def _(sp):
            def body(i):
                for b in range(SUB):
                    n = i * SUB + b
                    sp.wait_ge(evacuated, n + 1)
                    sp.dma_start(table[bass.ds(n * P, P), :], rows[:, b, :]).then_inc(stored[b], 16)
            looped(sp, BLOCKS // SUB, body)
            for b in range(SUB):
                sp.wait_ge(stored[b], 16 * (BLOCKS // SUB))


def linear_phase(nc, name, terms, outs):
    M = len(outs)
    with Scope(nc, name) as s:
        acc = s.ps("acc", [P, 2, M, 512])
        summed, evacuated = s.sem("summed"), s.sem("evacuated")
        block = s.block()

        @block.tensor
        def _(pe):
            def body(i):
                for c in range(2):
                    n = i * 2 + c
                    if holds_back(n - 1):
                        pe.wait_ge(evacuated, n - 1)
                    for m in range(M):
                        for k, (lhsT, region) in enumerate(terms):
                            ins = nc.tensor.matmul(acc[:, c, m, 0:CHUNK], lhsT[m], cols(region, n * CHUNK, CHUNK),
                                                   start=(k == 0), stop=(k == len(terms) - 1))
                    ins.then_inc(summed, 1)
            looped(pe, CHUNKS // 2, body)

        @block.scalar
        def _(act):
            def body(i):
                for c in range(2):
                    n = i * 2 + c
                    act.wait_ge(summed, n + 1)
                    for m, (region, bias) in enumerate(outs):
                        ins = nc.scalar.activation(cols(region, n * CHUNK, CHUNK), acc[:, c, m, 0:CHUNK],
                                                   ACT.Identity, bias=bias)
                    ins.then_inc(evacuated, 1)
            looped(act, CHUNKS // 2, body)


def layernorm_phase(nc, name, X, mean_w, eps):
    with Scope(nc, name) as s:
        mean_ps, var_ps = s.ps("mean", [P, 2, 512]), s.ps("var", [P, 2, 512])
        xc, sq = s.sb("xc", [P, 2, CHUNK]), s.sb("sq", [P, 2, CHUNK])
        sd, rs = s.sb("sd", [P, 2, CHUNK]), s.sb("rs", [P, 2, CHUNK])
        meaned, centred, squared = s.sem("meaned"), s.sem("centred"), s.sem("squared")
        vared, rooted, inverted, done = s.sem("vared"), s.sem("rooted"), s.sem("inverted"), s.sem("done")
        block = s.block()

        @block.tensor
        def _(pe):
            def body(i):
                for c in range(2):
                    n = 2 * i + c
                    if holds_back(n - 1):
                        pe.wait_ge(centred, n - 1)
                    nc.tensor.matmul(mean_ps[:, c, 0:CHUNK], mean_w[:], cols(X, n * CHUNK, CHUNK),
                                     start=True, stop=True).then_inc(meaned, 1)
                for c in range(2):
                    n = 2 * i + c
                    if holds_back(n - 1):
                        pe.wait_ge(rooted, n - 1)
                    pe.wait_ge(squared, n + 1)
                    nc.tensor.matmul(var_ps[:, c, 0:CHUNK], mean_w[:], sq[:, c, :],
                                     start=True, stop=True).then_inc(vared, 1)
            looped(pe, CHUNKS // 2, body)

        @block.scalar
        def _(act):
            def body(i):
                for c in range(2):
                    n = 2 * i + c
                    if holds_back(n - 1):
                        act.wait_ge(vared, n - 1)
                    act.wait_ge(centred, n + 1)
                    nc.scalar.activation(sq[:, c, :], xc[:, c, :], ACT.Square).then_inc(squared, 1)
                for c in range(2):
                    n = 2 * i + c
                    if holds_back(n - 1):
                        act.wait_ge(inverted, n - 1)
                    act.wait_ge(vared, n + 1)
                    nc.scalar.activation(sd[:, c, :], var_ps[:, c, 0:CHUNK], ACT.Sqrt,
                                         bias=eps[:, 0:1]).then_inc(rooted, 1)
            looped(act, CHUNKS // 2, body)

        @block.vector
        def _(dve):
            def body(i):
                for c in range(2):
                    n = 2 * i + c
                    if holds_back(n - 1):
                        dve.wait_ge(done, n - 1)
                    dve.wait_ge(meaned, n + 1)
                    nc.vector.tensor_tensor(xc[:, c, :], cols(X, n * CHUNK, CHUNK), mean_ps[:, c, 0:CHUNK],
                                            ALU.subtract).then_inc(centred, 1)
                for c in range(2):
                    n = 2 * i + c
                    dve.wait_ge(rooted, n + 1)
                    nc.vector.reciprocal(rs[:, c, :], sd[:, c, :]).then_inc(inverted, 1)
                for c in range(2):
                    n = 2 * i + c
                    dve.wait_ge(inverted, n + 1)
                    nc.vector.tensor_tensor(cols(X, n * CHUNK, CHUNK), xc[:, c, :], rs[:, c, :],
                                            ALU.mult).then_inc(done, 1)
            looped(dve, CHUNKS // 2, body)


def looped_pairs(eng, count, body):
    for i in range(3):
        body(i, i % 2)
    with eng.Fori(1, (count - 1) // 2) as j:
        body(j * 2 + 1, 1)
        body(j * 2 + 2, 0)


def norm_table_phase(nc, name, X, table, ident, eps, plus=None, normed_by=None, rhs=None, bias=None, keep=True,
                     clear=()):
    SUB = 7
    W = SUB * P
    count = BLOCKS // SUB
    with Scope(nc, name) as s:
        stage = s.sb("stage", [P, 2, W])
        stats, mv = s.sb("stats", [P, 2, SUB, 6]), s.sb("mv", [P, 2, SUB, 2])
        sd, rs, nm = s.sb("sd", [P, 2, SUB]), s.sb("rs", [P, 2, SUB]), s.sb("nm", [P, 2, SUB])
        rows = s.sb("rows", [P, 2, SUB, P])
        turned, back = s.ps("turned", [P, 2, 1024]), s.ps("back", [P, 1024])
        staged, flipped, counted, aggregated = s.sem("staged"), s.sem("flipped"), s.sem("counted"), s.sem("aggregated")
        rooted, inverted, factored = s.sem("rooted"), s.sem("inverted"), s.sem("factored")
        normed, flipped_back, restored = s.sem("normed"), s.sem("flipped_back"), s.sem("restored")
        tick = s.sem("tick")
        stored = [s.sem(f"stored{b}") for b in range(2)]
        if normed_by is not None:
            addend, addend_made = s.sb("addend", [P, 2, W]), s.sem("addend_made")
        if rhs is not None:
            width = rhs.shape[-1]
            again = s.sb("again", [P, 2, W])
            product = s.ps("product", [P, 1024])
            rows_out = s.sb("rows_out", [P, 2, SUB, width])
            copied, multiplied, evacuated = s.sem("copied"), s.sem("multiplied"), s.sem("evacuated")
        else:
            rows_out = rows
        block = s.block()

        @block.gpsimd
        def _(pool):
            def add(i, c):
                if holds_back(i - 1):
                    pool.wait_ge(flipped, i - 1)
                if normed_by is not None:
                    pool.wait_ge(addend_made, i + 1)
                if plus is None:
                    ins = nc.gpsimd.tensor_copy(stage[:, c, :], cols(X, i * W, W))
                else:
                    other = cols(plus, i * W, W) if normed_by is None else addend[:, c, :]
                    ins = nc.gpsimd.tensor_tensor(stage[:, c, :], cols(X, i * W, W), other, ALU.add)
                ins.then_inc(staged, 1)

            add(0, 0)
            add(1, 1)
            for region in clear:
                nc.gpsimd.memset(region, 0.0)

            def body(i, c):
                if rhs is not None:
                    pool.wait_ge(restored, i + 1)
                    nc.gpsimd.tensor_copy(cols(X, i * W, W), again[:, c, :]).then_inc(copied, 1)
                if isinstance(i, int) and i + 2 >= count:
                    return
                add(i + 2, c)
            for i in range(count):
                body(i, i % 2)

        @block.scalar
        def _(act):
            def scaled_addend(i, c):
                if holds_back(i - 1):
                    act.wait_ge(staged, i - 1)
                nc.scalar.activation(addend[:, c, :], cols(plus, i * W, W), ACT.Identity, bias=normed_by[1],
                                     scale=normed_by[0]).then_inc(addend_made, 1)

            def body(i, c):
                if normed_by is not None:
                    scaled_addend(i, c)
                act.wait_ge(aggregated, i + 1)
                nc.scalar.activation(sd[:, c, :], mv[:, c, :, 1], ACT.Sqrt, bias=eps[:, 0:1]).then_inc(rooted, 1)
                if holds_back(i - 1):
                    if keep:
                        act.wait_ge(flipped_back, i - 1)
                    if rhs is None:
                        act.wait_ge(stored[c], (i - c) * 8)
                act.wait_ge(factored, i + 1)
                for b in range(SUB):
                    ins = nc.scalar.activation(rows[:, c, b, :], turned[:, c, b * P:(b + 1) * P], ACT.Identity,
                                               bias=nm[:, c, b:b + 1], scale=rs[:, c, b:b + 1])
                ins.then_inc(normed, 1)
            looped_pairs(act, count, body)

        @block.tensor
        def _(pe):
            def turn(i, c):
                if holds_back(i - 1):
                    pe.wait_ge(normed, i - 1)
                pe.wait_ge(staged, i + 1)
                for b in range(SUB):
                    ins = nc.tensor.transpose(turned[:, c, b * P:(b + 1) * P], stage[:, c, b * P:(b + 1) * P], ident[:])
                ins.then_inc(flipped, 1)

            def body(i, c):
                if not (isinstance(i, int) and i + 1 >= count):
                    turn(i + 1, 1 - c)
                if not keep:
                    return
                if holds_back(i):
                    pe.wait_ge(restored, i)
                pe.wait_ge(normed, i + 1)
                for b in range(SUB):
                    ins = nc.tensor.transpose(back[:, b * P:(b + 1) * P], rows[:, c, b, :], ident[:])
                ins.then_inc(flipped_back, 1)
                if rhs is not None:
                    if holds_back(i):
                        pe.wait_ge(evacuated, i)
                    pe.wait_ge(restored, i + 1)
                    for b in range(SUB):
                        nodes = again[:, c, b * P:(b + 1) * P]
                        ins = nc.tensor.matmul(product[:, b * P:(b + 1) * P], nodes, rhs[:, 0:P], start=True, stop=True)
                        if width > P:
                            ins = nc.tensor.matmul(product[:, W + b:W + b + 1], nodes, rhs[:, P:P + 1],
                                                   start=True, stop=True)
                    ins.then_inc(multiplied, 1)
            turn(0, 0)
            for i in range(count):
                body(i, i % 2)

        @block.vector
        def _(dve):
            def finish(i, c):
                if not keep:
                    return
                dve.wait_ge(flipped_back, i + 1)
                if rhs is None:
                    nc.vector.tensor_copy(cols(X, i * W, W), back[:, 0:W]).then_inc(restored, 1)
                    return
                if holds_back(i - 1):
                    dve.wait_ge(copied, i - 1)
                    dve.wait_ge(multiplied, i - 1)
                nc.vector.tensor_copy(again[:, c, :], back[:, 0:W]).then_inc(restored, 1)
                dve.wait_ge(multiplied, i + 1)
                if holds_back(i - 1):
                    dve.wait_ge(stored[c], (i - c) * 8)
                ins = nc.vector.tensor_tensor(rows_out[:, c, :, 0:P], product[:, 0:W].rearrange("p (b f) -> p b f", f=P),
                                              bias[:, 0:P].unsqueeze(1).broadcast_to([P, SUB, P]), ALU.add)
                if width > P:
                    ins = nc.vector.tensor_tensor(rows_out[:, c, :, P], product[:, W:W + SUB],
                                                  bias[:, P:P + 1].broadcast_to([P, SUB]), ALU.add)
                ins.then_inc(evacuated, 1)

            def body(i, c):
                dve.wait_ge(flipped, i + 1)
                for b in range(SUB):
                    ins = nc.vector.bn_stats(stats[:, c, b, :], turned[:, c, b * P:(b + 1) * P])
                ins.then_inc(counted, 1)
                dve.wait_ge(counted, i + 1)
                dve.sem_inc(tick, 1)
                for b in range(SUB):
                    ins = nc.vector.bn_aggr(mv[:, c, b, :], stats[:, c, b, :])
                ins.then_inc(aggregated, 1)
                dve.wait_ge(rooted, i + 1)
                if holds_back(i - 1):
                    dve.wait_ge(normed, i - 1)
                nc.vector.reciprocal(rs[:, c, :], sd[:, c, :]).then_inc(inverted, 1)
                dve.wait_ge(inverted, i + 1)
                nc.vector.scalar_tensor_tensor(nm[:, c, :], mv[:, c, :, 0], -1.0, rs[:, c, :],
                                               ALU.mult, ALU.mult).then_inc(factored, 1)
                if holds_back(i):
                    finish(i - 1, 1 - c)
            looped_pairs(dve, count, body)
            finish(count - 1, (count - 1) % 2)

        @block.sync
        def _(sp):
            def body(i, c):
                sp.wait_ge(normed if rhs is None else evacuated, i + 1)
                sp.dma_start(table[bass.ds(i * W, W), :].rearrange("(b p) f -> p b f", p=P), rows_out[:, c, :, :])\
                    .then_inc(stored[c], 16)
            looped_pairs(sp, count, body)
            for c in range(2):
                sp.wait_ge(stored[c], 16 * ((count + 1 - c) // 2))


def batchnorm_params_phase(nc, name, items, stats, eps):
    with Scope(nc, name) as s:
        K = len(items)
        mv, sd, rs, ms = s.sb("mv", [P, K, 2]), s.sb("sd", [P, K]), s.sb("rs", [P, K]), s.sb("ms", [P, K])
        aggregated, rooted, step = s.sem("aggregated"), s.sem("rooted"), s.sem("step")
        block = s.block()

        @block.vector
        def _(dve):
            for k in range(K):
                nc.vector.bn_aggr(mv[:, k, :], stats[k]).then_inc(aggregated, 1)
            for k, (gamma, beta, scale, shift) in enumerate(items):
                dve.wait_ge(rooted, k + 1)
                nc.vector.reciprocal(rs[:, k:k + 1], sd[:, k:k + 1]).then_inc(step, 1)
                dve.wait_ge(step, 3 * k + 1)
                nc.vector.tensor_tensor(scale, rs[:, k:k + 1], gamma, ALU.mult).then_inc(step, 1)
                dve.wait_ge(step, 3 * k + 2)
                nc.vector.tensor_tensor(ms[:, k:k + 1], mv[:, k, 0:1], scale, ALU.mult).then_inc(step, 1)
                dve.wait_ge(step, 3 * k + 3)
                nc.vector.tensor_tensor(shift, beta, ms[:, k:k + 1], ALU.subtract)

        @block.scalar
        def _(act):
            for k in range(K):
                act.wait_ge(aggregated, k + 1)
                nc.scalar.activation(sd[:, k:k + 1], mv[:, k, 1:2], ACT.Sqrt, bias=eps[:, 0:1]).then_inc(rooted, 1)


def add_normed_phase(nc, name, out, base, H, scale, shift):
    cuts = [0, NP // 2, NP]
    with Scope(nc, name) as s:
        normed, done = s.sem("normed"), s.sem("done")
        block = s.block()

        @block.scalar
        def _(act):
            for a, b in zip(cuts, cuts[1:]):
                nc.scalar.activation(H[:, a:b], H[:, a:b], ACT.Identity, bias=shift, scale=scale).then_inc(normed, 1)

        @block.vector
        def _(dve):
            for j, (a, b) in enumerate(zip(cuts, cuts[1:])):
                dve.wait_ge(normed, j + 1)
                nc.vector.tensor_tensor(out[:, a:b], base[:, a:b], H[:, a:b], ALU.add).then_inc(done, 1)


def zero_phase(nc, name, regions):
    with Scope(nc, name) as s:
        block = s.block()

        @block.vector
        def _(dve):
            for r in regions:
                nc.vector.memset(r, 0.0)


class TensorMath:

    def __init__(self, nc, T, w, y, y_ea0, ea, y_ea1, w2_y0, dot, prod_a, prod_b):
        by_channel = "p t (c u) -> p t c u"
        self.nc, self.by3, self.w2_y0, self.dot, self.y_ea1 = nc, [P, T, 3, MUL], w2_y0, dot, y_ea1
        self.w = w.rearrange("p (t c u) -> p t c u", c=4, u=MUL)
        self.y, self.y_ea0 = y.rearrange(by_channel, u=MUL), y_ea0.rearrange(by_channel, u=MUL)
        self.a, self.b = prod_a.rearrange(by_channel, u=MUL), prod_b.rearrange(by_channel, u=MUL)
        self.ea1 = ea.rearrange("p (t x) -> p t x", x=4)[:, :, 1:4].unsqueeze(3).broadcast_to(self.by3)

    def mult(self, out, a, b):
        return self.nc.vector.tensor_tensor(out, a, b, ALU.mult)

    def y1_times_ea1(self):
        return self.mult(self.y_ea1, self.y[:, :, 1:4, :], self.ea1)

    def y0_weighed(self):
        return self.mult(self.w2_y0, self.w[:, :, 1, :], self.y[:, :, 0, :])

    def dot_first(self):
        return self.nc.vector.tensor_tensor(self.dot[:, :, 0, :], self.y_ea1[:, :, 0, :], self.y_ea1[:, :, 1, :], ALU.add)

    def dot_second(self):
        return self.nc.vector.tensor_tensor(self.dot[:, :, 1, :], self.dot[:, :, 0, :], self.y_ea1[:, :, 2, :], ALU.add)

    def a_scalars(self):
        return self.mult(self.a[:, :, 0, :], self.w[:, :, 0, :], self.y_ea0[:, :, 0, :])

    def a_vectors(self):
        return self.mult(self.a[:, :, 1:4, :], self.w[:, :, 2:3, :].broadcast_to(self.by3), self.y_ea0[:, :, 1:4, :])

    def b_vectors(self):
        return self.mult(self.b[:, :, 0:3, :], self.w2_y0.unsqueeze(2).broadcast_to(self.by3), self.ea1)

    def b_scalars(self):
        return self.mult(self.b[:, :, 3, :], self.w[:, :, 3, :], self.dot[:, :, 1, :])


class SlotMath:

    def __init__(self, nc, T, extra, group, reaches, rank, slot_in):
        by_tile, shape = "p (t s) -> p t s", [P, T, SLOTS]
        self.nc, self.reaches, self.rank, self.slot_in = nc, reaches, rank, slot_in
        self.before = cols(extra["dst_before"], group * (T * SLOTS), T * SLOTS).rearrange(by_tile, s=SLOTS)
        self.dst = cols(extra["dst"], group * T, T).unsqueeze(2).broadcast_to(shape)
        self.src = cols(extra["src"], group * T, T).unsqueeze(2).broadcast_to(shape)

    def reach(self):
        return self.nc.vector.tensor_tensor(self.reaches[:, :, 1:SLOTS + 1], self.before, self.dst, ALU.is_equal)

    def rank_edges(self):
        return self.nc.vector.tensor_tensor(self.rank, self.reaches[:, :, 0:SLOTS], self.reaches[:, :, 1:SLOTS + 1],
                                            ALU.subtract)

    def place_sources(self):
        return self.nc.vector.tensor_tensor(self.slot_in[:, :, 0:SLOTS], self.rank, self.src, ALU.mult)


def edge_pass(nc, gathers, name, kind, table, width, src_dram, rel, iota, bases, aggs, extra):
    tensor, gate, plain = kind == "tensor", kind == "gate", kind == "sum"
    A = 1 if gate else 2 if tensor else width // P
    with Scope(nc, name) as s:
        idx = s.sb("idx", [P, RING, GROUP_TILES], I32)
        rows = s.sb("rows", [P, RING, GROUP_TILES, width])
        hot = s.sb("hot", [P, 2, GROUP_TILES, WIN])
        sums = [s.ps(f"sums{a}", [P, 2, 512]) for a in range(A)]
        idx_loaded = [s.sem(f"idx_loaded{h}") for h in range(RING)]
        gathered = gathers.sems
        tick = s.sem("tick")
        hot_made, operands_made = s.sem("hot_made"), s.sem("operands_made")
        summed, added = s.sem("summed"), s.sem("added")
        if tensor:
            edge_in = s.sb("edge_in", [BASIS, 4, GROUP_TILES * P])
            hidden = s.sb("hidden", [HID, 2, GROUP_TILES * P])
            y_ea0, y_ea1 = s.sb("y_ea0", [P, 2, GROUP_TILES, P]), s.sb("y_ea1", [P, GROUP_TILES, 3, MUL])
            w2_y0, dot = s.sb("w2_y0", [P, GROUP_TILES, MUL]), s.sb("dot", [P, GROUP_TILES, 2, MUL])
            prod_a, prod_b = s.sb("prod_a", [P, 2, GROUP_TILES, P]), s.sb("prod_b", [P, 2, GROUP_TILES, P])
            ea0_made, step, dotted = s.sem("ea0_made"), s.sem("step"), s.sem("dotted")
            hidden_ps, weight_ps = s.ps("hidden", [P, 2, 512]), s.ps("weight", [P, 2, 512])
            edge_in_loaded = [s.sem(f"edge_in_loaded{h}") for h in range(4)]
            hidden_summed, hidden_made, weight_made = s.sem("hidden_summed"), s.sem("hidden_made"), s.sem("weight_made")
        if gate:
            sig = s.sb("sig", [P, 2, GROUP_TILES, WIN])
            hot_sig = s.sb("hot_sig", [P, 2, GROUP_TILES, WIN])
            slot_in = s.sb("slot_in", [P, 2, GROUP_TILES, SLOTS + 1])
            reaches, rank = s.sb("reaches", [P, 2, GROUP_TILES, SLOTS + 1]), s.sb("rank", [P, GROUP_TILES, SLOTS])
            at_ps = s.ps("at", [P, 2, 512])
            slot_ps = s.ps("slot", [P, 2, 512])
            sig_made, at_made = s.sem("sig_made"), s.sem("at_made")
            filled, reached, ranked = s.sem("filled"), s.sem("reached"), s.sem("ranked")
        if plain:
            own = extra["own"]
            scaled_sums, scaled = s.sb("scaled_sums", [P, A, WIN]), s.sem("scaled")
            z_block = s.sb("z_block", [P, len(own["sources"]), P])
            own_ps, encoded_ps = s.ps("own", [P, 512]), s.ps("encoded", [P, 512])
            own_tick = s.sem("own_tick")
            z_encoded, z_made, own_summed, own_stored = (s.sem("z_encoded"), s.sem("z_made"), s.sem("own_summed"),
                                                         s.sem("own_stored"))
        n_acc = A + (1 if gate else 0)
        block = s.block()

        @block.sync
        def _(sp):
            if tensor:
                for q in range(LOOK):
                    sp.dma_start(edge_in[:, q, :], extra["edge_in"][:, q * 512:(q + 1) * 512])\
                        .then_inc(edge_in_loaded[q], 16)

            def body(i):
                for h in range(RING):
                    q = i * RING + h
                    if holds_back(q - RING + 1):
                        sp.wait_ge(summed, q - RING + 1)
                    sp.dma_start(idx[:, h, :], cols(src_dram, q * GROUP_TILES, GROUP_TILES)).then_inc(idx_loaded[h], 16)
                    if tensor:
                        r = (h + LOOK) % 4
                        if holds_back(q + LOOK - 4 + 1):
                            sp.wait_ge(hidden_summed, q + LOOK - 4 + 1)
                        sp.dma_start(edge_in[:, r, :], cols(extra["edge_in"], (q + LOOK) * 512, 512))\
                            .then_inc(edge_in_loaded[r], 16)
            looped(sp, ITERS, body)
            if tensor:
                for r in range(4):
                    sp.wait_ge(edge_in_loaded[r], 16 * (ITERS + (r < LOOK)))

        @block.gpsimd
        def _(pool):
            def body(i):
                for h in range(RING):
                    q = i * RING + h
                    if holds_back(q - RING + 1):
                        pool.wait_ge(summed, q - RING + 1)
                    pool.wait_ge(idx_loaded[h], 16 * i + 16)
                    pool.sem_inc(tick, 1)
                    for t in range(GROUP_TILES):
                        nc.gpsimd.indirect_dma_start(
                            rows[:, h, t, :], None, table, bass.IndirectOffsetOnAxis(ap=idx[:, h, t:t + 1], axis=0)
                        ).then_inc(gathered[h], 16)
            looped(pool, ITERS, body)

        def load_bases(engine, at, count):
            _, values = nc.values_load_multi_w_load_instructions(
                bases[0:1, bass.ds(at, count)], engines=[engine], min_val=0, max_val=N_NODES - 1,
                skip_runtime_bounds_check_because="bases are nodes: 0 to N_NODES - 1")
            return values

        @block.scalar
        def _(act):
            if tensor:
                def silu(q, r):
                    if holds_back(q - 1):
                        act.wait_ge(weight_made, q - 1)
                    act.wait_ge(hidden_summed, q + 1)
                    nc.scalar.activation(hidden[:, r, :], hidden_ps[0:HID, r, :], ACT.Silu,
                                         scale=1.0 / math.sqrt(BASIS)).then_inc(hidden_made, 1)
                silu(0, 0)

                def body(i):
                    for h in range(RING):
                        q, r = i * RING + h, h % 2
                        silu(q + 1, (h + 1) % 2)
                        if holds_back(q - 1):
                            act.wait_ge(operands_made, q - 1)
                        act.wait_ge(gathered[h], gathers.count(h, GROUP_TILES * (i + 1)))
                        for t in range(GROUP_TILES):
                            ins = nc.scalar.activation(y_ea0[:, r, t, :], rows[:, h, t, :], ACT.Copy,
                                                       scale=cols(extra["edge_attr"], (q * GROUP_TILES + t) * 4, 1))
                        ins.then_inc(ea0_made, 1)
                looped(act, ITERS, body)
            if plain:
                def body(i):
                    if holds_back(i):
                        act.wait_ge(own_summed, i)
                        act.sem_inc(own_tick, 1)
                    for k, source in enumerate(own["sources"]):
                        if own["enc"] is not None:
                            act.wait_ge(z_encoded, i + 1)
                            ins = nc.scalar.activation(z_block[:, k, :], encoded_ps[:, 0:P], ACT.Identity,
                                                       bias=own["enc"][1])
                        else:
                            scale, shift = own["params"][k]
                            ins = nc.scalar.activation(z_block[:, k, :], cols(source, i * P, P), ACT.Relu,
                                                       bias=shift, scale=scale)
                    ins.then_inc(z_made, 1)
                    act.wait_ge(own_summed, i + 1)
                    act.sem_inc(own_tick, 1)
                    for m, out in enumerate(own["outs"]):
                        ins = nc.scalar.activation(cols(out, i * P, P), own_ps[:, m * P:(m + 1) * P], ACT.Identity,
                                                   bias=own["bias"][:, m:m + 1])
                    ins.then_inc(own_stored, 1)
                looped(act, BLOCKS, body)
            if gate:
                def body(i):
                    for h in range(RING):
                        q, r = i * RING + h, h % 2
                        act.wait_ge(at_made, q + 1)
                        if holds_back(q - 1):
                            act.wait_ge(operands_made, q - 1)
                        act.wait_ge(gathered[h], gathers.count(h, GROUP_TILES * (i + 1)))
                        for t in range(GROUP_TILES):
                            ins = nc.scalar.activation(sig[:, r, t, :], at_ps[:, r, 0:WIN], ACT.Sigmoid, bias=rows[:, h, t, P:P + 1])
                        ins.then_inc(sig_made, 1)
                looped(act, ITERS, body)

        @block.tensor
        def _(pe):
            def hidden_layer(i, q, r4):
                if holds_back(q - 1):
                    pe.wait_ge(hidden_made, q - 1)
                pe.wait_ge(edge_in_loaded[r4], 16 * i + 16)
                nc.tensor.matmul(hidden_ps[0:HID, r4 % 2, :], extra["w_fc1"], edge_in[:, r4, :],
                                 start=True, stop=True).then_inc(hidden_summed, 1)

            def weights(q, r):
                if holds_back(q - 1):
                    pe.wait_ge(operands_made, q - 1)
                pe.wait_ge(hidden_made, q + 1)
                for t in range(GROUP_TILES):
                    ins = nc.tensor.matmul(weight_ps[:, r, t * P:(t + 1) * P], hidden[:, r, t * P:(t + 1) * P],
                                           extra["w_fc2"], start=True, stop=True)
                ins.then_inc(weight_made, 1)

            def at_dst(q, r, base):
                if holds_back(q - 1):
                    pe.wait_ge(sig_made, q - 1)
                nc.tensor.matmul(at_ps[:, r, 0:WIN], extra["w_dst"], cols(extra["x"], base, WIN),
                                 start=True, stop=True).then_inc(at_made, 1)

            if gate:
                at_dst(0, 0, load_bases(PE_E, 1, 1)[0])
            if tensor:
                hidden_layer(0, 0, 0)
                hidden_layer(0, 1, 1)
                weights(0, 0)

            def own_term(i, h):
                if h == 1 and own["enc"] is not None:
                    if holds_back(i):
                        pe.wait_ge(z_made, i)
                    nc.tensor.matmul(encoded_ps[:, 0:P], own["enc"][0], cols(own["sources"][0], i * P, P),
                                     start=True, stop=True).then_inc(z_encoded, 1)
                if h == 3:
                    if holds_back(i):
                        pe.wait_ge(own_stored, i)
                    pe.wait_ge(z_made, i + 1)
                    K = len(own["sources"])
                    for m in range(len(own["outs"])):
                        for k in range(K):
                            ins = nc.tensor.matmul(own_ps[:, m * P:(m + 1) * P], own["wr"][k][:, m * P:(m + 1) * P],
                                                   z_block[:, k, :], start=(k == 0), stop=(k == K - 1))
                    ins.then_inc(own_summed, 1)

            def body(i):
                if gate:
                    ahead = load_bases(PE_E, i * RING + 2, RING)
                for h in range(RING):
                    q, r = i * RING + h, h % 2
                    if plain:
                        own_term(i, h)
                    if gate:
                        at_dst(q + 1, (h + 1) % 2, ahead[h])
                    if tensor:
                        r4 = (h + LOOK) % 4
                        hidden_layer(i + (1 if h + LOOK >= 4 else 0), q + LOOK, r4)
                        weights(q + 1, (h + 1) % 2)
                    if holds_back((q - 1) * n_acc):
                        pe.wait_ge(added, (q - 1) * n_acc)
                    if not plain:
                        pe.wait_ge(operands_made, q + 1)
                    else:
                        pe.wait_ge(hot_made, q + 1)
                        pe.wait_ge(gathered[h], gathers.count(h, GROUP_TILES * (i + 1)))
                    for t in range(GROUP_TILES):
                        first, last = t == 0, t == GROUP_TILES - 1
                        if plain:
                            for a in range(A):
                                ins = nc.tensor.matmul(sums[a][:, r, 0:WIN], rows[:, h, t, a * P:(a + 1) * P],
                                                       hot[:, r, t, :], start=first, stop=last)
                        elif gate:
                            nc.tensor.matmul(sums[0][:, r, 0:WIN], rows[:, h, t, 0:P], hot_sig[:, r, t, :],
                                             start=first, stop=last)
                            ins = nc.tensor.matmul(slot_ps[0:SLOTS + 1, r, 0:WIN], slot_in[:, r, t, :],
                                                   hot[:, r, t, :], start=first, stop=last)
                        else:
                            nc.tensor.matmul(sums[0][:, r, 0:WIN], prod_a[:, r, t, :], hot[:, r, t, :],
                                             start=first, stop=last)
                            ins = nc.tensor.matmul(sums[1][:, r, 0:WIN], prod_b[:, r, t, :], hot[:, r, t, :],
                                                   start=first, stop=last)
                    ins.then_inc(summed, 1)
            looped(pe, ITERS, body)

        @block.vector
        def _(dve):
            targets = [(sums[a], P, aggs[a]) for a in range(A)]
            if gate:
                targets.append((slot_ps, SLOTS + 1, extra["slot_sums"]))

            def add_up(q, r, start):
                dve.wait_ge(summed, q + 1)
                if holds_back(q * n_acc):
                    dve.wait_ge(added, q * n_acc)
                if plain:
                    for a in range(A):
                        ins = nc.vector.tensor_tensor(scaled_sums[:, a, :], sums[a][:, r, 0:WIN],
                                                      cols(extra["inv_count"], start, WIN), ALU.mult)
                    ins.then_inc(scaled, 1)
                    dve.wait_ge(scaled, q + 1)
                for a, (ps, rws, region) in enumerate(targets):
                    into = region[0:rws, bass.ds(start, WIN)]
                    term = scaled_sums[:, a, :] if plain else ps[0:rws, r, 0:WIN]
                    nc.vector.tensor_tensor(into, into, term, ALU.add).then_inc(added, 1)

            def operands(i, h):
                q, r = i * RING + h, h % 2
                if holds_back(q - 1):
                    dve.wait_ge(summed, q - 1)
                nc.vector.tensor_tensor(hot[:, r, :, :], iota[:].unsqueeze(1).broadcast_to([P, GROUP_TILES, WIN]),
                                        cols(rel, q * GROUP_TILES, GROUP_TILES).unsqueeze(2).broadcast_to([P, GROUP_TILES, WIN]),
                                        ALU.is_equal).then_inc(hot_made, 1)
                if gate:
                    slot_math = SlotMath(nc, GROUP_TILES, extra, q, reaches[:, r, :, :], rank[:], slot_in[:, r, :, :])
                    slot_math.reach().then_inc(reached, 1)
                    dve.wait_ge(reached, q + 1)
                    slot_math.rank_edges().then_inc(ranked, 1)
                    dve.wait_ge(ranked, q + 1)
                    slot_math.place_sources()
                    dve.wait_ge(hot_made, q + 1)
                    dve.wait_ge(sig_made, q + 1)
                    nc.vector.tensor_tensor(hot_sig[:, r, :, :], hot[:, r, :, :], sig[:, r, :, :],
                                            ALU.mult).then_inc(operands_made, 1)
                if tensor:
                    m = TensorMath(nc, GROUP_TILES, weight_ps[:, r, :], rows[:, h, :, :], y_ea0[:, r, :, :],
                                   cols(extra["edge_attr"], q * GROUP_TILES * 4, GROUP_TILES * 4), y_ea1[:],
                                   w2_y0[:], dot[:], prod_a[:, r, :, :], prod_b[:, r, :, :])
                    dve.wait_ge(gathered[h], gathers.count(h, GROUP_TILES * (i + 1)))
                    if holds_back(q):
                        dve.wait_ge(operands_made, q)
                    m.y1_times_ea1().then_inc(step, 1)
                    dve.wait_ge(weight_made, q + 1)
                    m.y0_weighed().then_inc(step, 1)
                    dve.wait_ge(step, 3 * q + 1)
                    m.dot_first().then_inc(step, 1)
                    dve.wait_ge(ea0_made, q + 1)
                    m.a_scalars()
                    dve.wait_ge(step, 3 * q + 3)
                    m.dot_second().then_inc(dotted, 1)
                    m.b_vectors()
                    m.a_vectors()
                    dve.wait_ge(dotted, q + 1)
                    m.b_scalars().then_inc(operands_made, 1)

            if gate:
                nc.vector.memset(reaches[:], 1.0)
                nc.vector.memset(slot_in[:], 1.0).then_inc(filled, 1)
                dve.wait_ge(filled, 1)

            def body(i):
                starts = load_bases(DVE_E, i * RING, RING)
                for h in range(RING):
                    operands(i, h)
                    if not (isinstance(i, int) and i == 0 and h == 0):
                        add_up(i * RING + h - 1, (h - 1) % 2, starts[h])
            looped(dve, ITERS, body)
            add_up(GROUPS - 1, (GROUPS - 1) % 2, load_bases(DVE_E, GROUPS, 1)[0])
            dve.wait_ge(added, GROUPS * n_acc)
    gathers.end_phase(RING, GROUP_TILES * ITERS)


class Far:

    def __init__(self, nc, sb):
        self.any, self.group = sb("far_any", [1, 1], I32), sb("far_group", [1, WINDOWS], I32)
        self.shift = sb("far_shift", [P, WINDOWS])
        self.gathered = nc.alloc_semaphore("far_gathered", 250)
        self.passes = 0


def prep_phase(nc, rel, bases, far, inputs, ident):
    with Scope(nc, "prep") as s:
        dst, base_bc = s.sb("dst", [P, TILES], I32), s.sb("base_bc", [P, GROUPS], I32)
        base_cols, starts = s.sb("base_cols", [P, 2, BASE_COLS], I32), s.sb("starts", [P, WINDOWS])
        base_f, delta = s.sb("base_f", [P, BASE_COLS]), s.sb("delta", [P, BASE_COLS])
        ones = s.sb("ones", [P, P])
        passed, stepped = s.sb("passed", [P, BASE_COLS, WINDOWS]), s.sb("stepped", [P, BASE_COLS, WINDOWS])
        last, none, off = s.sb("last", [P, WINDOWS]), s.sb("none", [P, WINDOWS]), s.sb("off", [P, WINDOWS])
        most, top = s.sb("most", [P, 1]), s.sb("top", [1, 1])
        count_ps, base_ps, most_ps = s.ps("count", [P, 512]), s.ps("base", [P, 512]), s.ps("most", [1, 512])
        loaded, step, counted, turned = s.sem("loaded"), s.sem("step"), s.sem("counted"), s.sem("turned")
        block = s.block()

        @block.sync
        def _(sp):
            sp.dma_start(dst[:], inputs["dst"]).then_inc(loaded, 16)
            sp.dma_start(base_bc[:], inputs["bases"][0:1, 1:1 + GROUPS].broadcast_to([P, GROUPS])).then_inc(loaded, 16)
            sp.dma_start(bases[:], inputs["bases"]).then_inc(loaded, 16)
            sp.dma_start(base_cols[:].rearrange("p a k -> p (a k)"), inputs["base_cols"]).then_inc(loaded, 16)
            sp.dma_start(starts[:], inputs["win_start"]).then_inc(loaded, 16)
            sp.wait_ge(loaded, 80)

        @block.vector
        def _(dve):
            done = 0

            def after(ins):
                nonlocal done
                done += 1
                ins.then_inc(step, 1)
                dve.wait_ge(step, done)

            dve.wait_ge(loaded, 80)
            nc.vector.memset(ones[:], 1.0)
            nc.vector.tensor_copy(base_f[:], base_cols[:, 0, :])
            nc.vector.tensor_tensor(delta[:], base_cols[:, 0, :], base_cols[:, 1, :], ALU.subtract)
            shape = [P, GROUPS, GROUP_TILES]
            after(nc.vector.tensor_tensor(rel[:, 0:TILES].rearrange("p (g t) -> p g t", t=GROUP_TILES),
                                          dst[:].rearrange("p (g t) -> p g t", t=GROUP_TILES),
                                          base_bc[:].unsqueeze(2).broadcast_to(shape), ALU.subtract))
            for k in range(BASE_COLS):
                nc.vector.tensor_scalar(passed[:, k, :], starts[:], base_f[:, k:k + 1], None, ALU.is_gt)
            for k in range(BASE_COLS):
                nc.vector.tensor_scalar(stepped[:, k, :], starts[:], base_f[:, k:k + 1], delta[:, k:k + 1],
                                        ALU.is_gt, ALU.mult)
            after(nc.vector.reduce_max(most[:], rel[:, 0:TILES], mybir.AxisListType.X))
            dve.wait_ge(counted, 1)
            nc.vector.tensor_scalar(far.group[:], count_ps[0:1, 0:WINDOWS], -1.0, 0.0, ALU.add, ALU.max)
            after(nc.vector.tensor_copy(last[:], base_ps[:, 0:WINDOWS]))
            nc.vector.tensor_scalar(none[:], last[:], 0.0, -float(after_all_nodes()), ALU.is_equal, ALU.mult)
            after(nc.vector.scalar_tensor_tensor(off[:], last[:], -1.0, starts[:], ALU.add, ALU.subtract))
            nc.vector.tensor_tensor(far.shift[:], off[:], none[:], ALU.add)
            dve.wait_ge(turned, 1)
            after(nc.vector.reduce_max(top[:], most_ps[:, 0:P], mybir.AxisListType.X))
            nc.vector.tensor_scalar(far.any[:], top[:], float(WIN), None, ALU.is_ge)

        @block.tensor
        def _(pe):
            pe.wait_ge(step, 2)
            for src, ps in ((passed, count_ps), (stepped, base_ps)):
                for k in range(BASE_COLS):
                    ins = nc.tensor.matmul(ps[:, 0:WINDOWS], ones[:], src[:, k, :],
                                           start=(k == 0), stop=(k == BASE_COLS - 1))
            ins.then_inc(counted, 1)
            nc.tensor.transpose(most_ps[:, 0:P], most[:], ident[:]).then_inc(turned, 1)


def after_all_nodes():
    return 1 << 17


def far_pass(nc, far, name, kind, table, width, src_dram, rel, iota, aggs, extra):
    tensor, gate, plain = kind == "tensor", kind == "gate", kind == "sum"
    A = 1 if gate else 2 if tensor else width // P
    T = GROUP_TILES
    before = far.passes * (WINDOWS - 1) * T * 16
    with Scope(nc, name) as s:
        idx, rows = s.sb("idx", [P, T], I32), s.sb("rows", [P, T, width])
        moved, match, past = s.sb("moved", [P, T]), s.sb("match", [P, T, WIN]), s.sb("past", [P, T])
        hot = s.sb("hot", [P, T, WIN])
        sums = [s.ps(f"sums{a}", [P, 512]) for a in range(A)]
        loaded, step, hot_made, summed = s.sem("loaded"), s.sem("step"), s.sem("hot_made"), s.sem("summed")
        done, tick, sp_tick, operands_made = s.sem("done"), s.sem("tick"), s.sem("sp_tick"), s.sem("operands_made")
        targets = [(sums[a], P, aggs[a]) for a in range(A)]
        if tensor:
            edge_in, hidden = s.sb("edge_in", [BASIS, T * P]), s.sb("hidden", [HID, T * P])
            y_ea0, y_ea1 = s.sb("y_ea0", [P, T, P]), s.sb("y_ea1", [P, T, 3, MUL])
            w2_y0, dot = s.sb("w2_y0", [P, T, MUL]), s.sb("dot", [P, T, 2, MUL])
            prod_a, prod_b = s.sb("prod_a", [P, T, P]), s.sb("prod_b", [P, T, P])
            hidden_ps, weight_ps = s.ps("hidden", [P, 512]), s.ps("weight", [P, 512])
            hidden_summed, hidden_made, weight_made = s.sem("hidden_summed"), s.sem("hidden_made"), s.sem("weight_made")
            ea0_made, prepared = s.sem("ea0_made"), s.sem("prepared")
        if gate:
            sig, hot_sig = s.sb("sig", [P, T, WIN]), s.sb("hot_sig", [P, T, WIN])
            slot_in, at_ps = s.sb("slot_in", [P, T, SLOTS + 1]), s.ps("at", [P, 512])
            reaches, rank = s.sb("reaches", [P, T, SLOTS + 1]), s.sb("rank", [P, T, SLOTS])
            at_made, ranked, filled = s.sem("at_made"), s.sem("ranked"), s.sem("filled")
            slot_ps = s.ps("slot", [P, 512])
            sig_made = s.sem("sig_made")
            targets.append((slot_ps, SLOTS + 1, extra["slot_sums"]))
        if plain:
            scaled_sums, scaled = s.sb("scaled_sums", [P, A, WIN]), s.sem("scaled")
        block = s.block()

        def windows(eng, body, group=True):
            with eng.If(eng.value_load(far.any[0:1, 0:1], min_val=0, max_val=1)):
                with eng.Fori(1, WINDOWS) as w:
                    body(w, eng.value_load(far.group[0:1, bass.ds(w, 1)], min_val=0, max_val=GROUPS - 1) if group else None)

        @block.sync
        def _(sp):
            def body(w, g):
                sp.wait_ge(done, w)
                sp.sem_inc(sp_tick, 1)
                sp.dma_start(idx[:], cols(src_dram, g * T, T)).then_inc(loaded, 16)
                if tensor:
                    sp.dma_start(edge_in[:], cols(extra["edge_in"], g * (T * P), T * P)).then_inc(loaded, 16)
            windows(sp, body)

        @block.gpsimd
        def _(pool):
            def body(w, g):
                pool.wait_ge(loaded, w * (32 if tensor else 16))
                pool.sem_inc(tick, 1)
                for t in range(T):
                    nc.gpsimd.indirect_dma_start(
                        rows[:, t, :], None, table, bass.IndirectOffsetOnAxis(ap=idx[:, t:t + 1], axis=0)
                    ).then_inc(far.gathered, 16)
            windows(pool, body, group=False)

        @block.scalar
        def _(act):
            if tensor:
                def body(w, g):
                    act.wait_ge(hidden_summed, w)
                    nc.scalar.activation(hidden[:], hidden_ps[0:HID, 0:T * P], ACT.Silu,
                                         scale=1.0 / math.sqrt(BASIS)).then_inc(hidden_made, 1)
                    act.wait_ge(far.gathered, w * (16 * T) + before)
                    for t in range(T):
                        ins = nc.scalar.activation(y_ea0[:, t, :], rows[:, t, :], ACT.Copy,
                                                   scale=cols(extra["edge_attr"], g * (T * 4) + t * 4, 1))
                    ins.then_inc(ea0_made, 1)
                windows(act, body)
            if gate:
                def body(w, _):
                    act.wait_ge(at_made, w)
                    act.wait_ge(far.gathered, w * (16 * T) + before)
                    for t in range(T):
                        ins = nc.scalar.activation(sig[:, t, :], at_ps[:, 0:WIN], ACT.Sigmoid, bias=rows[:, t, P:P + 1])
                    ins.then_inc(sig_made, 1)
                windows(act, body, group=False)

        @block.tensor
        def _(pe):
            def body(w, _):
                if tensor:
                    pe.wait_ge(loaded, w * 32)
                    nc.tensor.matmul(hidden_ps[0:HID, 0:T * P], extra["w_fc1"], edge_in[:],
                                     start=True, stop=True).then_inc(hidden_summed, 1)
                    pe.wait_ge(hidden_made, w)
                    for t in range(T):
                        ins = nc.tensor.matmul(weight_ps[:, t * P:(t + 1) * P], hidden[:, t * P:(t + 1) * P],
                                               extra["w_fc2"], start=True, stop=True)
                    ins.then_inc(weight_made, 1)
                if gate:
                    pe.wait_ge(done, w)
                    nc.tensor.matmul(at_ps[:, 0:WIN], extra["w_dst"], cols(extra["x"], w * WIN, WIN),
                                     start=True, stop=True).then_inc(at_made, 1)
                if plain:
                    pe.wait_ge(hot_made, w)
                    pe.wait_ge(far.gathered, w * (16 * T) + before)
                else:
                    pe.wait_ge(operands_made, w)
                for t in range(T):
                    first, last = t == 0, t == T - 1
                    if plain:
                        for a in range(A):
                            ins = nc.tensor.matmul(sums[a][:, 0:WIN], rows[:, t, a * P:(a + 1) * P], hot[:, t, :],
                                                   start=first, stop=last)
                    elif gate:
                        nc.tensor.matmul(sums[0][:, 0:WIN], rows[:, t, 0:P], hot_sig[:, t, :], start=first, stop=last)
                        ins = nc.tensor.matmul(slot_ps[0:SLOTS + 1, 0:WIN],
                                               slot_in[:, t, :], hot[:, t, :],
                                               start=first, stop=last)
                    else:
                        nc.tensor.matmul(sums[0][:, 0:WIN], prod_a[:, t, :], hot[:, t, :], start=first, stop=last)
                        ins = nc.tensor.matmul(sums[1][:, 0:WIN], prod_b[:, t, :], hot[:, t, :], start=first, stop=last)
                ins.then_inc(summed, 1)
            windows(pe, body, group=False)

        @block.vector
        def _(dve):
            if gate:
                nc.vector.memset(reaches[:], 1.0)
                nc.vector.memset(slot_in[:], 1.0).then_inc(filled, 1)
                dve.wait_ge(filled, 1)
            dve.sem_inc(done, 1)

            def body(w, g):
                dve.wait_ge(done, w)
                r = cols(rel, g * T, T)
                shape = [P, T, WIN]
                nc.vector.tensor_scalar(past[:], r, float(WIN), None, ALU.is_ge)
                nc.vector.tensor_scalar(moved[:], r, cols(far.shift, w, 1), None, ALU.add).then_inc(step, 1)
                dve.wait_ge(step, w * 2 - 1)
                nc.vector.tensor_tensor(match[:], iota[:].unsqueeze(1).broadcast_to(shape),
                                        moved[:].unsqueeze(2).broadcast_to(shape), ALU.is_equal).then_inc(step, 1)
                dve.wait_ge(step, w * 2)
                nc.vector.tensor_tensor(hot[:], match[:], past[:].unsqueeze(2).broadcast_to(shape),
                                        ALU.mult).then_inc(hot_made, 1)
                if gate:
                    slot_math = SlotMath(nc, T, extra, g, reaches[:], rank[:], slot_in[:])
                    slot_math.reach().then_inc(ranked, 1)
                    dve.wait_ge(ranked, w * 2 - 1)
                    slot_math.rank_edges().then_inc(ranked, 1)
                    dve.wait_ge(ranked, w * 2)
                    slot_math.place_sources()
                    dve.wait_ge(hot_made, w)
                    dve.wait_ge(sig_made, w)
                    nc.vector.tensor_tensor(hot_sig[:], hot[:], sig[:], ALU.mult).then_inc(operands_made, 1)
                if tensor:
                    m = TensorMath(nc, T, weight_ps[:, 0:T * P], rows[:], y_ea0[:],
                                   cols(extra["edge_attr"], g * (T * 4), T * 4), y_ea1[:], w2_y0[:], dot[:],
                                   prod_a[:], prod_b[:])
                    dve.wait_ge(far.gathered, w * (16 * T) + before)
                    m.y1_times_ea1()
                    dve.wait_ge(weight_made, w)
                    m.y0_weighed().then_inc(prepared, 1)
                    dve.wait_ge(prepared, w * 3 - 2)
                    m.dot_first().then_inc(prepared, 1)
                    dve.wait_ge(prepared, w * 3 - 1)
                    m.dot_second().then_inc(prepared, 1)
                    dve.wait_ge(ea0_made, w)
                    m.a_scalars()
                    m.a_vectors()
                    m.b_vectors()
                    dve.wait_ge(prepared, w * 3)
                    m.b_scalars().then_inc(operands_made, 1)
                dve.wait_ge(summed, w)
                if plain:
                    for a in range(A):
                        ins = nc.vector.tensor_tensor(scaled_sums[:, a, :], sums[a][:, 0:WIN],
                                                      cols(extra["inv_count"], w * WIN, WIN), ALU.mult)
                    ins.then_inc(scaled, 1)
                    dve.wait_ge(scaled, w)
                for a, (ps, rws, region) in enumerate(targets):
                    into = region[0:rws, bass.ds(w * WIN, WIN)]
                    term = scaled_sums[:, a, :] if plain else ps[0:rws, 0:WIN]
                    ins = nc.vector.tensor_tensor(into, into, term, ALU.add)
                ins.then_inc(done, 1)
            windows(dve, body)
    far.passes += 1


def tensor_post_phase(nc, X, aggs, lhs, attr_bc):
    with Scope(nc, "tpost") as s:
        acc = s.ps("acc", [P, 2, 512])
        scaled = s.sb("scaled", [P, 2, CHUNK])
        summed, weighed, added = s.sem("summed"), s.sem("weighed"), s.sem("added")
        block = s.block()

        @block.tensor
        def _(pe):
            def body(i):
                for c in range(2):
                    n = i * 2 + c
                    if holds_back(n - 1):
                        pe.wait_ge(weighed, n - 1)
                    for k, region in enumerate([X] + aggs):
                        ins = nc.tensor.matmul(acc[:, c, 0:CHUNK], lhs[k], cols(region, n * CHUNK, CHUNK),
                                               start=(k == 0), stop=(k == len(aggs)))
                    ins.then_inc(summed, 1)
            looped(pe, CHUNKS // 2, body)

        @block.vector
        def _(dve):
            def body(i):
                for c in range(2):
                    n = i * 2 + c
                    dve.wait_ge(summed, n + 1)
                    if holds_back(n - 1):
                        dve.wait_ge(added, n - 1)
                    nc.vector.tensor_tensor(scaled[:, c, :], acc[:, c, 0:CHUNK], cols(attr_bc, n * CHUNK, CHUNK),
                                            ALU.mult).then_inc(weighed, 1)
                for c in range(2):
                    n = i * 2 + c
                    dve.wait_ge(weighed, n + 1)
                    nc.vector.tensor_tensor(cols(X, n * CHUNK, CHUNK), cols(X, n * CHUNK, CHUNK), scaled[:, c, :],
                                            ALU.add).then_inc(added, 1)
            looped(dve, CHUNKS // 2, body)


def slot_tables_phase(nc, slot_sums, slot_idx, inv_count, ident):
    C = SLOTS + 1
    with Scope(nc, "slott") as s:
        turned = s.ps("turned", [P, BLOCKS * C])
        sl, empty = s.sb("sl", [P, BLOCKS, C]), s.sb("empty", [P, BLOCKS, SLOTS])
        floored = s.sb("floored", [P, BLOCKS])
        flipped, step = s.sem("flipped"), s.sem("step")
        block = s.block()

        @block.tensor
        def _(pe):
            for b in range(BLOCKS):
                ins = nc.tensor.transpose(turned[:, b * C:(b + 1) * C], slot_sums[0:C, b * P:(b + 1) * P], ident[0:C, 0:C])
            ins.then_inc(flipped, 1)

        @block.vector
        def _(dve):
            dve.wait_ge(flipped, 1)
            nc.vector.tensor_copy(sl[:].rearrange("p b c -> p (b c)"), turned[:]).then_inc(step, 1)
            dve.wait_ge(step, 1)
            nc.vector.tensor_scalar(floored[:], sl[:, :, SLOTS], 1.0, None, ALU.max)
            for j in range(SLOTS):
                ins = nc.vector.tensor_scalar(empty[:, :, j], sl[:, :, SLOTS], float(j), float(N_NODES), ALU.is_le, ALU.mult)
            ins.then_inc(step, 1)
            dve.wait_ge(step, 2)
            nc.vector.reciprocal(inv_count, floored[:])
            nc.vector.tensor_tensor(slot_idx.rearrange("p (b s) -> p b s", s=SLOTS), sl[:, :, 0:SLOTS], empty[:], ALU.add)


def gru_phase(nc, X, agg, H, w, stats):
    names = ("r", "z", "in", "hn")
    with Scope(nc, "gru") as s:
        ps = {g: s.ps(g, [P, 2, 512]) for g in names}
        t = {g: s.sb(g, [P, 2, CHUNK]) for g in ("r", "z", "hn", "rh", "pre", "n", "d", "e")}
        summed, gated, mixed, tanhed, done, step, tick = (s.sem("summed"), s.sem("gated"), s.sem("mixed"),
                                                          s.sem("tanhed"), s.sem("done"), s.sem("step"), s.sem("tick"))
        block = s.block()

        @block.tensor
        def _(pe):
            def body(i):
                for c in range(2):
                    n = 2 * i + c
                    if holds_back(n - 1):
                        pe.wait_ge(gated, n - 1)
                    if holds_back(n - 1):
                        pe.wait_ge(mixed, n - 1)
                    x, m = cols(X, n * CHUNK, CHUNK), cols(agg, n * CHUNK, CHUNK)
                    for k, g in enumerate(("r", "z")):
                        nc.tensor.matmul(ps[g][:, c, 0:CHUNK], w["ih"][:, k * P:(k + 1) * P], m, start=True, stop=False)
                        nc.tensor.matmul(ps[g][:, c, 0:CHUNK], w["hh"][:, k * P:(k + 1) * P], x, start=False, stop=True)
                    nc.tensor.matmul(ps["in"][:, c, 0:CHUNK], w["ih"][:, 2 * P:3 * P], m, start=True, stop=True)
                    nc.tensor.matmul(ps["hn"][:, c, 0:CHUNK], w["hh"][:, 2 * P:3 * P], x, start=True, stop=True).then_inc(summed, 1)
            looped(pe, CHUNKS // 2, body)

        @block.scalar
        def _(act):
            def body(i):
                for c in range(2):
                    n = 2 * i + c
                    if holds_back(n - 1):
                        act.wait_ge(done, n - 1)
                    act.wait_ge(summed, n + 1)
                    nc.scalar.activation(t["r"][:, c, :], ps["r"][:, c, 0:CHUNK], ACT.Sigmoid, bias=w["b_r"])
                    nc.scalar.activation(t["z"][:, c, :], ps["z"][:, c, 0:CHUNK], ACT.Sigmoid, bias=w["b_z"])
                    nc.scalar.activation(t["hn"][:, c, :], ps["hn"][:, c, 0:CHUNK], ACT.Identity, bias=w["b_hn"]).then_inc(gated, 1)
                for c in range(2):
                    n = 2 * i + c
                    act.wait_ge(mixed, n + 1)
                    nc.scalar.activation(t["n"][:, c, :], t["pre"][:, c, :], ACT.Tanh, bias=w["b_in"]).then_inc(tanhed, 1)
            looped(act, CHUNKS // 2, body)

        @block.vector
        def _(dve):
            def body(i):
                for c in range(2):
                    n = 2 * i + c
                    dve.wait_ge(gated, n + 1)
                    if holds_back(n - 1):
                        dve.wait_ge(tanhed, n - 1)
                    nc.vector.tensor_tensor(t["rh"][:, c, :], t["r"][:, c, :], t["hn"][:, c, :], ALU.mult).then_inc(step, 1)
                    dve.wait_ge(step, 6 * i + c + 1)
                    nc.vector.tensor_tensor(t["pre"][:, c, :], t["rh"][:, c, :], ps["in"][:, c, 0:CHUNK],
                                            ALU.add).then_inc(mixed, 1)
                for c in range(2):
                    n = 2 * i + c
                    dve.wait_ge(tanhed, n + 1)
                    nc.vector.tensor_tensor(t["d"][:, c, :], cols(X, n * CHUNK, CHUNK), t["n"][:, c, :],
                                            ALU.subtract).then_inc(step, 1)
                    dve.wait_ge(step, 6 * i + 2 + 2 * c + 1)
                    nc.vector.tensor_tensor(t["e"][:, c, :], t["d"][:, c, :], t["z"][:, c, :], ALU.mult).then_inc(step, 1)
                    dve.wait_ge(step, 6 * i + 2 + 2 * c + 2)
                    nc.vector.tensor_tensor(cols(H, n * CHUNK, CHUNK), t["e"][:, c, :], t["n"][:, c, :],
                                            ALU.add).then_inc(done, 1)
                    dve.wait_ge(done, n + 1)
                    dve.sem_inc(tick, 1)
                    chunk_stats(nc, stats, H, n)
            looped_but_last(dve, CHUNKS // 2, body)


def blank_row_phase(nc, name, blank, w_T, b_row, table):
    with Scope(nc, name) as s:
        ps, row = s.ps("ps", [1, P]), s.sb("row", [1, P])
        summed, added, stored = s.sem("summed"), s.sem("added"), s.sem("stored")
        block = s.block()

        @block.tensor
        def _(pe):
            nc.tensor.matmul(ps[:], blank, w_T, start=True, stop=True).then_inc(summed, 1)

        @block.vector
        def _(dve):
            dve.wait_ge(summed, 1)
            nc.vector.tensor_tensor(row[:], ps[:], b_row, ALU.add).then_inc(added, 1)

        @block.sync
        def _(sp):
            sp.wait_ge(added, 1)
            sp.dma_start(table[N_NODES:N_NODES + 1, :], row[:]).then_inc(stored, 16)
            sp.wait_ge(stored, 16)


def sort_phase(nc, gathers, name, X, H, table, slot_idx, w, ident, stats, spread):
    SUB = 7
    with Scope(nc, name) as s:
        idx = s.sb("idx", [P, SUB, SLOTS], I32)
        rows = s.sb("rows", [P, SUB, SLOTS, P])
        t1, t2, t3 = s.sb("t1", [P, SLOTS, P]), s.sb("t2", [P, SLOTS, P]), s.sb("t3", [P, 2, P])
        acc = s.sb("acc", [P, 3, P])
        out = s.sb("out", [P, SUB, P])
        turned = s.ps("turned", [P, SUB, 512])
        idx_copied = [s.sem(f"idx_copied{b}") for b in range(SUB)]
        gathered = gathers.sems
        ticked = s.sem("ticked")
        if spread is not None:
            diagonal, spread_ps = s.sb("diagonal", [P, P]), s.ps("spread", [P, 512])
            diagonal_made, spread_made, ticked_act = s.sem("diagonal_made"), s.sem("spread_made"), s.sem("ticked_act")
        tick, step, sorted_, flipped, done = s.sem("tick"), s.sem("step"), s.sem("sorted"), s.sem("flipped"), s.sem("done")
        block = s.block()

        @block.sync
        def _(sp):
            def body(i):
                for b in range(SUB):
                    n = i * SUB + b
                    if holds_back(n - SUB + 1):
                        sp.wait_ge(sorted_, n - SUB + 1)
                    sp.dma_start(idx[:, b, :], cols(slot_idx, n * SLOTS, SLOTS)).then_inc(idx_copied[b], 16)
            looped(sp, BLOCKS // SUB, body)

        @block.gpsimd
        def _(pool):
            def body(i):
                for b in range(SUB):
                    n = i * SUB + b
                    if holds_back(n - SUB + 1):
                        pool.wait_ge(sorted_, n - SUB + 1)
                    pool.wait_ge(idx_copied[b], 16 * i + 16)
                    pool.sem_inc(tick, 1)
                    for j in range(SLOTS):
                        nc.gpsimd.indirect_dma_start(
                            rows[:, b, j, :], None, table, bass.IndirectOffsetOnAxis(ap=idx[:, b, j:j + 1], axis=0)
                        ).then_inc(gathered[b], 16)
            looped(pool, BLOCKS // SUB, body)

        @block.tensor
        def _(pe):
            def body(i):
                for b in range(SUB):
                    n = i * SUB + b
                    if holds_back(n - SUB + 1):
                        pe.wait_ge(done, n - SUB + 1)
                    if spread is not None:
                        pe.wait_ge(diagonal_made, n + 1)
                        nc.tensor.matmul(spread_ps[:, 0:P], spread[1][:], diagonal[:], start=True, stop=True)\
                            .then_inc(spread_made, 1)
                    pe.wait_ge(sorted_, n + 1)
                    nc.tensor.transpose(turned[:, b, 0:P], out[:, b, :], ident[:]).then_inc(flipped, 1)
            looped(pe, BLOCKS // SUB, body)

        if spread is not None:
            @block.scalar
            def _(act):
                def body(n):
                    nc.scalar.activation(diagonal[:], ident[:], ACT.Copy, scale=cols(spread[0], n, 1))\
                        .then_inc(diagonal_made, 1)
                    act.wait_ge(spread_made, n + 1)
                    act.sem_inc(ticked_act, 1)
                    nc.scalar.activation(cols(spread[2], n * P, P), spread_ps[:, 0:P], ACT.Copy)
                looped(act, BLOCKS, body)

        @block.vector
        def _(dve):
            STEPS = 5

            def finish(n, b):
                dve.wait_ge(flipped, n + 1)
                nc.vector.scalar_tensor_tensor(cols(H, n * P, P), cols(X, n * P, P), w["a"], turned[:, b, 0:P],
                                               ALU.mult, ALU.add).then_inc(done, 1)

            def block_stats(n):
                dve.wait_ge(done, n + 1)
                dve.sem_inc(ticked, 1)
                width = min(P, N_NODES - n * P) if isinstance(n, int) else P
                nc.vector.bn_stats(cols(stats, n * 6, 6), cols(H, n * P, width))

            def body(i):
                for b in range(SUB):
                    n = i * SUB + b

                    def after(k):
                        dve.wait_ge(step, n * STEPS + k)
                    dve.wait_ge(gathered[b], gathers.count(b, SLOTS * (i + 1)))
                    if holds_back(n - SUB + 1):
                        dve.wait_ge(flipped, n - SUB + 1)
                    r = rows[:, b, :, :]
                    nc.vector.tensor_tensor(t1[:, 0:2, :], r[:, 0:4:2, :], r[:, 1:4:2, :], ALU.min)
                    nc.vector.tensor_tensor(t1[:, 2:4, :], r[:, 0:4:2, :], r[:, 1:4:2, :], ALU.max).then_inc(step, 1)
                    after(1)
                    if holds_back(n):
                        dve.wait_ge(sorted_, n)
                    nc.vector.tensor_tensor(t2[:, 0:2, :], t1[:, 0:4:2, :], t1[:, 1:4:2, :], ALU.min)
                    nc.vector.tensor_tensor(t2[:, 2:4, :], t1[:, 0:4:2, :], t1[:, 1:4:2, :], ALU.max).then_inc(step, 1)
                    after(2)
                    nc.vector.tensor_tensor(t3[:, 0, :], t2[:, 1, :], t2[:, 2, :], ALU.min)
                    nc.vector.tensor_tensor(t3[:, 1, :], t2[:, 1, :], t2[:, 2, :], ALU.max)
                    nc.vector.tensor_scalar(acc[:, 0, :], t2[:, 0, :], w["cw"][:, 0:1], w["cb"], ALU.mult, ALU.add).then_inc(step, 1)
                    after(3)
                    nc.vector.scalar_tensor_tensor(acc[:, 1, :], t3[:, 0, :], w["cw"][:, 1:2], acc[:, 0, :],
                                                   ALU.mult, ALU.add).then_inc(step, 1)
                    after(4)
                    nc.vector.scalar_tensor_tensor(acc[:, 2, :], t3[:, 1, :], w["cw"][:, 2:3], acc[:, 1, :],
                                                   ALU.mult, ALU.add).then_inc(step, 1)
                    after(5)
                    nc.vector.scalar_tensor_tensor(out[:, b, :], t2[:, 3, :], w["cw"][:, 3:4], acc[:, 2, :],
                                                   ALU.mult, ALU.add).then_inc(sorted_, 1)
                    if not (isinstance(i, int) and i == 0 and b == 0):
                        finish(n - 1, (b - 1) % SUB)
                        block_stats(n - 1)
            looped(dve, BLOCKS // SUB, body)
            finish(BLOCKS - 1, SUB - 1)
            block_stats(BLOCKS - 1)
    gathers.end_phase(SUB, SLOTS * (BLOCKS // SUB))


def sage_phase(nc, name, means, wl, outs, stats):
    M, K = len(outs), len(means)
    with Scope(nc, name) as s:
        acc = s.ps("acc", [P, 2, M, 512])
        summed, added, tick = s.sem("summed"), s.sem("added"), s.sem("tick")
        block = s.block()

        @block.tensor
        def _(pe):
            def body(i):
                for c in range(2):
                    n = 2 * i + c
                    if holds_back(n - 1):
                        pe.wait_ge(added, n - 1)
                    for m in range(M):
                        for k in range(K):
                            ins = nc.tensor.matmul(acc[:, c, m, 0:CHUNK], wl[k][:, m * P:(m + 1) * P],
                                                   cols(means[k], n * CHUNK, CHUNK), start=(k == 0), stop=(k == K - 1))
                    ins.then_inc(summed, 1)
            looped(pe, CHUNKS // 2, body)

        @block.vector
        def _(dve):
            def body(i):
                for c in range(2):
                    n = 2 * i + c
                    dve.wait_ge(summed, n + 1)
                    for m in range(M):
                        out = cols(outs[m], n * CHUNK, CHUNK)
                        ins = nc.vector.tensor_tensor(out, out, acc[:, c, m, 0:CHUNK], ALU.add)
                    ins.then_inc(added, 1)
                    dve.wait_ge(added, n + 1)
                    dve.sem_inc(tick, 1)
                    for m in range(M):
                        chunk_stats(nc, stats[m], outs[m], n)
            looped_but_last(dve, CHUNKS // 2, body)


def gnn_kernel(nc, inp, out, stop=99):
    Scope.turn = Loads.count = 0
    gathers = Gathers(nc, 7)
    sbuf = ExitStack()
    with sbuf:
        def sb(name, shape, dt=F32):
            return sbuf.enter_context(nc.sbuf_tensor(name, shape, dt))

        def dram(name, shape):
            return nc.dram_tensor(name, shape, F32, kind="Internal").ap()

        X, A, B, C, D, E = (sb(n, [P, REGION]) for n in ("x", "ra", "rb", "rc", "rd", "re"))
        rel = sb("rel", [P, TILES + GROUP_TILES])
        bases = sb("bases", [1, GROUPS + 2], I32)
        iota, ident = sb("iota", [P, WIN]), sb("ident", [P, P])
        ones, eps = sb("ones", [P, P]), sb("eps", [P, 1])
        inv_cols = sb("inv_cols", [P, BLOCKS])
        slot_idx = sb("slot_idx", [P, BLOCKS * SLOTS], I32)
        scale, shift = sb("scale", [P, 2]), sb("shift", [P, 2])
        stats = sb("stats", [P, BLOCKS * 6])
        chunk_halves = [stats[:, m * CHUNKS * 6:(m + 1) * CHUNKS * 6] for m in range(2)]

        far = Far(nc, sb)
        with Scope(nc, "const") as s:
            block = s.block()

            @block.vector
            def _(dve):
                nc.vector.memset(ones[:], 1.0)
                nc.vector.memset(X[:, NP:REGION], 0.0)
                nc.vector.memset(eps[:], EPS)
                nc.vector.memset(rel[:, TILES:], -1.0)

        def edges(name, kind, table, width, aggs, **extra):
            edge_pass(nc, gathers, name, kind, table, width, inp["src"], rel, iota, bases, aggs, extra)
            far_pass(nc, far, name + "_far", kind, table, width, inp["src"], rel, iota, aggs, extra)

        with ExitStack() as st:
            def w(name, shape):
                return st.enter_context(nc.sbuf_tensor(name, shape, F32))
            wl1, wsc, wa, wb = w("wl1", [P, P]), w("wsc", [P, P]), w("wa", [P, P]), w("wb", [P, P])
            fc1, fc2, attr_col = w("fc1", [BASIS, HID]), w("fc2", [HID, P]), w("attr_col", [P, BLOCKS])
            edge_attr = D[:, 0:TILES * 4]
            first = Loads(nc, "first", [(wl1[:], inp["t_l1"]), (wsc[:], inp["t_sc"]), (wa[:], inp["t_l2a"]),
                                        (wb[:], inp["t_l2b"]), (fc1[:], inp["t_fc1"]), (fc2[:], inp["t_fc2"]),
                                        (attr_col[:], inp["attr_col"]), (iota[:], inp["iota"]), (ident[:], inp["ident"]),
                                        (X[:, 0:NP], inp["x_T"])])
            attributes = Loads(nc, "attributes", [(edge_attr, inp["edge_attr"]),
                                                  (C[:, 0:NP], inp["attr_row"].broadcast_to([P, NP]))])
            first.start()
            attributes.start()
            first.await_all()
            s_in, s_mid = 1.0 / math.sqrt(MUL), 1.0 / math.sqrt(2 * MUL) / math.sqrt(16.0)
            c_s, c_x = math.sin(math.pi / 8.0), math.cos(math.pi / 8.0)
            with Scope(nc, "scale_w0") as s:
                block = s.block()

                @block.vector
                def _(dve):
                    nc.vector.tensor_scalar(wl1[:], wl1[:], s_in, None, ALU.mult)
                    nc.vector.tensor_scalar(wsc[:], wsc[:], s_in * c_s, None, ALU.mult)
                    nc.vector.tensor_scalar(wa[:], wa[:], s_mid * c_x, None, ALU.mult)
                    nc.vector.tensor_scalar(wb[:, :], wb[:, :], s_mid * c_x, None, ALU.mult)
                    nc.vector.tensor_scalar(fc2[:], fc2[:], 1.0 / math.sqrt(HID), None, ALU.mult)
            with Scope(nc, "scale_w0b") as s:
                block = s.block()

                @block.vector
                def _(dve):
                    nc.vector.tensor_scalar(wb[3 * MUL:P, :], wb[3 * MUL:P, :], 1.0 / math.sqrt(3.0), None, ALU.mult)
            t0 = dram("table_tensor", (NP, P))
            prep_phase(nc, rel, bases, far, inp, ident)
            table_phase(nc, "tab0", [X], t0, P, ident, rhs=[wl1[:]], row_scale=attr_col, clear=[A[:], B[:], E[:]])
            attributes.await_all()
            edges("pass0", "tensor", t0, P, [A, B], edge_in=inp["edge_in"], edge_attr=edge_attr, w_fc1=fc1[:], w_fc2=fc2[:])
            tensor_post_phase(nc, X, [A, B], [wsc[:], wa[:], wb[:]], C)

        if stop > 0:
            with ExitStack() as st:
                def w(name, shape, dt=F32):
                    return st.enter_context(nc.sbuf_tensor(name, shape, dt))
                wmsg, bmsg = w("wmsg", [P, P + 1]), w("bmsg", [P, P + 1])
                wdst = w("wdst", [P, P])
                wih, whh, gb = w("wih", [P, 3 * P]), w("whh", [P, 3 * P]), w("gb", [P, 8])
                src, dst, before = (D[:, a * TILES:b * TILES].bitcast(I32) for a, b in ((0, 1), (1, 2), (2, 2 + SLOTS)))
                gsum = w("gsum", [P, 2])
                gate_loads = Loads(nc, "gate", [(wmsg[:], inp["g_msg"]), (bmsg[:], inp["g_bmsg"].broadcast_to([P, P + 1])),
                                           (wdst[:], inp["g_dst"]),
                                           (wih[:], inp["g_ih"]), (whh[:], inp["g_hh"]), (gb[:], inp["g_vec"])])
                slot_loads = Loads(nc, "slot", [(src, inp["src"]), (dst, inp["dst"]), (before, inp["dst_before"])])
                gate_loads.start()
                slot_loads.start()
                gate_loads.await_all()
                with Scope(nc, "gsum") as s:
                    block = s.block()

                    @block.vector
                    def _(dve):
                        nc.vector.tensor_tensor(gsum[:], gb[:, 0:2], gb[:, 3:5], ALU.add)
                t1 = dram("table_gate", (NP, P + 1))
                norm_table_phase(nc, "tab1", X, t1, ident, eps, rhs=wmsg[:], bias=bmsg, clear=[A[:]])
                slot_loads.await_all()
                edges("pass1", "gate", t1, P + 1, [A], w_dst=wdst[:], x=X, src=src, dst=dst, dst_before=before,
                      slot_sums=E[0:SLOTS + 1, :])
                slot_tables_phase(nc, E, slot_idx[:], inv_cols[:], ident)
                gru_phase(nc, X, A, B, dict(ih=wih, hh=whh, b_r=gsum[:, 0:1], b_z=gsum[:, 1:2], b_in=gb[:, 2:3],
                                            b_hn=gb[:, 5:6]), chunk_halves[0])
                batchnorm_params_phase(nc, "bn1", [(gb[:, 6:7], gb[:, 7:8], scale[:, 0:1], shift[:, 0:1])],
                                       chunk_halves[:1], eps)

        if stop > 1:
            for k, (src, dst) in enumerate([(X, B), (B, B)]):
                with ExitStack() as st:
                    def w(name, shape):
                        return st.enter_context(nc.sbuf_tensor(f"{name}{k}", shape, F32))
                    wT, brow, vec, sc = w("swT", [P, P]), w("sb", [1, P]), w("svec", [P, 3]), w("ssc", [P, 6])
                    loads = Loads(nc, f"sort{k}_weights", [(wT[:], inp[f"s_w{k}"]), (brow[:], inp[f"s_b{k}"]), (vec[:], inp[f"s_vec{k}"]),
                                                   (sc[:], inp[f"s_sc{k}"].broadcast_to([P, 6]))])
                    loads.start()
                    t2 = dram(f"table_sort{k}", (NP, P))
                    if k == 0:
                        norm_table_phase(nc, "tab20", X, t2, ident, eps, plus=B, normed_by=(scale[:, 0:1], shift[:, 0:1]))
                    else:
                        table_phase(nc, "tab21", [src], t2, P, ident)
                    loads.await_all()
                    blank_row_phase(nc, f"blank{k}", vec[:, 2:3], wT[:], brow[:], t2)
                    sort_phase(nc, gathers, f"sort{k}", src, A, t2, slot_idx, dict(cw=sc[:, 0:4], cb=sc[:, 4:5], a=sc[:, 5:6]), ident,
                               stats, (inv_cols, ones, C) if k == 0 else None)
                    batchnorm_params_phase(nc, f"bn2{k}", [(vec[:, 0:1], vec[:, 1:2], scale[:, 0:1], shift[:, 0:1])],
                                           [stats[:]], eps)
                    add_normed_phase(nc, f"res2{k}", dst, src, A, scale[:, 0:1], shift[:, 0:1])

        if stop > 2:
            with ExitStack() as st:
                def w(name, shape):
                    return st.enter_context(nc.sbuf_tensor("sage_" + name, shape, F32))
                H = 2 * P
                vec = w("avec", [P, 3 + 3 * 6])
                enc, dec, enc_b = w("enc", [P, P]), w("dec", [P, P]), w("enc_b", [P, P])
                wl = [w(f"wl{k}", [P, 1 if k == 0 else 2, P if k == 3 else H]) for k in range(4)]
                wr = [w(f"wr{k}", [P, 1 if k == 0 else 2, P if k == 3 else H]) for k in range(4)]
                flat = "p k m -> p (k m)"
                loads = Loads(nc, "sage", [(vec[:], inp["a_vec"]), (enc[:], inp["a_enc"]), (dec[:], inp["a_dec"]),
                                           (enc_b[:], inp["a_enc_b"].broadcast_to([P, P]))]
                           + [(wl[k][:].rearrange(flat), inp[f"a_wl{k}"]) for k in range(4)]
                           + [(wr[k][:].rearrange(flat), inp[f"a_wr{k}"]) for k in range(4)])
                loads.start()
                zero_phase(nc, "zero_c", [C[:, NP:REGION]])
                loads.await_all()
                t3 = dram("table_sage0", (NP, P))
                norm_table_phase(nc, "tab30", X, t3, ident, eps, plus=B, rhs=enc[:], bias=enc_b, clear=[A[:]])
                sources, params, encoder = [X], None, (enc[:], vec[:, 0:1])
                for k in range(4):
                    K, hidden = len(sources), k < 3
                    own = dict(sources=sources, params=params, enc=encoder, wr=[wr[k][:, j, :] for j in range(K)],
                               outs=[D, E] if hidden else [D], bias=inp_cols(vec, k, 0) if hidden else vec[:, 2:3])
                    aggs = [A, B][:K] if hidden else [A]
                    if k == 0:
                        tab = t3
                    else:
                        tab = dram(f"table_sage{k}", (NP, len(aggs) * P))
                        table_phase(nc, f"tab3{k}", sources, tab, len(aggs) * P, ident, func=ACT.Relu, params=params,
                                    rhs=None if hidden else [wl[3][:, j, :] for j in range(2)],
                                    clear=[r[:] for r in aggs])
                    edges(f"pass3{k}", "sum", tab, len(aggs) * P, aggs, own=own, inv_count=C)
                    if hidden:
                        sage_phase(nc, f"sage{k}", aggs, [wl[k][:, j, :] for j in range(K)], [D, E], chunk_halves)
                        g, b = inp_cols(vec, k, 1), inp_cols(vec, k, 2)
                        batchnorm_params_phase(nc, f"bn3{k}", [(g[:, m:m + 1], b[:, m:m + 1], scale[:, m:m + 1],
                                                                shift[:, m:m + 1]) for m in range(2)], chunk_halves, eps)
                        params = [(scale[:, m:m + 1], shift[:, m:m + 1]) for m in range(2)]
                        sources, encoder = [D, E], None
                linear_phase(nc, "dec", [([dec[:]], D), ([dec[:]], A)], [(B, vec[:, 1:2])])
            norm_table_phase(nc, "out", X, out, ident, eps, plus=B, keep=False)


def inp_cols(vec, layer, what):
    at = 3 + layer * 6 + 2 * what
    return vec[:, at:at + 2]


def host_layout(inputs):
    import numpy as np
    g = {k: np.asarray(v) for k, v in inputs.items()}
    E_PAD = TILES * P
    f32 = np.float32

    def edges(a, fill=0):
        v = np.full(E_PAD, fill, a.dtype)
        v[:N_EDGES] = a
        return v.reshape(TILES, P).T

    def stack(W):
        return W.reshape(-1, P, W.shape[1]).transpose(1, 0, 2).reshape(P, -1)

    def comp(d):
        return slice(MUL + d, P, 3)

    src, dst = g["src"], g["dst"]
    nowhere = -1
    o = {}
    x_T = np.zeros((P, NP), f32)
    x_T[:, :N_NODES] = g["x"].T
    o["x_T"] = x_T
    o["src"], o["dst"] = edges(src), edges(dst, nowhere)
    before = []
    for j in range(1, SLOTS + 1):
        b = np.full(N_EDGES, -1, dst.dtype)
        b[j:] = dst[:-j]
        before.append(edges(b, -1))
    o["dst_before"] = np.stack(before, 2).reshape(P, TILES * SLOTS)
    bases = np.zeros((1, GROUPS + 2), dst.dtype)
    firsts = dst[::GROUP_TILES * P]
    bases[0, 1:1 + len(firsts)] = firsts
    o["bases"] = bases
    after_all = 1 << 20
    base_col = np.full((2, BASE_COLS * P), after_all, dst.dtype)
    base_col[0, :len(firsts)], base_col[1, 1:len(firsts)] = firsts, firsts[:-1]
    base_col[1, 0] = -1
    o["base_cols"] = base_col.reshape(2, BASE_COLS, P).transpose(2, 0, 1).reshape(P, 2 * BASE_COLS)
    ea = np.zeros((E_PAD, 4), f32)
    ea[:N_EDGES] = g["edge_attr_4"]
    o["edge_attr"] = ea.reshape(TILES, P, 4).transpose(1, 0, 2).reshape(P, TILES * 4)
    ein = np.zeros((BASIS, (GROUPS + LOOK) * GROUP_TILES * P), f32)
    ein[:, :N_EDGES] = g["edge_attr_10"].T
    o["edge_in"] = ein
    attr = np.zeros((NP,), f32)
    attr[:N_NODES] = g["node_vec1"][:, 0]
    o["attr_row"], o["attr_col"] = attr[None, :], attr.reshape(BLOCKS, P).T

    l1, sc, l2a, l2b = (np.zeros((P, P), f32) for _ in range(4))
    l1[:MUL, :MUL], sc[:MUL, :MUL] = g["L0_gnn_W_l10"], g["L0_gnn_W_sc0"]
    l2a[:MUL, :MUL] = g["L0_gnn_W_l20"][:MUL]
    l2b[3 * MUL:, :MUL] = g["L0_gnn_W_l20"][MUL:]
    for d in range(3):
        l1[comp(d), MUL * (d + 1):MUL * (d + 2)] = g["L0_gnn_W_l11"]
        sc[comp(d), comp(d)] = g["L0_gnn_W_sc1"]
        l2a[MUL * (d + 1):MUL * (d + 2), comp(d)] = g["L0_gnn_W_l21"][MUL:]
        l2b[MUL * d:MUL * (d + 1), comp(d)] = g["L0_gnn_W_l21"][:MUL]
    o["t_l1"], o["t_sc"], o["t_l2a"], o["t_l2b"] = l1, sc, l2a, l2b
    o["t_fc1"], o["t_fc2"] = g["L0_gnn_W_fc1"], g["L0_gnn_W_fc2"]

    p = "L1_gnn_"
    att = g[p + "W_att"]
    o["g_msg"] = np.concatenate([g[p + "W_msg"], att[:P]], 1)
    o["g_bmsg"] = np.concatenate([g[p + "b_msg"], g[p + "b_att"].reshape(1)])[None, :]
    o["g_dst"] = np.repeat(att[P:], P, 1)
    o["g_ih"], o["g_hh"] = g[p + "W_ih"].T, g[p + "W_hh"].T
    o["g_vec"] = np.stack([*g[p + "b_ih"].reshape(3, P), *g[p + "b_hh"].reshape(3, P), g[p + "gamma"], g[p + "beta"]], 1)
    p = "L2_gnn_"
    for k in range(2):
        o[f"s_w{k}"], o[f"s_b{k}"] = g[p + f"W{k}"].T, g[p + f"b{k}"][None, :]
        o[f"s_vec{k}"] = np.stack([g[p + f"g{k}"], g[p + f"be{k}"], g[p + f"blank{k}"]], 1)
        o[f"s_sc{k}"] = np.concatenate([g[p + f"cw{k}"], g[p + f"cb{k}"], g[p + f"a{k}"]])[None, :]
    p = "L3_gnn_"
    o["a_enc"], o["a_dec"] = g[p + "enc_W"].T, g[p + "dec_W"].T
    for k in range(4):
        o[f"a_wl{k}"], o[f"a_wr{k}"] = stack(g[p + f"Wl{k}"].T), stack(g[p + f"Wr{k}"].T)
    v = [g[p + "enc_b"], g[p + "dec_b"], g[p + "bl3"]]
    for k in range(3):
        for n in (f"bl{k}", f"g{k}", f"b{k}"):
            v += [*g[p + n].reshape(2, P)]
    o["a_vec"] = np.stack(v, 1)
    o["a_enc_b"] = g[p + "enc_b"][None, :]

    o["win_start"] = np.tile(np.arange(WINDOWS, dtype=f32) * WIN, (P, 1))
    o["iota"] = np.tile(np.arange(WIN, dtype=f32), (P, 1))
    o["ident"] = np.eye(P, dtype=f32)
    return {k: np.ascontiguousarray(a) for k, a in o.items()}


STOP = 99


def kernel(**inputs):
    import numpy as _np
    import concourse.bacc as _bacc
    from concourse import mybir as _mybir
    from concourse.bass_utils import run_bass_kernel_spmd as _run

    nc = _bacc.Bacc("TRN2", target_bir_lowering=False, num_devices=1)
    arrays, aps = {}, {}
    for name, a in host_layout(inputs).items():
        arrays[f"in_{name}"] = a
        aps[name] = nc.dram_tensor(f"in_{name}", a.shape, _mybir.dt.from_np(a.dtype), kind="ExternalInput").ap()
    out = nc.dram_tensor("out_0", (NP, P), _mybir.dt.float32, kind="ExternalOutput").ap()
    gnn_kernel(nc, aps, out, STOP)
    r = _run(nc, [arrays], core_ids=[0])
    return _np.asarray(r.results[0]["out_0"])[:N_NODES]
```

```python
import math
from contextlib import ExitStack

import concourse.bass as bass
from concourse import mybir

F32 = mybir.dt.float32
I32 = mybir.dt.int32
ALU = mybir.AluOpType
ACT = mybir.ActivationFunctionType
DVE_E = mybir.EngineType.DVE
PE_E = mybir.EngineType.PE

P = 128
N_NODES = 6250
N_EDGES = 100000
BLOCKS = -(-N_NODES // P)
NP = BLOCKS * P
GROUP_TILES = 4
RING = 4
GROUPS = 196
TILES = GROUPS * GROUP_TILES
ITERS = GROUPS // RING
WIN = 128
REGION = 6400
CHUNK = 448
CHUNKS = NP // CHUNK
MUL = 32
HID = 100
BASIS = 10
SLOTS = 4
EPS = 1e-5
WINDOWS = NP // WIN
BASE_COLS = -(-GROUPS // P)
LOOK = 2
assert ITERS == BLOCKS and TILES * P >= N_EDGES and REGION >= N_NODES + WIN and CHUNK * CHUNKS == NP


def holds_back(value):
    return not isinstance(value, int) or value > 0


def looped(eng, count, body):
    body(0)
    if count > 1:
        with eng.Fori(1, count) as i:
            body(i)


def looped_pairs(eng, count, body):
    for i in range(3):
        body(i, i % 2)
    with eng.Fori(1, (count - 1) // 2) as j:
        body(j * 2 + 1, 1)
        body(j * 2 + 2, 0)


def looped_but_last(eng, count, body):
    looped(eng, count - 1, body)
    body(count - 1)


def chunk_stats(nc, stats, region, chunk):
    width = min(CHUNK, N_NODES - chunk * CHUNK) if isinstance(chunk, int) else CHUNK
    return nc.vector.bn_stats(cols(stats, chunk * 6, 6), cols(region, chunk * CHUNK, width))


class Scope:
    BANKS = (100, 170)
    turn = 0

    def __init__(self, nc, name):
        self.nc, self.name, self.stack, self.sems = nc, name, ExitStack(), []
        self.first = Scope.BANKS[Scope.turn]
        Scope.turn = 1 - Scope.turn

    def __enter__(self):
        return self

    def __exit__(self, *a):
        self.stack.__exit__(*a)
        if self.sems:
            self.nc.gpsimd.sem_clear(range(self.first, self.first + len(self.sems)))
            for sem in self.sems:
                self.nc.release_semaphore(sem)

    def sb(self, name, shape, dt=F32):
        return self.stack.enter_context(self.nc.sbuf_tensor(f"{self.name}_{name}", shape, dt))

    def ps(self, name, shape):
        return self.stack.enter_context(self.nc.psum_tensor(f"{self.name}_{name}_ps", shape, F32))

    def sem(self, name):
        self.sems.append(self.nc.alloc_semaphore(f"{self.name}_{name}", self.first + len(self.sems)))
        return self.sems[-1]

    def block(self):
        return self.stack.enter_context(self.nc.Block())


class Gathers:

    def __init__(self, nc, slots):
        self.sems = [nc.alloc_semaphore(f"gathered{k}", 240 + k) for k in range(slots)]
        self.base = [0] * slots

    def count(self, k, tiles):
        return 16 * tiles + self.base[k]

    def end_phase(self, slots, tiles):
        for k in range(slots):
            self.base[k] += 16 * tiles


def cols(region, start, width):
    return region[:, bass.ds(start, width)]


class Loads:
    count = 0

    def __init__(self, nc, name, pairs):
        self.nc, self.name, self.pairs = nc, name, pairs
        self.loaded = nc.alloc_semaphore(f"{name}_loaded", (247, 248, 249, 251, 252, 253, 254)[Loads.count])
        Loads.count += 1

    def start(self):
        with Scope(self.nc, self.name + "_start") as s:
            block = s.block()

            @block.sync
            def _(sp):
                for dst, src in self.pairs:
                    sp.dma_start(dst, src).then_inc(self.loaded, 16)

    def await_all(self):
        with Scope(self.nc, self.name + "_await") as s:
            block = s.block()

            @block.sync
            def _(sp):
                sp.wait_ge(self.loaded, 16 * len(self.pairs))


def table_phase(nc, name, sources, table, ident, func=None, params=None, rhs=None, row_scale=None, clear=()):
    K = len(sources)
    SUB = 7
    W, count = SUB * P, BLOCKS // SUB
    width = K * P if rhs is None else rhs[0].shape[-1]
    with Scope(nc, name) as s:
        stage = s.sb("stage", [P, 2, K, W])
        rows = s.sb("rows", [P, 2, SUB, width])
        turned = s.ps("turned", [P, 2, -(-SUB * width // 512) * 512])
        staged, flipped, evacuated = s.sem("staged"), s.sem("flipped"), s.sem("evacuated")
        stored = [s.sem(f"stored{c}") for c in range(2)]
        block = s.block()

        @block.gpsimd
        def _(pool):
            for region in clear:
                nc.gpsimd.memset(region, 0.0)

        @block.scalar
        def _(act):
            def body(i, c):
                if holds_back(i - 1):
                    act.wait_ge(flipped, i - 1)
                for k in range(K):
                    src = cols(sources[k], i * W, W)
                    if params is None:
                        ins = nc.scalar.activation(stage[:, c, k, :], src, ACT.Identity)
                    else:
                        scale, shift = params[k]
                        ins = nc.scalar.activation(stage[:, c, k, :], src, func, bias=shift, scale=scale)
                ins.then_inc(staged, 1)
            looped_pairs(act, count, body)

        @block.tensor
        def _(pe):
            def body(i, c):
                if holds_back(i - 1):
                    pe.wait_ge(evacuated, i - 1)
                pe.wait_ge(staged, i + 1)
                for b in range(SUB):
                    for k in range(K):
                        nodes = stage[:, c, k, b * P:(b + 1) * P]
                        if rhs is None:
                            at = (b * K + k) * P
                            ins = nc.tensor.transpose(turned[:, c, at:at + P], nodes, ident[:])
                        else:
                            ins = nc.tensor.matmul(turned[:, c, b * width:(b + 1) * width], nodes, rhs[k],
                                                   start=(k == 0), stop=(k == K - 1))
                ins.then_inc(flipped, 1)
            looped_pairs(pe, count, body)

        @block.vector
        def _(dve):
            def body(i, c):
                if holds_back(i - 1):
                    dve.wait_ge(stored[c], (i - c) * 8)
                dve.wait_ge(flipped, i + 1)
                found = turned[:, c, 0:SUB * width]
                if row_scale is None:
                    ins = nc.vector.tensor_copy(rows[:, c, :, :].rearrange("p b f -> p (b f)"), found)
                else:
                    ins = nc.vector.tensor_tensor(rows[:, c, :, :], found.rearrange("p (b f) -> p b f", f=width),
                                                  cols(row_scale, i * SUB, SUB).unsqueeze(2).broadcast_to([P, SUB, width]),
                                                  ALU.mult)
                ins.then_inc(evacuated, 1)
            looped_pairs(dve, count, body)

        @block.sync
        def _(sp):
            def body(i, c):
                sp.wait_ge(evacuated, i + 1)
                sp.dma_start(table[bass.ds(i * W, W), :].rearrange("(b p) f -> p b f", p=P), rows[:, c, :, :])\
                    .then_inc(stored[c], 16)
            looped_pairs(sp, count, body)
            for c in range(2):
                sp.wait_ge(stored[c], 16 * ((count + 1 - c) // 2))


def norm_table_phase(nc, name, X, table, ident, eps, plus=None, normed_by=None, rhs=None, bias=None, keep=True,
                     clear=()):
    SUB = 7
    W = SUB * P
    count = BLOCKS // SUB
    with Scope(nc, name) as s:
        stage = s.sb("stage", [P, 2, W])
        stats, mv = s.sb("stats", [P, 2, SUB, 6]), s.sb("mv", [P, 2, SUB, 2])
        sd, rs, nm = s.sb("sd", [P, 2, SUB]), s.sb("rs", [P, 2, SUB]), s.sb("nm", [P, 2, SUB])
        rows = s.sb("rows", [P, 2, SUB, P])
        turned, back = s.ps("turned", [P, 2, 1024]), s.ps("back", [P, 1024])
        staged, flipped, counted, aggregated = s.sem("staged"), s.sem("flipped"), s.sem("counted"), s.sem("aggregated")
        rooted, inverted, factored = s.sem("rooted"), s.sem("inverted"), s.sem("factored")
        normed, flipped_back, restored = s.sem("normed"), s.sem("flipped_back"), s.sem("restored")
        tick, tick_act = s.sem("tick"), s.sem("tick_act")
        stored = [s.sem(f"stored{b}") for b in range(2)]
        if normed_by is not None:
            addend, addend_made = s.sb("addend", [P, 2, W]), s.sem("addend_made")
        if rhs is not None:
            width = rhs.shape[-1]
            again = s.sb("again", [P, 2, W])
            product = s.ps("product", [P, 1024])
            rows_out = s.sb("rows_out", [P, 2, SUB, width])
            copied, multiplied, evacuated = s.sem("copied"), s.sem("multiplied"), s.sem("evacuated")
        else:
            rows_out = rows
        block = s.block()

        @block.gpsimd
        def _(pool):
            def add(i, c):
                if holds_back(i - 1):
                    pool.wait_ge(flipped, i - 1)
                if normed_by is not None:
                    pool.wait_ge(addend_made, i + 1)
                if plus is None:
                    ins = nc.gpsimd.tensor_copy(stage[:, c, :], cols(X, i * W, W))
                else:
                    other = cols(plus, i * W, W) if normed_by is None else addend[:, c, :]
                    ins = nc.gpsimd.tensor_tensor(stage[:, c, :], cols(X, i * W, W), other, ALU.add)
                ins.then_inc(staged, 1)
            looped_pairs(pool, count, add)
            for region in clear:
                nc.gpsimd.memset(region, 0.0)

        @block.scalar
        def _(act):
            def scaled_addend(i, c):
                if holds_back(i - 1):
                    act.wait_ge(staged, i - 1)
                    act.sem_inc(tick_act, 1)
                nc.scalar.activation(addend[:, c, :], cols(plus, i * W, W), ACT.Identity, bias=normed_by[1],
                                     scale=normed_by[0]).then_inc(addend_made, 1)

            def copy_to_x(i, c):
                act.wait_ge(restored, i + 1)
                act.sem_inc(tick_act, 1)
                nc.scalar.activation(cols(X, i * W, W), again[:, c, :], ACT.Identity).then_inc(copied, 1)

            def normalise(i, c):
                if rhs is not None and holds_back(i - 1):
                    copy_to_x(i - 2, c)
                act.wait_ge(aggregated, i + 1)
                nc.scalar.activation(sd[:, c, :], mv[:, c, :, 1], ACT.Sqrt, bias=eps[:, 0:1]).then_inc(rooted, 1)
                if holds_back(i - 1):
                    if keep:
                        act.wait_ge(flipped_back, i - 1)
                    if rhs is None:
                        act.wait_ge(stored[c], (i - c) * 8)
                act.wait_ge(factored, i + 1)
                for b in range(SUB):
                    ins = nc.scalar.activation(rows[:, c, b, :], turned[:, c, b * P:(b + 1) * P], ACT.Identity,
                                               bias=nm[:, c, b:b + 1], scale=rs[:, c, b:b + 1])
                ins.then_inc(normed, 1)

            def body(i, c):
                if normed_by is None:
                    normalise(i, c)
                else:
                    scaled_addend(i, c)
                    if holds_back(i - 1):
                        normalise(i - 2, c)
            looped_pairs(act, count, body)
            for i in range(count - 2 if normed_by is not None else count, count):
                normalise(i, i % 2)
            for i in range(count - 2 if rhs is not None else count, count):
                copy_to_x(i, i % 2)

        @block.tensor
        def _(pe):
            def turn(i, c):
                if holds_back(i - 1):
                    pe.wait_ge(normed, i - 1)
                pe.wait_ge(staged, i + 1)
                for b in range(SUB):
                    ins = nc.tensor.transpose(turned[:, c, b * P:(b + 1) * P], stage[:, c, b * P:(b + 1) * P], ident[:])
                ins.then_inc(flipped, 1)

            def turn_back(i, c):
                if holds_back(i):
                    pe.wait_ge(restored, i)
                pe.wait_ge(normed, i + 1)
                for b in range(SUB):
                    ins = nc.tensor.transpose(back[:, b * P:(b + 1) * P], rows[:, c, b, :], ident[:])
                ins.then_inc(flipped_back, 1)

            def multiply(i, c):
                if holds_back(i):
                    pe.wait_ge(evacuated, i)
                pe.wait_ge(restored, i + 1)
                for b in range(SUB):
                    nodes = again[:, c, b * P:(b + 1) * P]
                    ins = nc.tensor.matmul(product[:, b * P:(b + 1) * P], nodes, rhs[:, 0:P], start=True, stop=True)
                    if width > P:
                        ins = nc.tensor.matmul(product[:, W + b:W + b + 1], nodes, rhs[:, P:P + 1],
                                               start=True, stop=True)
                ins.then_inc(multiplied, 1)

            def body(i, c):
                turn(i, c)
                if keep and holds_back(i):
                    turn_back(i - 1, 1 - c)
                if rhs is not None and holds_back(i - 1):
                    multiply(i - 2, c)
            looped_pairs(pe, count, body)
            last = (count - 1) % 2
            if rhs is not None:
                multiply(count - 2, 1 - last)
            if keep:
                turn_back(count - 1, last)
            if rhs is not None:
                multiply(count - 1, last)

        @block.vector
        def _(dve):
            def restore(i, c):
                dve.wait_ge(flipped_back, i + 1)
                if rhs is None:
                    nc.vector.tensor_copy(cols(X, i * W, W), back[:, 0:W]).then_inc(restored, 1)
                    return
                if holds_back(i - 1):
                    dve.wait_ge(copied, i - 1)
                    dve.wait_ge(multiplied, i - 1)
                nc.vector.tensor_copy(again[:, c, :], back[:, 0:W]).then_inc(restored, 1)

            def evacuate(i, c):
                dve.wait_ge(multiplied, i + 1)
                if holds_back(i - 1):
                    dve.wait_ge(stored[c], (i - c) * 8)
                ins = nc.vector.tensor_tensor(rows_out[:, c, :, 0:P], product[:, 0:W].rearrange("p (b f) -> p b f", f=P),
                                              bias[:, 0:P].unsqueeze(1).broadcast_to([P, SUB, P]), ALU.add)
                if width > P:
                    ins = nc.vector.tensor_tensor(rows_out[:, c, :, P], product[:, W:W + SUB],
                                                  bias[:, P:P + 1].broadcast_to([P, SUB]), ALU.add)
                ins.then_inc(evacuated, 1)

            def body(i, c):
                dve.wait_ge(flipped, i + 1)
                for b in range(SUB):
                    ins = nc.vector.bn_stats(stats[:, c, b, :], turned[:, c, b * P:(b + 1) * P])
                ins.then_inc(counted, 1)
                dve.wait_ge(counted, i + 1)
                dve.sem_inc(tick, 1)
                for b in range(SUB):
                    ins = nc.vector.bn_aggr(mv[:, c, b, :], stats[:, c, b, :])
                ins.then_inc(aggregated, 1)
                dve.wait_ge(rooted, i + 1)
                if holds_back(i - 1):
                    dve.wait_ge(normed, i - 1)
                nc.vector.reciprocal(rs[:, c, :], sd[:, c, :]).then_inc(inverted, 1)
                dve.wait_ge(inverted, i + 1)
                nc.vector.scalar_tensor_tensor(nm[:, c, :], mv[:, c, :, 0], -1.0, rs[:, c, :],
                                               ALU.mult, ALU.mult).then_inc(factored, 1)
                if keep and holds_back(i):
                    restore(i - 1, 1 - c)
                if rhs is not None and holds_back(i - 1):
                    evacuate(i - 2, c)
            looped_pairs(dve, count, body)
            last = (count - 1) % 2
            if rhs is not None:
                evacuate(count - 2, 1 - last)
            if keep:
                restore(count - 1, last)
            if rhs is not None:
                evacuate(count - 1, last)

        @block.sync
        def _(sp):
            def body(i, c):
                sp.wait_ge(normed if rhs is None else evacuated, i + 1)
                sp.dma_start(table[bass.ds(i * W, W), :].rearrange("(b p) f -> p b f", p=P), rows_out[:, c, :, :])\
                    .then_inc(stored[c], 16)
            looped_pairs(sp, count, body)
            for c in range(2):
                sp.wait_ge(stored[c], 16 * ((count + 1 - c) // 2))


def batchnorm_params_phase(nc, name, items, stats, eps):
    with Scope(nc, name) as s:
        K = len(items)
        mv, sd, rs, ms = s.sb("mv", [P, K, 2]), s.sb("sd", [P, K]), s.sb("rs", [P, K]), s.sb("ms", [P, K])
        aggregated, rooted, step = s.sem("aggregated"), s.sem("rooted"), s.sem("step")
        block = s.block()

        @block.vector
        def _(dve):
            for k in range(K):
                nc.vector.bn_aggr(mv[:, k, :], stats[k]).then_inc(aggregated, 1)
            for k, (gamma, beta, scale, shift) in enumerate(items):
                dve.wait_ge(rooted, k + 1)
                nc.vector.reciprocal(rs[:, k:k + 1], sd[:, k:k + 1]).then_inc(step, 1)
                dve.wait_ge(step, 3 * k + 1)
                nc.vector.tensor_tensor(scale, rs[:, k:k + 1], gamma, ALU.mult).then_inc(step, 1)
                dve.wait_ge(step, 3 * k + 2)
                nc.vector.tensor_tensor(ms[:, k:k + 1], mv[:, k, 0:1], scale, ALU.mult).then_inc(step, 1)
                dve.wait_ge(step, 3 * k + 3)
                nc.vector.tensor_tensor(shift, beta, ms[:, k:k + 1], ALU.subtract)

        @block.scalar
        def _(act):
            for k in range(K):
                act.wait_ge(aggregated, k + 1)
                nc.scalar.activation(sd[:, k:k + 1], mv[:, k, 1:2], ACT.Sqrt, bias=eps[:, 0:1]).then_inc(rooted, 1)


def add_normed_phase(nc, name, out, base, H, scale, shift):
    cuts = [0, NP // 2, NP]
    with Scope(nc, name) as s:
        normed, done = s.sem("normed"), s.sem("done")
        block = s.block()

        @block.scalar
        def _(act):
            for a, b in zip(cuts, cuts[1:]):
                nc.scalar.activation(H[:, a:b], H[:, a:b], ACT.Identity, bias=shift, scale=scale).then_inc(normed, 1)

        @block.vector
        def _(dve):
            for j, (a, b) in enumerate(zip(cuts, cuts[1:])):
                dve.wait_ge(normed, j + 1)
                nc.vector.tensor_tensor(out[:, a:b], base[:, a:b], H[:, a:b], ALU.add).then_inc(done, 1)


def zero_phase(nc, name, regions):
    with Scope(nc, name) as s:
        block = s.block()

        @block.vector
        def _(dve):
            for r in regions:
                nc.vector.memset(r, 0.0)


class TensorMath:

    def __init__(self, nc, T, w, y, y_ea0, ea, y_ea1, w2_y0, dot, prod_a, prod_b):
        by_channel = "p t (c u) -> p t c u"
        self.nc, self.by3, self.w2_y0, self.dot, self.y_ea1 = nc, [P, T, 3, MUL], w2_y0, dot, y_ea1
        self.w = w.rearrange("p (t c u) -> p t c u", c=4, u=MUL)
        self.y, self.y_ea0 = y.rearrange(by_channel, u=MUL), y_ea0.rearrange(by_channel, u=MUL)
        self.a, self.b = prod_a.rearrange(by_channel, u=MUL), prod_b.rearrange(by_channel, u=MUL)
        self.ea1 = ea.rearrange("p (t x) -> p t x", x=4)[:, :, 1:4].unsqueeze(3).broadcast_to(self.by3)

    def mult(self, out, a, b):
        return self.nc.vector.tensor_tensor(out, a, b, ALU.mult)

    def y1_times_ea1(self):
        return self.mult(self.y_ea1, self.y[:, :, 1:4, :], self.ea1)

    def y0_weighed(self):
        return self.mult(self.w2_y0, self.w[:, :, 1, :], self.y[:, :, 0, :])

    def dot_first(self):
        return self.nc.vector.tensor_tensor(self.dot[:, :, 0, :], self.y_ea1[:, :, 0, :], self.y_ea1[:, :, 1, :], ALU.add)

    def dot_second(self):
        return self.nc.vector.tensor_tensor(self.dot[:, :, 1, :], self.dot[:, :, 0, :], self.y_ea1[:, :, 2, :], ALU.add)

    def a_scalars(self):
        return self.mult(self.a[:, :, 0, :], self.w[:, :, 0, :], self.y_ea0[:, :, 0, :])

    def a_vectors(self):
        return self.mult(self.a[:, :, 1:4, :], self.w[:, :, 2:3, :].broadcast_to(self.by3), self.y_ea0[:, :, 1:4, :])

    def b_vectors(self):
        return self.mult(self.b[:, :, 0:3, :], self.w2_y0.unsqueeze(2).broadcast_to(self.by3), self.ea1)

    def b_scalars(self):
        return self.mult(self.b[:, :, 3, :], self.w[:, :, 3, :], self.dot[:, :, 1, :])


class SlotMath:

    def __init__(self, nc, T, extra, group, reaches, rank, slot_in):
        by_tile, shape = "p (t s) -> p t s", [P, T, SLOTS]
        self.nc, self.reaches, self.rank, self.slot_in = nc, reaches, rank, slot_in
        self.before = cols(extra["dst_before"], group * (T * SLOTS), T * SLOTS).rearrange(by_tile, s=SLOTS)
        self.dst = cols(extra["dst"], group * T, T).unsqueeze(2).broadcast_to(shape)
        self.src = cols(extra["src"], group * T, T).unsqueeze(2).broadcast_to(shape)

    def reach(self):
        return self.nc.vector.tensor_tensor(self.reaches[:, :, 1:SLOTS + 1], self.before, self.dst, ALU.is_equal)

    def rank_edges(self):
        return self.nc.vector.tensor_tensor(self.rank, self.reaches[:, :, 0:SLOTS], self.reaches[:, :, 1:SLOTS + 1],
                                            ALU.subtract)

    def place_sources(self):
        return self.nc.vector.tensor_tensor(self.slot_in[:, :, 0:SLOTS], self.rank, self.src, ALU.mult)


def edge_pass(nc, gathers, name, kind, table, width, src_dram, rel, iota, bases, aggs, extra):
    tensor, gate, plain = kind == "tensor", kind == "gate", kind == "sum"
    A = 1 if gate else 2 if tensor else width // P
    with Scope(nc, name) as s:
        idx = s.sb("idx", [P, RING, GROUP_TILES], I32)
        rows = s.sb("rows", [P, RING, GROUP_TILES, width])
        hot = s.sb("hot", [P, 2, GROUP_TILES, WIN])
        sums = [s.ps(f"sums{a}", [P, 2, 512]) for a in range(A)]
        idx_loaded = [s.sem(f"idx_loaded{h}") for h in range(RING)]
        gathered = gathers.sems
        tick = s.sem("tick")
        hot_made, operands_made = s.sem("hot_made"), s.sem("operands_made")
        summed, added = s.sem("summed"), s.sem("added")
        if tensor:
            edge_in = s.sb("edge_in", [BASIS, 4, GROUP_TILES * P])
            hidden = s.sb("hidden", [HID, 2, GROUP_TILES * P])
            y_ea0, y_ea1 = s.sb("y_ea0", [P, 2, GROUP_TILES, P]), s.sb("y_ea1", [P, GROUP_TILES, 3, MUL])
            w2_y0, dot = s.sb("w2_y0", [P, GROUP_TILES, MUL]), s.sb("dot", [P, GROUP_TILES, 2, MUL])
            prod_a, prod_b = s.sb("prod_a", [P, 2, GROUP_TILES, P]), s.sb("prod_b", [P, 2, GROUP_TILES, P])
            ea0_made, step, dotted = s.sem("ea0_made"), s.sem("step"), s.sem("dotted")
            hidden_ps, weight_ps = s.ps("hidden", [P, 2, 512]), s.ps("weight", [P, 2, 512])
            edge_in_loaded = [s.sem(f"edge_in_loaded{h}") for h in range(4)]
            hidden_summed, hidden_made, weight_made = s.sem("hidden_summed"), s.sem("hidden_made"), s.sem("weight_made")
        if gate:
            sig = s.sb("sig", [P, 2, GROUP_TILES, WIN])
            hot_sig = s.sb("hot_sig", [P, 2, GROUP_TILES, WIN])
            slot_in = s.sb("slot_in", [P, 2, GROUP_TILES, SLOTS + 1])
            reaches, rank = s.sb("reaches", [P, 2, GROUP_TILES, SLOTS + 1]), s.sb("rank", [P, GROUP_TILES, SLOTS])
            at_ps = s.ps("at", [P, 2, 512])
            slot_ps = s.ps("slot", [P, 2, 512])
            sig_made, at_made = s.sem("sig_made"), s.sem("at_made")
            own_ps, own_tick = s.ps("own", [P, 512]), s.sem("own_tick")
            own_summed, own_stored = s.sem("own_summed"), s.sem("own_stored")
            filled, reached, ranked = s.sem("filled"), s.sem("reached"), s.sem("ranked")
        if plain:
            own = extra["own"]
            scaled_sums, scaled = s.sb("scaled_sums", [P, A, WIN]), s.sem("scaled")
            z_block = s.sb("z_block", [P, len(own["sources"]), P])
            own_ps, encoded_ps = s.ps("own", [P, 512]), s.ps("encoded", [P, 512])
            own_tick = s.sem("own_tick")
            z_encoded, z_made, own_summed, own_added = (s.sem("z_encoded"), s.sem("z_made"), s.sem("own_summed"),
                                                        s.sem("own_added"))
        n_acc = A + (1 if gate else 0)
        block = s.block()

        @block.sync
        def _(sp):
            if tensor:
                for q in range(LOOK):
                    sp.dma_start(edge_in[:, q, :], extra["edge_in"][:, q * 512:(q + 1) * 512])\
                        .then_inc(edge_in_loaded[q], 16)

            def body(i):
                for h in range(RING):
                    q = i * RING + h
                    if holds_back(q - RING + 1):
                        sp.wait_ge(summed, q - RING + 1)
                    sp.dma_start(idx[:, h, :], cols(src_dram, q * GROUP_TILES, GROUP_TILES)).then_inc(idx_loaded[h], 16)
                    if tensor:
                        r = (h + LOOK) % 4
                        if holds_back(q + LOOK - 4 + 1):
                            sp.wait_ge(hidden_summed, q + LOOK - 4 + 1)
                        sp.dma_start(edge_in[:, r, :], cols(extra["edge_in"], (q + LOOK) * 512, 512))\
                            .then_inc(edge_in_loaded[r], 16)
            looped(sp, ITERS, body)
            if tensor:
                for r in range(4):
                    sp.wait_ge(edge_in_loaded[r], 16 * (ITERS + (r < LOOK)))

        @block.gpsimd
        def _(pool):
            def body(i):
                for h in range(RING):
                    q = i * RING + h
                    if holds_back(q - RING + 1):
                        pool.wait_ge(summed, q - RING + 1)
                    pool.wait_ge(idx_loaded[h], 16 * i + 16)
                    pool.sem_inc(tick, 1)
                    for t in range(GROUP_TILES):
                        nc.gpsimd.indirect_dma_start(
                            rows[:, h, t, :], None, table, bass.IndirectOffsetOnAxis(ap=idx[:, h, t:t + 1], axis=0)
                        ).then_inc(gathered[h], 16)
            looped(pool, ITERS, body)

        def load_bases(engine, at, count):
            _, values = nc.values_load_multi_w_load_instructions(
                bases[0:1, bass.ds(at, count)], engines=[engine], min_val=0, max_val=N_NODES - 1,
                skip_runtime_bounds_check_because="bases are nodes: 0 to N_NODES - 1")
            return values

        @block.scalar
        def _(act):
            if tensor:
                def silu(q, r):
                    if holds_back(q - 1):
                        act.wait_ge(weight_made, q - 1)
                    act.wait_ge(hidden_summed, q + 1)
                    nc.scalar.activation(hidden[:, r, :], hidden_ps[0:HID, r, :], ACT.Silu,
                                         scale=1.0 / math.sqrt(BASIS)).then_inc(hidden_made, 1)
                silu(0, 0)

                def body(i):
                    for h in range(RING):
                        q, r = i * RING + h, h % 2
                        silu(q + 1, (h + 1) % 2)
                        if holds_back(q - 1):
                            act.wait_ge(operands_made, q - 1)
                        act.wait_ge(gathered[h], gathers.count(h, GROUP_TILES * (i + 1)))
                        for t in range(GROUP_TILES):
                            ins = nc.scalar.activation(y_ea0[:, r, t, :], rows[:, h, t, :], ACT.Copy,
                                                       scale=cols(extra["edge_attr"], (q * GROUP_TILES + t) * 4, 1))
                        ins.then_inc(ea0_made, 1)
                looped(act, ITERS, body)
            if plain:
                def body(i):
                    if holds_back(i):
                        act.wait_ge(own_summed, i)
                        act.sem_inc(own_tick, 1)
                    for k, source in enumerate(own["sources"]):
                        if own["enc"] is not None:
                            act.wait_ge(z_encoded, i + 1)
                            ins = nc.scalar.activation(z_block[:, k, :], encoded_ps[:, 0:P], ACT.Identity,
                                                       bias=own["enc"][1])
                        else:
                            scale, shift = own["params"][k]
                            ins = nc.scalar.activation(z_block[:, k, :], cols(source, i * P, P), ACT.Relu,
                                                       bias=shift, scale=scale)
                    ins.then_inc(z_made, 1)
                looped(act, BLOCKS, body)
            if gate:
                def body(i):
                    for h in range(RING):
                        q, r = i * RING + h, h % 2
                        act.wait_ge(at_made, q + 1)
                        if holds_back(q - 1):
                            act.wait_ge(operands_made, q - 1)
                        act.wait_ge(gathered[h], gathers.count(h, GROUP_TILES * (i + 1)))
                        for t in range(GROUP_TILES):
                            ins = nc.scalar.activation(sig[:, r, t, :], at_ps[:, r, 0:WIN], ACT.Sigmoid,
                                                       bias=rows[:, h, t, P:P + 1])
                        ins.then_inc(sig_made, 1)
                    act.wait_ge(own_summed, i + 1)
                    act.sem_inc(own_tick, 1)
                    for m, (_, out, bias) in enumerate(extra["own"]):
                        ins = nc.scalar.activation(cols(out, i * P, P), own_ps[:, m * P:(m + 1) * P], ACT.Identity, bias=bias)
                    ins.then_inc(own_stored, 1)
                looped(act, ITERS, body)

        @block.tensor
        def _(pe):
            def hidden_layer(i, q, r4):
                if holds_back(q - 1):
                    pe.wait_ge(hidden_made, q - 1)
                pe.wait_ge(edge_in_loaded[r4], 16 * i + 16)
                nc.tensor.matmul(hidden_ps[0:HID, r4 % 2, :], extra["w_fc1"], edge_in[:, r4, :],
                                 start=True, stop=True).then_inc(hidden_summed, 1)

            def weights(q, r):
                if holds_back(q - 1):
                    pe.wait_ge(operands_made, q - 1)
                pe.wait_ge(hidden_made, q + 1)
                for t in range(GROUP_TILES):
                    ins = nc.tensor.matmul(weight_ps[:, r, t * P:(t + 1) * P], hidden[:, r, t * P:(t + 1) * P],
                                           extra["w_fc2"], start=True, stop=True)
                ins.then_inc(weight_made, 1)

            def at_dst(q, r, base):
                if holds_back(q - 1):
                    pe.wait_ge(sig_made, q - 1)
                nc.tensor.matmul(at_ps[:, r, 0:WIN], extra["w_dst"], cols(extra["x"], base, WIN),
                                 start=True, stop=True).then_inc(at_made, 1)

            if gate:
                at_dst(0, 0, load_bases(PE_E, 1, 1)[0])
            if tensor:
                hidden_layer(0, 0, 0)
                hidden_layer(0, 1, 1)
                weights(0, 0)

            def own_term(i, h):
                if h == 1 and own["enc"] is not None:
                    if holds_back(i):
                        pe.wait_ge(z_made, i)
                    nc.tensor.matmul(encoded_ps[:, 0:P], own["enc"][0], cols(own["sources"][0], i * P, P),
                                     start=True, stop=True).then_inc(z_encoded, 1)
                if h == 3:
                    if holds_back(i):
                        pe.wait_ge(own_added, i)
                    pe.wait_ge(z_made, i + 1)
                    K = len(own["sources"])
                    for m in range(len(own["outs"])):
                        for k in range(K):
                            ins = nc.tensor.matmul(own_ps[:, m * P:(m + 1) * P], own["wr"][k][:, m * P:(m + 1) * P],
                                                   z_block[:, k, :], start=(k == 0), stop=(k == K - 1))
                    ins.then_inc(own_summed, 1)

            def body(i):
                if gate:
                    ahead = load_bases(PE_E, i * RING + 2, RING)
                for h in range(RING):
                    q, r = i * RING + h, h % 2
                    if plain:
                        own_term(i, h)
                    if gate:
                        at_dst(q + 1, (h + 1) % 2, ahead[h])
                    if gate and h == 3:
                        if holds_back(i):
                            pe.wait_ge(own_stored, i)
                        for m, (lhsT, _, _) in enumerate(extra["own"]):
                            ins = nc.tensor.matmul(own_ps[:, m * P:(m + 1) * P], lhsT, cols(extra["x"], i * P, P),
                                                   start=True, stop=True)
                        ins.then_inc(own_summed, 1)
                    if tensor:
                        r4 = (h + LOOK) % 4
                        hidden_layer(i + (1 if h + LOOK >= 4 else 0), q + LOOK, r4)
                        weights(q + 1, (h + 1) % 2)
                    if holds_back((q - 1) * n_acc):
                        pe.wait_ge(added, (q - 1) * n_acc)
                    if not plain:
                        pe.wait_ge(operands_made, q + 1)
                    else:
                        pe.wait_ge(hot_made, q + 1)
                        pe.wait_ge(gathered[h], gathers.count(h, GROUP_TILES * (i + 1)))
                    for t in range(GROUP_TILES):
                        first, last = t == 0, t == GROUP_TILES - 1
                        if plain:
                            for a in range(A):
                                ins = nc.tensor.matmul(sums[a][:, r, 0:WIN], rows[:, h, t, a * P:(a + 1) * P],
                                                       hot[:, r, t, :], start=first, stop=last)
                        elif gate:
                            nc.tensor.matmul(sums[0][:, r, 0:WIN], rows[:, h, t, 0:P], hot_sig[:, r, t, :],
                                             start=first, stop=last)
                            ins = nc.tensor.matmul(slot_ps[0:SLOTS + 1, r, 0:WIN], slot_in[:, r, t, :],
                                                   hot[:, r, t, :], start=first, stop=last)
                        else:
                            nc.tensor.matmul(sums[0][:, r, 0:WIN], prod_a[:, r, t, :], hot[:, r, t, :],
                                             start=first, stop=last)
                            ins = nc.tensor.matmul(sums[1][:, r, 0:WIN], prod_b[:, r, t, :], hot[:, r, t, :],
                                                   start=first, stop=last)
                    ins.then_inc(summed, 1)
            looped(pe, ITERS, body)

        @block.vector
        def _(dve):
            targets = [(sums[a], P, aggs[a]) for a in range(A)]
            if gate:
                targets.append((slot_ps, SLOTS + 1, extra["slot_sums"]))

            def add_up(q, r, start):
                dve.wait_ge(summed, q + 1)
                if holds_back(q * n_acc):
                    dve.wait_ge(added, q * n_acc)
                if plain:
                    for a in range(A):
                        ins = nc.vector.tensor_tensor(scaled_sums[:, a, :], sums[a][:, r, 0:WIN],
                                                      cols(extra["inv_count"], start, WIN), ALU.mult)
                    ins.then_inc(scaled, 1)
                    dve.wait_ge(scaled, q + 1)
                for a, (ps, rws, region) in enumerate(targets):
                    into = region[0:rws, bass.ds(start, WIN)]
                    term = scaled_sums[:, a, :] if plain else ps[0:rws, r, 0:WIN]
                    nc.vector.tensor_tensor(into, into, term, ALU.add).then_inc(added, 1)

            def add_own(block, groups):
                dve.wait_ge(own_summed, block + 1)
                dve.wait_ge(added, groups * n_acc)
                for m, out in enumerate(own["outs"]):
                    into = cols(out, block * P, P)
                    ins = nc.vector.scalar_tensor_tensor(into, own_ps[:, m * P:(m + 1) * P], own["bias"][:, m:m + 1],
                                                         into, ALU.add, ALU.add)
                ins.then_inc(own_added, 1)

            def operands(i, h):
                q, r = i * RING + h, h % 2
                if holds_back(q - 1):
                    dve.wait_ge(summed, q - 1)
                shape = [P, GROUP_TILES, WIN]
                destinations = cols(rel, q * GROUP_TILES, GROUP_TILES).unsqueeze(2).broadcast_to(shape)
                nc.vector.tensor_tensor(hot[:, r, :, :], iota[:].unsqueeze(1).broadcast_to(shape), destinations,
                                        ALU.is_equal).then_inc(hot_made, 1)
                if gate:
                    slot_math = SlotMath(nc, GROUP_TILES, extra, q, reaches[:, r, :, :], rank[:], slot_in[:, r, :, :])
                    slot_math.reach().then_inc(reached, 1)
                    dve.wait_ge(reached, q + 1)
                    slot_math.rank_edges().then_inc(ranked, 1)
                    dve.wait_ge(ranked, q + 1)
                    slot_math.place_sources()
                    dve.wait_ge(hot_made, q + 1)
                    dve.wait_ge(sig_made, q + 1)
                    nc.vector.tensor_tensor(hot_sig[:, r, :, :], hot[:, r, :, :], sig[:, r, :, :],
                                            ALU.mult).then_inc(operands_made, 1)
                if tensor:
                    m = TensorMath(nc, GROUP_TILES, weight_ps[:, r, :], rows[:, h, :, :], y_ea0[:, r, :, :],
                                   cols(extra["edge_attr"], q * GROUP_TILES * 4, GROUP_TILES * 4), y_ea1[:],
                                   w2_y0[:], dot[:], prod_a[:, r, :, :], prod_b[:, r, :, :])
                    dve.wait_ge(gathered[h], gathers.count(h, GROUP_TILES * (i + 1)))
                    if holds_back(q):
                        dve.wait_ge(operands_made, q)
                    m.y1_times_ea1().then_inc(step, 1)
                    dve.wait_ge(weight_made, q + 1)
                    m.y0_weighed().then_inc(step, 1)
                    dve.wait_ge(step, 3 * q + 1)
                    m.dot_first().then_inc(step, 1)
                    dve.wait_ge(ea0_made, q + 1)
                    m.a_scalars()
                    dve.wait_ge(step, 3 * q + 3)
                    m.dot_second().then_inc(dotted, 1)
                    m.b_vectors()
                    m.a_vectors()
                    dve.wait_ge(dotted, q + 1)
                    m.b_scalars().then_inc(operands_made, 1)

            if gate:
                nc.vector.memset(reaches[:], 1.0)
                nc.vector.memset(slot_in[:], 1.0).then_inc(filled, 1)
                dve.wait_ge(filled, 1)

            def body(i):
                starts = load_bases(DVE_E, i * RING, RING)
                for h in range(RING):
                    operands(i, h)
                    if plain and h == 2 and holds_back(i):
                        dve.wait_ge(own_added, i)
                    if not (isinstance(i, int) and i == 0 and h == 0):
                        add_up(i * RING + h - 1, (h - 1) % 2, starts[h])
                    if plain and h == 1 and holds_back(i):
                        add_own(i - 1, i * RING + 1)
            looped(dve, ITERS, body)
            add_up(GROUPS - 1, (GROUPS - 1) % 2, load_bases(DVE_E, GROUPS, 1)[0])
            if plain:
                add_own(BLOCKS - 1, GROUPS)
            dve.wait_ge(added, GROUPS * n_acc)
    gathers.end_phase(RING, GROUP_TILES * ITERS)


class Far:

    def __init__(self, nc, sb):
        self.any, self.group = sb("far_any", [1, 1], I32), sb("far_group", [1, WINDOWS], I32)
        self.shift = sb("far_shift", [P, WINDOWS])
        self.gathered = nc.alloc_semaphore("far_gathered", 250)
        self.passes = 0


def prep_phase(nc, rel, bases, far, inputs, ident):
    with Scope(nc, "prep") as s:
        dst, base_bc = s.sb("dst", [P, TILES], I32), s.sb("base_bc", [P, GROUPS], I32)
        base_cols, starts = s.sb("base_cols", [P, 2, BASE_COLS], I32), s.sb("starts", [P, WINDOWS])
        base_f, delta = s.sb("base_f", [P, BASE_COLS]), s.sb("delta", [P, BASE_COLS])
        ones = s.sb("ones", [P, P])
        passed, stepped = s.sb("passed", [P, BASE_COLS, WINDOWS]), s.sb("stepped", [P, BASE_COLS, WINDOWS])
        last, none, off = s.sb("last", [P, WINDOWS]), s.sb("none", [P, WINDOWS]), s.sb("off", [P, WINDOWS])
        most, top = s.sb("most", [P, 1]), s.sb("top", [1, 1])
        count_ps, base_ps, most_ps = s.ps("count", [P, 512]), s.ps("base", [P, 512]), s.ps("most", [1, 512])
        loaded, step, counted, turned = s.sem("loaded"), s.sem("step"), s.sem("counted"), s.sem("turned")
        block = s.block()

        @block.sync
        def _(sp):
            sp.dma_start(dst[:], inputs["dst"]).then_inc(loaded, 16)
            sp.dma_start(base_bc[:], inputs["bases"][0:1, 1:1 + GROUPS].broadcast_to([P, GROUPS])).then_inc(loaded, 16)
            sp.dma_start(bases[:], inputs["bases"]).then_inc(loaded, 16)
            sp.dma_start(base_cols[:].rearrange("p a k -> p (a k)"), inputs["base_cols"]).then_inc(loaded, 16)
            sp.dma_start(starts[:], inputs["win_start"]).then_inc(loaded, 16)
            sp.wait_ge(loaded, 80)

        @block.vector
        def _(dve):
            done = 0

            def after(ins):
                nonlocal done
                done += 1
                ins.then_inc(step, 1)
                dve.wait_ge(step, done)

            dve.wait_ge(loaded, 80)
            nc.vector.memset(ones[:], 1.0)
            nc.vector.tensor_copy(base_f[:], base_cols[:, 0, :])
            nc.vector.tensor_tensor(delta[:], base_cols[:, 0, :], base_cols[:, 1, :], ALU.subtract)
            shape = [P, GROUPS, GROUP_TILES]
            after(nc.vector.tensor_tensor(rel[:, 0:TILES].rearrange("p (g t) -> p g t", t=GROUP_TILES),
                                          dst[:].rearrange("p (g t) -> p g t", t=GROUP_TILES),
                                          base_bc[:].unsqueeze(2).broadcast_to(shape), ALU.subtract))
            for k in range(BASE_COLS):
                nc.vector.tensor_scalar(passed[:, k, :], starts[:], base_f[:, k:k + 1], None, ALU.is_gt)
            for k in range(BASE_COLS):
                nc.vector.tensor_scalar(stepped[:, k, :], starts[:], base_f[:, k:k + 1], delta[:, k:k + 1],
                                        ALU.is_gt, ALU.mult)
            after(nc.vector.reduce_max(most[:], rel[:, 0:TILES], mybir.AxisListType.X))
            dve.wait_ge(counted, 1)
            nc.vector.tensor_scalar(far.group[:], count_ps[0:1, 0:WINDOWS], -1.0, 0.0, ALU.add, ALU.max)
            after(nc.vector.tensor_copy(last[:], base_ps[:, 0:WINDOWS]))
            nc.vector.tensor_scalar(none[:], last[:], 0.0, -float(after_all_nodes()), ALU.is_equal, ALU.mult)
            after(nc.vector.scalar_tensor_tensor(off[:], last[:], -1.0, starts[:], ALU.add, ALU.subtract))
            nc.vector.tensor_tensor(far.shift[:], off[:], none[:], ALU.add)
            dve.wait_ge(turned, 1)
            after(nc.vector.reduce_max(top[:], most_ps[:, 0:P], mybir.AxisListType.X))
            nc.vector.tensor_scalar(far.any[:], top[:], float(WIN), None, ALU.is_ge)

        @block.tensor
        def _(pe):
            pe.wait_ge(step, 2)
            for src, ps in ((passed, count_ps), (stepped, base_ps)):
                for k in range(BASE_COLS):
                    ins = nc.tensor.matmul(ps[:, 0:WINDOWS], ones[:], src[:, k, :],
                                           start=(k == 0), stop=(k == BASE_COLS - 1))
            ins.then_inc(counted, 1)
            nc.tensor.transpose(most_ps[:, 0:P], most[:], ident[:]).then_inc(turned, 1)


def after_all_nodes():
    return 1 << 17


def far_pass(nc, far, name, kind, table, width, src_dram, rel, iota, aggs, extra):
    tensor, gate, plain = kind == "tensor", kind == "gate", kind == "sum"
    A = 1 if gate else 2 if tensor else width // P
    T = GROUP_TILES
    before = far.passes * (WINDOWS - 1) * T * 16
    with Scope(nc, name) as s:
        idx, rows = s.sb("idx", [P, T], I32), s.sb("rows", [P, T, width])
        moved, match, past = s.sb("moved", [P, T]), s.sb("match", [P, T, WIN]), s.sb("past", [P, T])
        hot = s.sb("hot", [P, T, WIN])
        sums = [s.ps(f"sums{a}", [P, 512]) for a in range(A)]
        loaded, step, hot_made, summed = s.sem("loaded"), s.sem("step"), s.sem("hot_made"), s.sem("summed")
        done, tick, sp_tick, operands_made = s.sem("done"), s.sem("tick"), s.sem("sp_tick"), s.sem("operands_made")
        targets = [(sums[a], P, aggs[a]) for a in range(A)]
        if tensor:
            edge_in, hidden = s.sb("edge_in", [BASIS, T * P]), s.sb("hidden", [HID, T * P])
            y_ea0, y_ea1 = s.sb("y_ea0", [P, T, P]), s.sb("y_ea1", [P, T, 3, MUL])
            w2_y0, dot = s.sb("w2_y0", [P, T, MUL]), s.sb("dot", [P, T, 2, MUL])
            prod_a, prod_b = s.sb("prod_a", [P, T, P]), s.sb("prod_b", [P, T, P])
            hidden_ps, weight_ps = s.ps("hidden", [P, 512]), s.ps("weight", [P, 512])
            hidden_summed, hidden_made, weight_made = s.sem("hidden_summed"), s.sem("hidden_made"), s.sem("weight_made")
            ea0_made, prepared = s.sem("ea0_made"), s.sem("prepared")
        if gate:
            sig, hot_sig = s.sb("sig", [P, T, WIN]), s.sb("hot_sig", [P, T, WIN])
            slot_in, at_ps = s.sb("slot_in", [P, T, SLOTS + 1]), s.ps("at", [P, 512])
            reaches, rank = s.sb("reaches", [P, T, SLOTS + 1]), s.sb("rank", [P, T, SLOTS])
            at_made, ranked, filled = s.sem("at_made"), s.sem("ranked"), s.sem("filled")
            slot_ps = s.ps("slot", [P, 512])
            sig_made = s.sem("sig_made")
            targets.append((slot_ps, SLOTS + 1, extra["slot_sums"]))
        if plain:
            scaled_sums, scaled = s.sb("scaled_sums", [P, A, WIN]), s.sem("scaled")
        block = s.block()

        def windows(eng, body, group=True):
            with eng.If(eng.value_load(far.any[0:1, 0:1], min_val=0, max_val=1)):
                with eng.Fori(1, WINDOWS) as w:
                    body(w, eng.value_load(far.group[0:1, bass.ds(w, 1)], min_val=0, max_val=GROUPS - 1) if group else None)

        @block.sync
        def _(sp):
            def body(w, g):
                sp.wait_ge(done, w)
                sp.sem_inc(sp_tick, 1)
                sp.dma_start(idx[:], cols(src_dram, g * T, T)).then_inc(loaded, 16)
                if tensor:
                    sp.dma_start(edge_in[:], cols(extra["edge_in"], g * (T * P), T * P)).then_inc(loaded, 16)
            windows(sp, body)

        @block.gpsimd
        def _(pool):
            def body(w, g):
                pool.wait_ge(loaded, w * (32 if tensor else 16))
                pool.sem_inc(tick, 1)
                for t in range(T):
                    nc.gpsimd.indirect_dma_start(
                        rows[:, t, :], None, table, bass.IndirectOffsetOnAxis(ap=idx[:, t:t + 1], axis=0)
                    ).then_inc(far.gathered, 16)
            windows(pool, body, group=False)

        @block.scalar
        def _(act):
            if tensor:
                def body(w, g):
                    act.wait_ge(hidden_summed, w)
                    nc.scalar.activation(hidden[:], hidden_ps[0:HID, 0:T * P], ACT.Silu,
                                         scale=1.0 / math.sqrt(BASIS)).then_inc(hidden_made, 1)
                    act.wait_ge(far.gathered, w * (16 * T) + before)
                    for t in range(T):
                        ins = nc.scalar.activation(y_ea0[:, t, :], rows[:, t, :], ACT.Copy,
                                                   scale=cols(extra["edge_attr"], g * (T * 4) + t * 4, 1))
                    ins.then_inc(ea0_made, 1)
                windows(act, body)
            if gate:
                def body(w, _):
                    act.wait_ge(at_made, w)
                    act.wait_ge(far.gathered, w * (16 * T) + before)
                    for t in range(T):
                        ins = nc.scalar.activation(sig[:, t, :], at_ps[:, 0:WIN], ACT.Sigmoid, bias=rows[:, t, P:P + 1])
                    ins.then_inc(sig_made, 1)
                windows(act, body, group=False)

        @block.tensor
        def _(pe):
            def body(w, _):
                if tensor:
                    pe.wait_ge(loaded, w * 32)
                    nc.tensor.matmul(hidden_ps[0:HID, 0:T * P], extra["w_fc1"], edge_in[:],
                                     start=True, stop=True).then_inc(hidden_summed, 1)
                    pe.wait_ge(hidden_made, w)
                    for t in range(T):
                        ins = nc.tensor.matmul(weight_ps[:, t * P:(t + 1) * P], hidden[:, t * P:(t + 1) * P],
                                               extra["w_fc2"], start=True, stop=True)
                    ins.then_inc(weight_made, 1)
                if gate:
                    pe.wait_ge(done, w)
                    nc.tensor.matmul(at_ps[:, 0:WIN], extra["w_dst"], cols(extra["x"], w * WIN, WIN),
                                     start=True, stop=True).then_inc(at_made, 1)
                if plain:
                    pe.wait_ge(hot_made, w)
                    pe.wait_ge(far.gathered, w * (16 * T) + before)
                else:
                    pe.wait_ge(operands_made, w)
                for t in range(T):
                    first, last = t == 0, t == T - 1
                    if plain:
                        for a in range(A):
                            ins = nc.tensor.matmul(sums[a][:, 0:WIN], rows[:, t, a * P:(a + 1) * P], hot[:, t, :],
                                                   start=first, stop=last)
                    elif gate:
                        nc.tensor.matmul(sums[0][:, 0:WIN], rows[:, t, 0:P], hot_sig[:, t, :], start=first, stop=last)
                        ins = nc.tensor.matmul(slot_ps[0:SLOTS + 1, 0:WIN],
                                               slot_in[:, t, :], hot[:, t, :],
                                               start=first, stop=last)
                    else:
                        nc.tensor.matmul(sums[0][:, 0:WIN], prod_a[:, t, :], hot[:, t, :], start=first, stop=last)
                        ins = nc.tensor.matmul(sums[1][:, 0:WIN], prod_b[:, t, :], hot[:, t, :], start=first, stop=last)
                ins.then_inc(summed, 1)
            windows(pe, body, group=False)

        @block.vector
        def _(dve):
            if gate:
                nc.vector.memset(reaches[:], 1.0)
                nc.vector.memset(slot_in[:], 1.0).then_inc(filled, 1)
                dve.wait_ge(filled, 1)
            dve.sem_inc(done, 1)

            def body(w, g):
                dve.wait_ge(done, w)
                r = cols(rel, g * T, T)
                shape = [P, T, WIN]
                nc.vector.tensor_scalar(past[:], r, float(WIN), None, ALU.is_ge)
                nc.vector.tensor_scalar(moved[:], r, cols(far.shift, w, 1), None, ALU.add).then_inc(step, 1)
                dve.wait_ge(step, w * 2 - 1)
                nc.vector.tensor_tensor(match[:], iota[:].unsqueeze(1).broadcast_to(shape),
                                        moved[:].unsqueeze(2).broadcast_to(shape), ALU.is_equal).then_inc(step, 1)
                dve.wait_ge(step, w * 2)
                nc.vector.tensor_tensor(hot[:], match[:], past[:].unsqueeze(2).broadcast_to(shape),
                                        ALU.mult).then_inc(hot_made, 1)
                if gate:
                    slot_math = SlotMath(nc, T, extra, g, reaches[:], rank[:], slot_in[:])
                    slot_math.reach().then_inc(ranked, 1)
                    dve.wait_ge(ranked, w * 2 - 1)
                    slot_math.rank_edges().then_inc(ranked, 1)
                    dve.wait_ge(ranked, w * 2)
                    slot_math.place_sources()
                    dve.wait_ge(hot_made, w)
                    dve.wait_ge(sig_made, w)
                    nc.vector.tensor_tensor(hot_sig[:], hot[:], sig[:], ALU.mult).then_inc(operands_made, 1)
                if tensor:
                    m = TensorMath(nc, T, weight_ps[:, 0:T * P], rows[:], y_ea0[:],
                                   cols(extra["edge_attr"], g * (T * 4), T * 4), y_ea1[:], w2_y0[:], dot[:],
                                   prod_a[:], prod_b[:])
                    dve.wait_ge(far.gathered, w * (16 * T) + before)
                    m.y1_times_ea1()
                    dve.wait_ge(weight_made, w)
                    m.y0_weighed().then_inc(prepared, 1)
                    dve.wait_ge(prepared, w * 3 - 2)
                    m.dot_first().then_inc(prepared, 1)
                    dve.wait_ge(prepared, w * 3 - 1)
                    m.dot_second().then_inc(prepared, 1)
                    dve.wait_ge(ea0_made, w)
                    m.a_scalars()
                    m.a_vectors()
                    m.b_vectors()
                    dve.wait_ge(prepared, w * 3)
                    m.b_scalars().then_inc(operands_made, 1)
                dve.wait_ge(summed, w)
                if plain:
                    for a in range(A):
                        ins = nc.vector.tensor_tensor(scaled_sums[:, a, :], sums[a][:, 0:WIN],
                                                      cols(extra["inv_count"], w * WIN, WIN), ALU.mult)
                    ins.then_inc(scaled, 1)
                    dve.wait_ge(scaled, w)
                for a, (ps, rws, region) in enumerate(targets):
                    into = region[0:rws, bass.ds(w * WIN, WIN)]
                    term = scaled_sums[:, a, :] if plain else ps[0:rws, 0:WIN]
                    ins = nc.vector.tensor_tensor(into, into, term, ALU.add)
                ins.then_inc(done, 1)
            windows(dve, body)
    far.passes += 1


def tensor_post_phase(nc, X, aggs, lhs, attr_bc):
    with Scope(nc, "tpost") as s:
        acc = s.ps("acc", [P, 2, 512])
        scaled = s.sb("scaled", [P, 2, CHUNK])
        summed, weighed, added = s.sem("summed"), s.sem("weighed"), s.sem("added")
        block = s.block()

        @block.tensor
        def _(pe):
            def body(i):
                for c in range(2):
                    n = i * 2 + c
                    if holds_back(n - 1):
                        pe.wait_ge(weighed, n - 1)
                    for k, region in enumerate([X] + aggs):
                        ins = nc.tensor.matmul(acc[:, c, 0:CHUNK], lhs[k], cols(region, n * CHUNK, CHUNK),
                                               start=(k == 0), stop=(k == len(aggs)))
                    ins.then_inc(summed, 1)
            looped(pe, CHUNKS // 2, body)

        @block.vector
        def _(dve):
            def body(i):
                for c in range(2):
                    n = i * 2 + c
                    dve.wait_ge(summed, n + 1)
                    if holds_back(n - 1):
                        dve.wait_ge(added, n - 1)
                    nc.vector.tensor_tensor(scaled[:, c, :], acc[:, c, 0:CHUNK], cols(attr_bc, n * CHUNK, CHUNK),
                                            ALU.mult).then_inc(weighed, 1)
                for c in range(2):
                    n = i * 2 + c
                    dve.wait_ge(weighed, n + 1)
                    nc.vector.tensor_tensor(cols(X, n * CHUNK, CHUNK), cols(X, n * CHUNK, CHUNK), scaled[:, c, :],
                                            ALU.add).then_inc(added, 1)
            looped(dve, CHUNKS // 2, body)


def slot_tables_phase(nc, slot_sums, slot_idx, inv_count, ident):
    C = SLOTS + 1
    with Scope(nc, "slott") as s:
        turned = s.ps("turned", [P, BLOCKS * C])
        sl, empty = s.sb("sl", [P, BLOCKS, C]), s.sb("empty", [P, BLOCKS, SLOTS])
        floored = s.sb("floored", [P, BLOCKS])
        flipped, step = s.sem("flipped"), s.sem("step")
        block = s.block()

        @block.tensor
        def _(pe):
            for b in range(BLOCKS):
                ins = nc.tensor.transpose(turned[:, b * C:(b + 1) * C], slot_sums[0:C, b * P:(b + 1) * P], ident[0:C, 0:C])
            ins.then_inc(flipped, 1)

        @block.vector
        def _(dve):
            dve.wait_ge(flipped, 1)
            nc.vector.tensor_copy(sl[:].rearrange("p b c -> p (b c)"), turned[:]).then_inc(step, 1)
            dve.wait_ge(step, 1)
            nc.vector.tensor_scalar(floored[:], sl[:, :, SLOTS], 1.0, None, ALU.max)
            for j in range(SLOTS):
                ins = nc.vector.tensor_scalar(empty[:, :, j], sl[:, :, SLOTS], float(j), float(N_NODES), ALU.is_le, ALU.mult)
            ins.then_inc(step, 1)
            dve.wait_ge(step, 2)
            nc.vector.reciprocal(inv_count, floored[:])
            nc.vector.tensor_tensor(slot_idx.rearrange("p (b s) -> p b s", s=SLOTS), sl[:, :, 0:SLOTS], empty[:], ALU.add)


def gru_phase(nc, X, agg, H, hidden_r, hidden_n, w, stats):
    W, count = 2 * CHUNK, CHUNKS // 2
    with Scope(nc, "gru") as s:
        r_ps, z_ps, n_ps = s.ps("r", [P, 2, 512]), s.ps("z", [P, 2, 512]), s.ps("n", [P, 2, 512])
        pre_r, r, z, rh = s.sb("pre_r", [P, 2, W]), s.sb("r", [P, 2, W]), s.sb("z", [P, 2, W]), s.sb("rh", [P, 2, W])
        d, e = s.sb("d", [P, 2, W]), s.sb("e", [P, 2, W])
        pre_n, n = pre_r, r
        r_summed, z_summed, n_summed = s.sem("r_summed"), s.sem("z_summed"), s.sem("n_summed")
        r_added, r_gated, z_gated, weighed = s.sem("r_added"), s.sem("r_gated"), s.sem("z_gated"), s.sem("weighed")
        mixed, tanhed, d_made, e_made = s.sem("mixed"), s.sem("tanhed"), s.sem("d_made"), s.sem("e_made")
        done, tick = s.sem("done"), s.sem("tick")
        block = s.block()

        def sums(ps):
            return ps[:, :, 0:CHUNK]

        def chunks(ap):
            return ap.rearrange("p (c n) -> p c n", n=CHUNK)

        @block.tensor
        def _(pe):
            def products(i, ps, terms):
                for c in range(2):
                    for k, (lhsT, region) in enumerate(terms):
                        ins = nc.tensor.matmul(ps[:, c, 0:CHUNK], lhsT, cols(region, i * W + c * CHUNK, CHUNK),
                                               start=(k == 0), stop=(k == len(terms) - 1))
                return ins

            def body(i, _):
                if holds_back(i):
                    pe.wait_ge(r_added, i)
                products(i, r_ps, [(w["ih"][:, 0:P], agg)]).then_inc(r_summed, 1)
                if holds_back(i):
                    pe.wait_ge(z_gated, i)
                products(i, z_ps, [(w["ih"][:, P:2 * P], agg), (w["hh"][:, P:2 * P], X)]).then_inc(z_summed, 1)
                if holds_back(i):
                    pe.wait_ge(mixed, i)
                products(i, n_ps, [(w["ih"][:, 2 * P:3 * P], agg)]).then_inc(n_summed, 1)
            looped_pairs(pe, count, body)

        @block.scalar
        def _(act):
            def body(i, c):
                act.wait_ge(r_added, i + 1)
                nc.scalar.activation(r[:, c, :], pre_r[:, c, :], ACT.Sigmoid).then_inc(r_gated, 1)
                if holds_back(i - 1):
                    act.wait_ge(e_made, i - 1)
                act.wait_ge(z_summed, i + 1)
                nc.scalar.activation(chunks(z[:, c, :]), sums(z_ps), ACT.Sigmoid, bias=w["b_z"]).then_inc(z_gated, 1)
                act.wait_ge(mixed, i + 1)
                nc.scalar.activation(n[:, c, :], pre_n[:, c, :], ACT.Tanh, bias=w["b_in"]).then_inc(tanhed, 1)
            looped_pairs(act, count, body)

        @block.gpsimd
        def _(pool):
            def body(i, c):
                pool.wait_ge(tanhed, i + 1)
                nc.gpsimd.tensor_tensor(d[:, c, :], cols(X, i * W, W), n[:, c, :], ALU.subtract).then_inc(d_made, 1)
                pool.wait_ge(d_made, i + 1)
                nc.gpsimd.tensor_tensor(e[:, c, :], d[:, c, :], z[:, c, :], ALU.mult).then_inc(e_made, 1)
            looped_pairs(pool, count, body)

        @block.vector
        def _(dve):
            def finish(i, c):
                dve.wait_ge(e_made, i + 1)
                nc.vector.tensor_tensor(cols(H, i * W, W), e[:, c, :], n[:, c, :], ALU.add).then_inc(done, 1)
                dve.wait_ge(done, i + 1)
                dve.sem_inc(tick, 1)
                for half in range(2):
                    chunk_stats(nc, stats, H, i * 2 + half)

            def body(i, c):
                dve.wait_ge(r_summed, i + 1)
                if holds_back(i - 1):
                    dve.wait_ge(done, i - 1)
                nc.vector.tensor_tensor(chunks(pre_r[:, c, :]), chunks(cols(hidden_r, i * W, W)), sums(r_ps),
                                        ALU.add).then_inc(r_added, 1)
                dve.wait_ge(r_gated, i + 1)
                nc.vector.tensor_tensor(rh[:, c, :], r[:, c, :], cols(hidden_n, i * W, W), ALU.mult).then_inc(weighed, 1)
                dve.wait_ge(weighed, i + 1)
                dve.wait_ge(n_summed, i + 1)
                nc.vector.tensor_tensor(chunks(pre_n[:, c, :]), chunks(rh[:, c, :]), sums(n_ps),
                                        ALU.add).then_inc(mixed, 1)
                if holds_back(i):
                    finish(i - 1, 1 - c)
            looped_pairs(dve, count, body)
            finish(count - 1, (count - 1) % 2)


def blank_row_phase(nc, name, blank, w_T, b_row, table):
    with Scope(nc, name) as s:
        ps, row = s.ps("ps", [1, P]), s.sb("row", [1, P])
        summed, added, stored = s.sem("summed"), s.sem("added"), s.sem("stored")
        block = s.block()

        @block.tensor
        def _(pe):
            nc.tensor.matmul(ps[:], blank, w_T, start=True, stop=True).then_inc(summed, 1)

        @block.vector
        def _(dve):
            dve.wait_ge(summed, 1)
            nc.vector.tensor_tensor(row[:], ps[:], b_row, ALU.add).then_inc(added, 1)

        @block.sync
        def _(sp):
            sp.wait_ge(added, 1)
            sp.dma_start(table[N_NODES:N_NODES + 1, :], row[:]).then_inc(stored, 16)
            sp.wait_ge(stored, 16)


def sort_phase(nc, gathers, name, X, H, table, slot_idx, w, ident, stats, spread):
    SUB = 7
    with Scope(nc, name) as s:
        idx = s.sb("idx", [P, SUB, SLOTS], I32)
        rows = s.sb("rows", [P, SUB, SLOTS, P])
        t1, t2, t3 = s.sb("t1", [P, SLOTS, P]), s.sb("t2", [P, SLOTS, P]), s.sb("t3", [P, 2, P])
        acc = s.sb("acc", [P, 3, P])
        out = s.sb("out", [P, SUB, P])
        turned = s.ps("turned", [P, SUB, 512])
        idx_copied = [s.sem(f"idx_copied{b}") for b in range(SUB)]
        gathered = gathers.sems
        ticked = s.sem("ticked")
        if spread is not None:
            diagonal, spread_ps = s.sb("diagonal", [P, P]), s.ps("spread", [P, 512])
            diagonal_made, spread_made, ticked_act = s.sem("diagonal_made"), s.sem("spread_made"), s.sem("ticked_act")
        tick, step, sorted_, flipped, done = s.sem("tick"), s.sem("step"), s.sem("sorted"), s.sem("flipped"), s.sem("done")
        block = s.block()

        @block.sync
        def _(sp):
            def body(i):
                for b in range(SUB):
                    n = i * SUB + b
                    if holds_back(n - SUB + 1):
                        sp.wait_ge(sorted_, n - SUB + 1)
                    sp.dma_start(idx[:, b, :], cols(slot_idx, n * SLOTS, SLOTS)).then_inc(idx_copied[b], 16)
            looped(sp, BLOCKS // SUB, body)

        @block.gpsimd
        def _(pool):
            def body(i):
                for b in range(SUB):
                    n = i * SUB + b
                    if holds_back(n - SUB + 1):
                        pool.wait_ge(sorted_, n - SUB + 1)
                    pool.wait_ge(idx_copied[b], 16 * i + 16)
                    pool.sem_inc(tick, 1)
                    for j in range(SLOTS):
                        nc.gpsimd.indirect_dma_start(
                            rows[:, b, j, :], None, table, bass.IndirectOffsetOnAxis(ap=idx[:, b, j:j + 1], axis=0)
                        ).then_inc(gathered[b], 16)
            looped(pool, BLOCKS // SUB, body)

        @block.tensor
        def _(pe):
            def body(i):
                for b in range(SUB):
                    n = i * SUB + b
                    if holds_back(n - SUB + 1):
                        pe.wait_ge(done, n - SUB + 1)
                    if spread is not None:
                        pe.wait_ge(diagonal_made, n + 1)
                        nc.tensor.matmul(spread_ps[:, 0:P], spread[1][:], diagonal[:], start=True, stop=True)\
                            .then_inc(spread_made, 1)
                    pe.wait_ge(sorted_, n + 1)
                    nc.tensor.transpose(turned[:, b, 0:P], out[:, b, :], ident[:]).then_inc(flipped, 1)
            looped(pe, BLOCKS // SUB, body)

        if spread is not None:
            @block.scalar
            def _(act):
                def body(n):
                    nc.scalar.activation(diagonal[:], ident[:], ACT.Copy, scale=cols(spread[0], n, 1))\
                        .then_inc(diagonal_made, 1)
                    act.wait_ge(spread_made, n + 1)
                    act.sem_inc(ticked_act, 1)
                    nc.scalar.activation(cols(spread[2], n * P, P), spread_ps[:, 0:P], ACT.Copy)
                looped(act, BLOCKS, body)

        @block.vector
        def _(dve):
            STEPS = 5

            def finish(n, b):
                dve.wait_ge(flipped, n + 1)
                nc.vector.scalar_tensor_tensor(cols(H, n * P, P), cols(X, n * P, P), w["a"], turned[:, b, 0:P],
                                               ALU.mult, ALU.add).then_inc(done, 1)

            def block_stats(n):
                dve.wait_ge(done, n + 1)
                dve.sem_inc(ticked, 1)
                width = min(P, N_NODES - n * P) if isinstance(n, int) else P
                nc.vector.bn_stats(cols(stats, n * 6, 6), cols(H, n * P, width))

            def body(i):
                for b in range(SUB):
                    n = i * SUB + b

                    def after(k):
                        dve.wait_ge(step, n * STEPS + k)
                    dve.wait_ge(gathered[b], gathers.count(b, SLOTS * (i + 1)))
                    if holds_back(n - SUB + 1):
                        dve.wait_ge(flipped, n - SUB + 1)
                    r = rows[:, b, :, :]
                    nc.vector.tensor_tensor(t1[:, 0:2, :], r[:, 0:4:2, :], r[:, 1:4:2, :], ALU.min)
                    nc.vector.tensor_tensor(t1[:, 2:4, :], r[:, 0:4:2, :], r[:, 1:4:2, :], ALU.max).then_inc(step, 1)
                    after(1)
                    if holds_back(n):
                        dve.wait_ge(sorted_, n)
                    nc.vector.tensor_tensor(t2[:, 0:2, :], t1[:, 0:4:2, :], t1[:, 1:4:2, :], ALU.min)
                    nc.vector.tensor_tensor(t2[:, 2:4, :], t1[:, 0:4:2, :], t1[:, 1:4:2, :], ALU.max).then_inc(step, 1)
                    after(2)
                    nc.vector.tensor_tensor(t3[:, 0, :], t2[:, 1, :], t2[:, 2, :], ALU.min)
                    nc.vector.tensor_tensor(t3[:, 1, :], t2[:, 1, :], t2[:, 2, :], ALU.max)
                    nc.vector.tensor_scalar(acc[:, 0, :], t2[:, 0, :], w["cw"][:, 0:1], w["cb"],
                                            ALU.mult, ALU.add).then_inc(step, 1)
                    after(3)
                    nc.vector.scalar_tensor_tensor(acc[:, 1, :], t3[:, 0, :], w["cw"][:, 1:2], acc[:, 0, :],
                                                   ALU.mult, ALU.add).then_inc(step, 1)
                    after(4)
                    nc.vector.scalar_tensor_tensor(acc[:, 2, :], t3[:, 1, :], w["cw"][:, 2:3], acc[:, 1, :],
                                                   ALU.mult, ALU.add).then_inc(step, 1)
                    after(5)
                    nc.vector.scalar_tensor_tensor(out[:, b, :], t2[:, 3, :], w["cw"][:, 3:4], acc[:, 2, :],
                                                   ALU.mult, ALU.add).then_inc(sorted_, 1)
                    if not (isinstance(i, int) and i == 0 and b == 0):
                        finish(n - 1, (b - 1) % SUB)
                        block_stats(n - 1)
            looped(dve, BLOCKS // SUB, body)
            finish(BLOCKS - 1, SUB - 1)
            block_stats(BLOCKS - 1)
    gathers.end_phase(SUB, SLOTS * (BLOCKS // SUB))


def stats_phase(nc, name, regions, stats):
    with Scope(nc, name) as s:
        block = s.block()

        @block.vector
        def _(dve):
            for region, found in zip(regions, stats):
                for chunk in range(CHUNKS):
                    chunk_stats(nc, found, region, chunk)


def sage_phase(nc, name, means, wl, outs, stats):
    M, K = len(outs), len(means)
    with Scope(nc, name) as s:
        acc = s.ps("acc", [P, 2, M, 512])
        summed, added, tick = s.sem("summed"), s.sem("added"), s.sem("tick")
        block = s.block()

        @block.tensor
        def _(pe):
            def body(i):
                for c in range(2):
                    n = 2 * i + c
                    if holds_back(n - 1):
                        pe.wait_ge(added, n - 1)
                    for m in range(M):
                        for k in range(K):
                            ins = nc.tensor.matmul(acc[:, c, m, 0:CHUNK], wl[k][:, m * P:(m + 1) * P],
                                                   cols(means[k], n * CHUNK, CHUNK), start=(k == 0), stop=(k == K - 1))
                    ins.then_inc(summed, 1)
            looped(pe, CHUNKS // 2, body)

        @block.vector
        def _(dve):
            def body(i):
                for c in range(2):
                    n = 2 * i + c
                    dve.wait_ge(summed, n + 1)
                    for m in range(M):
                        out = cols(outs[m], n * CHUNK, CHUNK)
                        ins = nc.vector.tensor_tensor(out, out, acc[:, c, m, 0:CHUNK], ALU.add)
                    ins.then_inc(added, 1)
                    dve.wait_ge(added, n + 1)
                    dve.sem_inc(tick, 1)
                    for m in range(M):
                        chunk_stats(nc, stats[m], outs[m], n)
            looped_but_last(dve, CHUNKS // 2, body)


def decode_weights_phase(nc, wl, wr, dec, bias, dec_b, out_l, out_r, out_b):
    with Scope(nc, "decode") as s:
        ps, bias_ps = s.ps("ps", [P, 4, P]), s.ps("bias", [P, 512])
        multiplied = s.sem("multiplied")
        block = s.block()

        @block.tensor
        def _(pe):
            for j, (src, k) in enumerate(((wl, 0), (wl, 1), (wr, 0), (wr, 1))):
                nc.tensor.matmul(ps[:, j, :], src[:, k, :], dec[:], start=True, stop=True)
            nc.tensor.matmul(bias_ps[:, 0:1], dec[:], bias, start=True, stop=True).then_inc(multiplied, 1)

        @block.vector
        def _(dve):
            dve.wait_ge(multiplied, 1)
            nc.vector.tensor_copy(out_l[:].rearrange("p k m -> p (k m)"), ps[:, 0:2, :].rearrange("p k m -> p (k m)"))
            nc.vector.tensor_copy(out_r[:].rearrange("p k m -> p (k m)"), ps[:, 2:4, :].rearrange("p k m -> p (k m)"))
            nc.vector.tensor_tensor(out_b[:], bias_ps[:, 0:1], dec_b, ALU.add)


def gnn_kernel(nc, inp, out):
    Scope.turn = Loads.count = 0
    gathers = Gathers(nc, 7)
    sbuf = ExitStack()
    with sbuf:
        def sb(name, shape, dt=F32):
            return sbuf.enter_context(nc.sbuf_tensor(name, shape, dt))

        def dram(name, shape):
            return nc.dram_tensor(name, shape, F32, kind="Internal").ap()

        X, A, B, C, D, E = (sb(n, [P, REGION]) for n in ("x", "ra", "rb", "rc", "rd", "re"))
        rel = sb("rel", [P, TILES + GROUP_TILES])
        bases = sb("bases", [1, GROUPS + 2], I32)
        iota, ident = sb("iota", [P, WIN]), sb("ident", [P, P])
        ones, eps = sb("ones", [P, P]), sb("eps", [P, 1])
        inv_cols = sb("inv_cols", [P, BLOCKS])
        slot_idx = sb("slot_idx", [P, BLOCKS * SLOTS], I32)
        scale, shift = sb("scale", [P, 2]), sb("shift", [P, 2])
        stats = sb("stats", [P, BLOCKS * 6])
        chunk_halves = [stats[:, m * CHUNKS * 6:(m + 1) * CHUNKS * 6] for m in range(2)]

        far = Far(nc, sb)
        with Scope(nc, "const") as s:
            block = s.block()

            @block.vector
            def _(dve):
                nc.vector.memset(ones[:], 1.0)
                nc.vector.memset(X[:, NP:REGION], 0.0)
                nc.vector.memset(eps[:], EPS)
                nc.vector.memset(rel[:, TILES:], -1.0)

        def edges(name, kind, table, width, aggs, **extra):
            edge_pass(nc, gathers, name, kind, table, width, inp["src"], rel, iota, bases, aggs, extra)
            far_pass(nc, far, name + "_far", kind, table, width, inp["src"], rel, iota, aggs, extra)

        with ExitStack() as st:
            def w(name, shape):
                return st.enter_context(nc.sbuf_tensor(name, shape, F32))
            wl1, wsc, wa, wb = w("wl1", [P, P]), w("wsc", [P, P]), w("wa", [P, P]), w("wb", [P, P])
            fc1, fc2, attr_col = w("fc1", [BASIS, HID]), w("fc2", [HID, P]), w("attr_col", [P, BLOCKS])
            edge_attr = D[:, 0:TILES * 4]
            first = Loads(nc, "first", [(wl1[:], inp["t_l1"]), (wsc[:], inp["t_sc"]), (wa[:], inp["t_l2a"]),
                                        (wb[:], inp["t_l2b"]), (fc1[:], inp["t_fc1"]), (fc2[:], inp["t_fc2"]),
                                        (attr_col[:], inp["attr_col"]), (iota[:], inp["iota"]), (ident[:], inp["ident"]),
                                        (X[:, 0:NP], inp["x_T"])])
            attributes = Loads(nc, "attributes", [(edge_attr, inp["edge_attr"]),
                                                  (C[:, 0:NP], inp["attr_row"].broadcast_to([P, NP]))])
            first.start()
            attributes.start()
            first.await_all()
            s_in, s_mid = 1.0 / math.sqrt(MUL), 1.0 / math.sqrt(2 * MUL) / math.sqrt(16.0)
            c_s, c_x = math.sin(math.pi / 8.0), math.cos(math.pi / 8.0)
            with Scope(nc, "scale_w0") as s:
                block = s.block()

                @block.vector
                def _(dve):
                    nc.vector.tensor_scalar(wl1[:], wl1[:], s_in, None, ALU.mult)
                    nc.vector.tensor_scalar(wsc[:], wsc[:], s_in * c_s, None, ALU.mult)
                    nc.vector.tensor_scalar(wa[:], wa[:], s_mid * c_x, None, ALU.mult)
                    nc.vector.tensor_scalar(wb[:, :], wb[:, :], s_mid * c_x, None, ALU.mult)
                    nc.vector.tensor_scalar(fc2[:], fc2[:], 1.0 / math.sqrt(HID), None, ALU.mult)
            with Scope(nc, "scale_w0b") as s:
                block = s.block()

                @block.vector
                def _(dve):
                    nc.vector.tensor_scalar(wb[3 * MUL:P, :], wb[3 * MUL:P, :], 1.0 / math.sqrt(3.0), None, ALU.mult)
            t0 = dram("table_tensor", (NP, P))
            prep_phase(nc, rel, bases, far, inp, ident)
            table_phase(nc, "tab0", [X], t0, ident, rhs=[wl1[:]], row_scale=attr_col, clear=[A[:], B[:], E[:]])
            attributes.await_all()
            edges("pass0", "tensor", t0, P, [A, B], edge_in=inp["edge_in"], edge_attr=edge_attr, w_fc1=fc1[:], w_fc2=fc2[:])
            tensor_post_phase(nc, X, [A, B], [wsc[:], wa[:], wb[:]], C)

        with ExitStack() as st:
            def w(name, shape, dt=F32):
                return st.enter_context(nc.sbuf_tensor(name, shape, dt))
            wmsg, bmsg = w("wmsg", [P, P + 1]), w("bmsg", [P, P + 1])
            wdst = w("wdst", [P, P])
            wih, whh, gb = w("wih", [P, 3 * P]), w("whh", [P, 3 * P]), w("gb", [P, 8])
            src, dst, before = (D[:, a * TILES:b * TILES].bitcast(I32) for a, b in ((0, 1), (1, 2), (2, 2 + SLOTS)))
            gsum = w("gsum", [P, 2])
            gate_loads = Loads(nc, "gate", [(wmsg[:], inp["g_msg"]), (bmsg[:], inp["g_bmsg"].broadcast_to([P, P + 1])),
                                       (wdst[:], inp["g_dst"]),
                                       (wih[:], inp["g_ih"]), (whh[:], inp["g_hh"]), (gb[:], inp["g_vec"])])
            slot_loads = Loads(nc, "slot", [(src, inp["src"]), (dst, inp["dst"]), (before, inp["dst_before"])])
            gate_loads.start()
            slot_loads.start()
            gate_loads.await_all()
            with Scope(nc, "gsum") as s:
                block = s.block()

                @block.vector
                def _(dve):
                    nc.vector.tensor_tensor(gsum[:], gb[:, 0:2], gb[:, 3:5], ALU.add)
            t1 = dram("table_gate", (NP, P + 1))
            norm_table_phase(nc, "tab1", X, t1, ident, eps, rhs=wmsg[:], bias=bmsg, clear=[A[:]])
            slot_loads.await_all()
            edges("pass1", "gate", t1, P + 1, [A], w_dst=wdst[:], x=X, src=src, dst=dst, dst_before=before,
                  slot_sums=E[0:SLOTS + 1, :],
                  own=[(whh[:, 0:P], B, gsum[:, 0:1]), (whh[:, 2 * P:3 * P], C, gb[:, 5:6])])
            slot_tables_phase(nc, E, slot_idx[:], inv_cols[:], ident)
            gru_phase(nc, X, A, B, B, C, dict(ih=wih, hh=whh, b_z=gsum[:, 1:2], b_in=gb[:, 2:3]), chunk_halves[0])
            batchnorm_params_phase(nc, "bn1", [(gb[:, 6:7], gb[:, 7:8], scale[:, 0:1], shift[:, 0:1])],
                                   chunk_halves[:1], eps)

        for k, (src, dst) in enumerate([(X, B), (B, B)]):
            with ExitStack() as st:
                def w(name, shape):
                    return st.enter_context(nc.sbuf_tensor(f"{name}{k}", shape, F32))
                wT, brow, vec, sc = w("swT", [P, P]), w("sb", [1, P]), w("svec", [P, 3]), w("ssc", [P, 6])
                loads = Loads(nc, f"sort{k}_weights", [(wT[:], inp[f"s_w{k}"]), (brow[:], inp[f"s_b{k}"]),
                                                       (vec[:], inp[f"s_vec{k}"]),
                                                       (sc[:], inp[f"s_sc{k}"].broadcast_to([P, 6]))])
                loads.start()
                t2 = dram(f"table_sort{k}", (NP, P))
                if k == 0:
                    norm_table_phase(nc, "tab20", X, t2, ident, eps, plus=B, normed_by=(scale[:, 0:1], shift[:, 0:1]))
                else:
                    table_phase(nc, "tab21", [src], t2, ident)
                loads.await_all()
                blank_row_phase(nc, f"blank{k}", vec[:, 2:3], wT[:], brow[:], t2)
                sort_phase(nc, gathers, f"sort{k}", src, A, t2, slot_idx,
                           dict(cw=sc[:, 0:4], cb=sc[:, 4:5], a=sc[:, 5:6]), ident, stats, (inv_cols, ones, C) if k == 0 else None)
                batchnorm_params_phase(nc, f"bn2{k}", [(vec[:, 0:1], vec[:, 1:2], scale[:, 0:1], shift[:, 0:1])],
                                       [stats[:]], eps)
                add_normed_phase(nc, f"res2{k}", dst, src, A, scale[:, 0:1], shift[:, 0:1])

        with ExitStack() as st:
            def w(name, shape):
                return st.enter_context(nc.sbuf_tensor("sage_" + name, shape, F32))
            H = 2 * P
            vec = w("avec", [P, 3 + 3 * 6])
            enc, dec, enc_b = w("enc", [P, P]), w("dec", [P, P]), w("enc_b", [P, P])
            wl = [w(f"wl{k}", [P, 1 if k == 0 else 2, P if k == 3 else H]) for k in range(4)]
            wr = [w(f"wr{k}", [P, 1 if k == 0 else 2, P if k == 3 else H]) for k in range(4)]
            flat = "p k m -> p (k m)"
            loads = Loads(nc, "sage", [(vec[:], inp["a_vec"]), (enc[:], inp["a_enc"]), (dec[:], inp["a_dec"]),
                                       (enc_b[:], inp["a_enc_b"].broadcast_to([P, P]))]
                       + [(wl[k][:].rearrange(flat), inp[f"a_wl{k}"]) for k in range(4)]
                       + [(wr[k][:].rearrange(flat), inp[f"a_wr{k}"]) for k in range(4)])
            loads.start()
            zero_phase(nc, "zero_c", [C[:, NP:REGION]])
            loads.await_all()
            decoded_wl, decoded_wr, decoded_b = w("decoded_wl", [P, 2, P]), w("decoded_wr", [P, 2, P]), w("decoded_b", [P, 1])
            decode_weights_phase(nc, wl[3], wr[3], dec, vec[:, 2:3], vec[:, 1:2], decoded_wl, decoded_wr, decoded_b)
            wl[3], wr[3] = decoded_wl, decoded_wr
            t3 = dram("table_sage0", (NP, P))
            norm_table_phase(nc, "tab30", X, t3, ident, eps, plus=B, rhs=enc[:], bias=enc_b, clear=[A[:], D[:], E[:]])
            sources, params, encoder, tab = [X], None, (enc[:], vec[:, 0:1]), t3
            for k, (aggs, outs) in enumerate([([A], [D, E]), ([A, B], [A, B]), ([D, E], [D, E]), ([A], [A])]):
                K = len(sources)
                if k > 0:
                    tab = dram(f"table_sage{k}", (NP, len(aggs) * P))
                    table_phase(nc, f"tab3{k}", sources, tab, ident, func=ACT.Relu, params=params,
                                rhs=[wl[k][:, j, :] for j in range(K)], clear=[r[:] for r in aggs])
                own = dict(sources=sources, params=params, enc=encoder, wr=[wr[k][:, j, :] for j in range(K)],
                           outs=outs, bias=inp_cols(vec, k, 0) if k < 3 else decoded_b[:])
                edges(f"pass3{k}", "sum", tab, len(aggs) * P, aggs, own=own, inv_count=C)
                if k == 0:
                    sage_phase(nc, "sage0", aggs, [wl[0][:, 0, :]], outs, chunk_halves)
                elif k < 3:
                    stats_phase(nc, f"stats{k}", outs, chunk_halves)
                if k < 3:
                    g, b = inp_cols(vec, k, 1), inp_cols(vec, k, 2)
                    batchnorm_params_phase(nc, f"bn3{k}", [(g[:, m:m + 1], b[:, m:m + 1], scale[:, m:m + 1],
                                                            shift[:, m:m + 1]) for m in range(2)], chunk_halves, eps)
                    params = [(scale[:, m:m + 1], shift[:, m:m + 1]) for m in range(2)]
                    sources, encoder = outs, None
        norm_table_phase(nc, "out", X, out, ident, eps, plus=A, keep=False)


def inp_cols(vec, layer, what):
    at = 3 + layer * 6 + 2 * what
    return vec[:, at:at + 2]


def host_layout(inputs):
    import numpy as np
    g = {k: np.asarray(v) for k, v in inputs.items()}
    E_PAD = TILES * P
    f32 = np.float32

    def edges(a, fill=0):
        v = np.full(E_PAD, fill, a.dtype)
        v[:N_EDGES] = a
        return v.reshape(TILES, P).T

    def stack(W):
        return W.reshape(-1, P, W.shape[1]).transpose(1, 0, 2).reshape(P, -1)

    def comp(d):
        return slice(MUL + d, P, 3)

    src, dst = g["src"], g["dst"]
    nowhere = -1
    o = {}
    x_T = np.zeros((P, NP), f32)
    x_T[:, :N_NODES] = g["x"].T
    o["x_T"] = x_T
    o["src"], o["dst"] = edges(src), edges(dst, nowhere)
    before = []
    for j in range(1, SLOTS + 1):
        b = np.full(N_EDGES, -1, dst.dtype)
        b[j:] = dst[:-j]
        before.append(edges(b, -1))
    o["dst_before"] = np.stack(before, 2).reshape(P, TILES * SLOTS)
    bases = np.zeros((1, GROUPS + 2), dst.dtype)
    firsts = dst[::GROUP_TILES * P]
    bases[0, 1:1 + len(firsts)] = firsts
    o["bases"] = bases
    after_all = 1 << 20
    base_col = np.full((2, BASE_COLS * P), after_all, dst.dtype)
    base_col[0, :len(firsts)], base_col[1, 1:len(firsts)] = firsts, firsts[:-1]
    base_col[1, 0] = -1
    o["base_cols"] = base_col.reshape(2, BASE_COLS, P).transpose(2, 0, 1).reshape(P, 2 * BASE_COLS)
    ea = np.zeros((E_PAD, 4), f32)
    ea[:N_EDGES] = g["edge_attr_4"]
    o["edge_attr"] = ea.reshape(TILES, P, 4).transpose(1, 0, 2).reshape(P, TILES * 4)
    ein = np.zeros((BASIS, (GROUPS + LOOK) * GROUP_TILES * P), f32)
    ein[:, :N_EDGES] = g["edge_attr_10"].T
    o["edge_in"] = ein
    attr = np.zeros((NP,), f32)
    attr[:N_NODES] = g["node_vec1"][:, 0]
    o["attr_row"], o["attr_col"] = attr[None, :], attr.reshape(BLOCKS, P).T

    l1, sc, l2a, l2b = (np.zeros((P, P), f32) for _ in range(4))
    l1[:MUL, :MUL], sc[:MUL, :MUL] = g["L0_gnn_W_l10"], g["L0_gnn_W_sc0"]
    l2a[:MUL, :MUL] = g["L0_gnn_W_l20"][:MUL]
    l2b[3 * MUL:, :MUL] = g["L0_gnn_W_l20"][MUL:]
    for d in range(3):
        l1[comp(d), MUL * (d + 1):MUL * (d + 2)] = g["L0_gnn_W_l11"]
        sc[comp(d), comp(d)] = g["L0_gnn_W_sc1"]
        l2a[MUL * (d + 1):MUL * (d + 2), comp(d)] = g["L0_gnn_W_l21"][MUL:]
        l2b[MUL * d:MUL * (d + 1), comp(d)] = g["L0_gnn_W_l21"][:MUL]
    o["t_l1"], o["t_sc"], o["t_l2a"], o["t_l2b"] = l1, sc, l2a, l2b
    o["t_fc1"], o["t_fc2"] = g["L0_gnn_W_fc1"], g["L0_gnn_W_fc2"]

    p = "L1_gnn_"
    att = g[p + "W_att"]
    o["g_msg"] = np.concatenate([g[p + "W_msg"], att[:P]], 1)
    o["g_bmsg"] = np.concatenate([g[p + "b_msg"], g[p + "b_att"].reshape(1)])[None, :]
    o["g_dst"] = np.repeat(att[P:], P, 1)
    o["g_ih"], o["g_hh"] = g[p + "W_ih"].T, g[p + "W_hh"].T
    o["g_vec"] = np.stack([*g[p + "b_ih"].reshape(3, P), *g[p + "b_hh"].reshape(3, P), g[p + "gamma"], g[p + "beta"]], 1)
    p = "L2_gnn_"
    for k in range(2):
        o[f"s_w{k}"], o[f"s_b{k}"] = g[p + f"W{k}"].T, g[p + f"b{k}"][None, :]
        o[f"s_vec{k}"] = np.stack([g[p + f"g{k}"], g[p + f"be{k}"], g[p + f"blank{k}"]], 1)
        o[f"s_sc{k}"] = np.concatenate([g[p + f"cw{k}"], g[p + f"cb{k}"], g[p + f"a{k}"]])[None, :]
    p = "L3_gnn_"
    o["a_enc"], o["a_dec"] = g[p + "enc_W"].T, g[p + "dec_W"].T
    for k in range(4):
        o[f"a_wl{k}"], o[f"a_wr{k}"] = ((g[p + f"Wl{k}"], g[p + f"Wr{k}"]) if k == 3 else
                                        (stack(g[p + f"Wl{k}"].T), stack(g[p + f"Wr{k}"].T)))
    v = [g[p + "enc_b"], g[p + "dec_b"], g[p + "bl3"]]
    for k in range(3):
        for n in (f"bl{k}", f"g{k}", f"b{k}"):
            v += [*g[p + n].reshape(2, P)]
    o["a_vec"] = np.stack(v, 1)
    o["a_enc_b"] = g[p + "enc_b"][None, :]

    o["win_start"] = np.tile(np.arange(WINDOWS, dtype=f32) * WIN, (P, 1))
    o["iota"] = np.tile(np.arange(WIN, dtype=f32), (P, 1))
    o["ident"] = np.eye(P, dtype=f32)
    return {k: np.ascontiguousarray(a) for k, a in o.items()}


def kernel(**inputs):
    import numpy as _np
    import concourse.bacc as _bacc
    from concourse import mybir as _mybir
    from concourse.bass_utils import run_bass_kernel_spmd as _run

    nc = _bacc.Bacc("TRN2", target_bir_lowering=False, num_devices=1)
    arrays, aps = {}, {}
    for name, a in host_layout(inputs).items():
        arrays[f"in_{name}"] = a
        aps[name] = nc.dram_tensor(f"in_{name}", a.shape, _mybir.dt.from_np(a.dtype), kind="ExternalInput").ap()
    out = nc.dram_tensor("out_0", (NP, P), _mybir.dt.float32, kind="ExternalOutput").ap()
    gnn_kernel(nc, aps, out)
    r = _run(nc, [arrays], core_ids=[0])
    return _np.asarray(r.results[0]["out_0"])[:N_NODES]
```
